# Optimizing a Trainium2 kernel written in Bass

```python
import numpy as np
import jax
import jax.numpy as jnp

def _softmax(x, axis=-1):
    return jax.nn.softmax(x, axis=axis)

def _gelu(x):
    return jax.nn.gelu(x, approximate=True)

def _silu(x):
    return jax.nn.silu(x)

def _sigmoid(x):
    return jax.nn.sigmoid(x)

def _layernorm(x, axis=-1, eps=1e-05):
    m = jnp.mean(x, axis=axis, keepdims=True)
    v = jnp.var(x, axis=axis, keepdims=True)
    return (x - m) / jnp.sqrt(v + eps)

def _scatter_add(tgt, idx, src, axis=0):
    return tgt.at[idx].add(src)

def _segment_sum(src, seg, n):
    return jax.ops.segment_sum(src, seg, n)
kernel_name = 'mk_perceiver_d2_seqx_r8_9ee1ab'

def setup_inputs(seed: int=0):
    np.random.seed(seed)
    _w = jnp.asarray

    def _rec_inputs():
        import jax
        import jax.numpy as jnp
        _rk = jax.random.key(seed)
        x = -0.0003929 + 0.9999 * jax.random.normal(jax.random.fold_in(_rk, 1), (4, 128, 128), jnp.float32)
        _lenS = 128 - jax.random.randint(jax.random.fold_in(_rk, 7), (4,), 0, max(1, 128 // 4) + 1, jnp.int32)
        _lenS2 = 2048 - jax.random.randint(jax.random.fold_in(_rk, 8), (4,), 0, max(1, 2048 // 4) + 1, jnp.int32)
        _ctx_1024P = jax.random.normal(jax.random.fold_in(_rk, 11), (4, 16, 128), jnp.float32)
        _ctx_1024c = jax.random.dirichlet(jax.random.fold_in(_rk, 511), 0.3 * jnp.ones((16,), jnp.float32), (4, 2048))
        _ctx_1024t = jnp.einsum('bsk,bkd->bsd', _ctx_1024c, _ctx_1024P)
        _ctx_1024t = _ctx_1024t * jax.lax.rsqrt(jnp.mean(jnp.square(_ctx_1024t)) + 1e-12) * 0.953939
        ctx_1024 = 2.81802e-05 + 1.00001 * (_ctx_1024t + 0.3 * jax.random.normal(jax.random.fold_in(_rk, 611), (4, 2048, 128), jnp.float32))
        _validS = jnp.arange(128)[None, :] < _lenS[:, None]
        _validS2 = jnp.arange(2048)[None, :] < _lenS2[:, None]
        _causal = jnp.tril(jnp.ones((128, 128), dtype=bool))
        mask_BxS2_ik1 = jnp.where(jnp.broadcast_to(_validS2[:, :], (4, 2048)), 1, 0).astype(jnp.int32)
        return (x, ctx_1024, mask_BxS2_ik1)
    x, ctx_1024, mask_BxS2_ik1 = _rec_inputs()

    def _L0_xattn_setup():
        import jax, jax.numpy as jnp
        import numpy as np
        MASK_FILL = -99999.0
        key = jax.random.key(seed)
        k1, k2, k3, k4, k5, k6, k7 = jax.random.split(key, 7)
        B, S, H = (8, 256, 128)
        query = jax.random.normal(k1, (B, S, H), dtype=jnp.float32)
        key_t = jax.random.normal(k2, (B, S, H), dtype=jnp.float32)
        value = jax.random.normal(k3, (B, S, H), dtype=jnp.float32)
        mask = jax.random.randint(k4, (B, S), 0, 2, dtype=jnp.int32)
        s = 1.0 / np.sqrt(H)
        Wq = jax.random.uniform(k5, (H, H), dtype=jnp.float32, minval=-s, maxval=s)
        Wk = jax.random.uniform(k6, (H, H), dtype=jnp.float32, minval=-s, maxval=s)
        Wv = jax.random.uniform(k7, (H, H), dtype=jnp.float32, minval=-s, maxval=s)
        return {'query': query, 'key': key_t, 'value': value, 'Wq': Wq, 'Wk': Wk, 'Wv': Wv, 'mask': mask}
    _L0_xattn_all = _L0_xattn_setup()
    _L0_xattn_in = {k: v for k, v in _L0_xattn_all.items() if k in ('Wq', 'Wk', 'Wv')}
    del _L0_xattn_all

    def _L0_attn_setup():
        import jax, jax.numpy as jnp
        import numpy as np
        B, S, D_IN = (2, 256, 128)
        H, D_HEAD = (16, 64)
        key = jax.random.key(seed)
        k1, k2, k3 = jax.random.split(key, 3)
        x = jax.random.normal(k1, (B, S, D_IN), dtype=jnp.float32)
        kernel = jax.random.normal(k2, (3, H, D_IN, D_HEAD), dtype=jnp.float32) * np.float32(np.sqrt(2.0 / D_IN))
        WO = jax.random.normal(k3, (1, H * D_HEAD, D_IN), dtype=jnp.float32) * np.float32(np.sqrt(2.0 / (H * D_HEAD)))
        return {'x': x, 'kernel': kernel, 'WO': WO}
    _L0_attn_all = _L0_attn_setup()
    _L0_attn_in = {k: v for k, v in _L0_attn_all.items() if k in ('kernel', 'WO')}
    del _L0_attn_all

    def _L0_ffn_setup():
        import jax, jax.numpy as jnp
        import numpy as np
        B, T, C = (4, 256, 128)
        E, H, K = (8, 256, 2)
        key = jax.random.key(seed)
        ks = jax.random.split(key, 7)
        s_in = 1.0 / np.sqrt(C)
        s_hid = 1.0 / np.sqrt(H)
        return {'x': jax.random.normal(ks[0], (B, T, C), dtype=jnp.float32), 'gate_w': jax.random.uniform(ks[1], (C, E), jnp.float32, -s_in, s_in), 'gate_b': jnp.zeros((E,), jnp.float32), 'w1': jax.random.uniform(ks[2], (E, C, H), jnp.float32, -s_in, s_in), 'b1': jax.random.uniform(ks[3], (E, H), jnp.float32, -s_in, s_in), 'w2': jax.random.uniform(ks[4], (E, H, C), jnp.float32, -s_hid, s_hid), 'b2': jax.random.uniform(ks[5], (E, C), jnp.float32, -s_hid, s_hid)}
    _L0_ffn_all = _L0_ffn_setup()
    _L0_ffn_in = {k: v for k, v in _L0_ffn_all.items() if k in ('gate_w', 'gate_b', 'w1', 'b1', 'w2', 'b2')}
    del _L0_ffn_all

    def _L1_xattn_setup():
        import jax, jax.numpy as jnp
        import numpy as np
        B, N, T = (2, 256, 256)
        ENC, DEC, HID = (128, 128, 128)
        HEADS = 16
        DH = HID // HEADS
        HALF = DH // 2
        LAMBDA_INIT = 0.8
        key = jax.random.key(seed)
        ks = jax.random.split(key, 9)
        s = 0.02
        return {'encoder_feature': jax.random.normal(ks[0], (B, N, ENC), jnp.float32), 'decoder_feature': jax.random.normal(ks[1], (B, T, DEC), jnp.float32), 'Wq': jax.random.normal(ks[2], (HID, DEC), jnp.float32) * s, 'Wk': jax.random.normal(ks[3], (HID, ENC), jnp.float32) * s, 'Wv': jax.random.normal(ks[4], (HID, ENC), jnp.float32) * s, 'lambda_q1': jax.random.normal(ks[5], (HALF,), jnp.float32) * 0.1, 'lambda_q2': jax.random.normal(ks[6], (HALF,), jnp.float32) * 0.1, 'lambda_k1': jax.random.normal(ks[7], (HALF,), jnp.float32) * 0.1, 'lambda_k2': jax.random.normal(ks[8], (HALF,), jnp.float32) * 0.1}
    _L1_xattn_all = _L1_xattn_setup()
    _L1_xattn_in = {k: v for k, v in _L1_xattn_all.items() if k in ('Wq', 'Wk', 'Wv', 'lambda_q1', 'lambda_q2', 'lambda_k1', 'lambda_k2')}
    del _L1_xattn_all

    def _L1_attn_setup():
        import math
        import jax, jax.numpy as jnp
        import numpy as np
        H = 128
        NH = 16
        HD = H // NH
        FF = 512
        EPS = 1e-12

        def _lin(key, fan_in, fan_out):
            k1, k2 = jax.random.split(key)
            bound = 1.0 / math.sqrt(fan_in)
            W = jax.random.uniform(k1, (fan_in, fan_out), jnp.float32, -bound, bound)
            b = jax.random.uniform(k2, (fan_out,), jnp.float32, -bound, bound)
            return (W, b)

        def _layernorm(x, g, b):
            mu = jnp.mean(x, axis=-1, keepdims=True)
            var = jnp.mean((x - mu) ** 2, axis=-1, keepdims=True)
            return (x - mu) * jax.lax.rsqrt(var + EPS) * g + b

        def _gelu(x):
            return x * 0.5 * (1.0 + jax.lax.erf(x / jnp.sqrt(jnp.float32(2.0))))
        key = jax.random.key(seed)
        ks = jax.random.split(key, 8)
        x = jax.random.normal(ks[0], (4, 512, H), jnp.float32)
        Wq, bq = _lin(ks[1], H, H)
        Wk, bk = _lin(ks[2], H, H)
        Wv, bv = _lin(ks[3], H, H)
        Wo, bo = _lin(ks[4], H, H)
        W1, b1 = _lin(ks[5], H, FF)
        W2, b2 = _lin(ks[6], FF, H)
        g1 = jnp.ones((H,), jnp.float32)
        be1 = jnp.zeros((H,), jnp.float32)
        g2 = jnp.ones((H,), jnp.float32)
        be2 = jnp.zeros((H,), jnp.float32)
        return dict(x=x, Wq=Wq, bq=bq, Wk=Wk, bk=bk, Wv=Wv, bv=bv, Wo=Wo, bo=bo, g1=g1, be1=be1, W1=W1, b1=b1, W2=W2, b2=b2, g2=g2, be2=be2)
    _L1_attn_all = _L1_attn_setup()
    _L1_attn_in = {k: v for k, v in _L1_attn_all.items() if k in ('Wq', 'bq', 'Wk', 'bk', 'Wv', 'bv', 'Wo', 'bo', 'g1', 'be1', 'W1', 'b1', 'W2', 'b2', 'g2', 'be2')}
    del _L1_attn_all

    def _L1_ffn_setup():
        import jax, jax.numpy as jnp
        import numpy as np
        B, S = (2, 256)
        H = 128
        I = 32
        E = 32
        K = 8
        G = 8
        TG = 4
        NS = 2

        def _mlp(x, w_gu, w_d):
            gu = x @ w_gu
            g, u = (gu[..., :I], gu[..., I:])
            return jax.nn.silu(g) * u @ w_d
        key = jax.random.key(seed)
        ks = jax.random.split(key, 6)
        s = 0.02
        return {'x': jax.random.normal(ks[0], (B, S, H), jnp.float32), 'Wg': jax.random.normal(ks[1], (E, H), jnp.float32) * s, 'W_gate_up': jax.random.normal(ks[2], (E, H, 2 * I), jnp.float32) * s, 'W_down': jax.random.normal(ks[3], (E, I, H), jnp.float32) * s, 'Ws_gate_up': jax.random.normal(ks[4], (NS, H, 2 * I), jnp.float32) * s, 'Ws_down': jax.random.normal(ks[5], (NS, I, H), jnp.float32) * s}
    _L1_ffn_all = _L1_ffn_setup()
    _L1_ffn_in = {k: v for k, v in _L1_ffn_all.items() if k in ('Wg', 'W_gate_up', 'W_down', 'Ws_gate_up', 'Ws_down')}
    del _L1_ffn_all
    return {'x': x, 'ctx_1024': ctx_1024, 'mask_BxS2_ik1': mask_BxS2_ik1, 'L0_xattn_Wq': _L0_xattn_in['Wq'], 'L0_xattn_Wk': _L0_xattn_in['Wk'], 'L0_xattn_Wv': _L0_xattn_in['Wv'], 'L0_attn_kernel': _L0_attn_in['kernel'], 'L0_attn_WO': _L0_attn_in['WO'], 'L0_ffn_gate_w': _L0_ffn_in['gate_w'], 'L0_ffn_gate_b': _L0_ffn_in['gate_b'], 'L0_ffn_w1': _L0_ffn_in['w1'], 'L0_ffn_b1': _L0_ffn_in['b1'], 'L0_ffn_w2': _L0_ffn_in['w2'], 'L0_ffn_b2': _L0_ffn_in['b2'], 'L1_xattn_Wq': _L1_xattn_in['Wq'], 'L1_xattn_Wk': _L1_xattn_in['Wk'], 'L1_xattn_Wv': _L1_xattn_in['Wv'], 'L1_xattn_lambda_q1': _L1_xattn_in['lambda_q1'], 'L1_xattn_lambda_q2': _L1_xattn_in['lambda_q2'], 'L1_xattn_lambda_k1': _L1_xattn_in['lambda_k1'], 'L1_xattn_lambda_k2': _L1_xattn_in['lambda_k2'], 'L1_attn_Wq': _L1_attn_in['Wq'], 'L1_attn_bq': _L1_attn_in['bq'], 'L1_attn_Wk': _L1_attn_in['Wk'], 'L1_attn_bk': _L1_attn_in['bk'], 'L1_attn_Wv': _L1_attn_in['Wv'], 'L1_attn_bv': _L1_attn_in['bv'], 'L1_attn_Wo': _L1_attn_in['Wo'], 'L1_attn_bo': _L1_attn_in['bo'], 'L1_attn_g1': _L1_attn_in['g1'], 'L1_attn_be1': _L1_attn_in['be1'], 'L1_attn_W1': _L1_attn_in['W1'], 'L1_attn_b1': _L1_attn_in['b1'], 'L1_attn_W2': _L1_attn_in['W2'], 'L1_attn_b2': _L1_attn_in['b2'], 'L1_attn_g2': _L1_attn_in['g2'], 'L1_attn_be2': _L1_attn_in['be2'], 'L1_ffn_Wg': _L1_ffn_in['Wg'], 'L1_ffn_W_gate_up': _L1_ffn_in['W_gate_up'], 'L1_ffn_W_down': _L1_ffn_in['W_down'], 'L1_ffn_Ws_gate_up': _L1_ffn_in['Ws_gate_up'], 'L1_ffn_Ws_down': _L1_ffn_in['Ws_down']}

def reference(x, ctx_1024, mask_BxS2_ik1, L0_xattn_Wq, L0_xattn_Wk, L0_xattn_Wv, L0_attn_kernel, L0_attn_WO, L0_ffn_gate_w, L0_ffn_gate_b, L0_ffn_w1, L0_ffn_b1, L0_ffn_w2, L0_ffn_b2, L1_xattn_Wq, L1_xattn_Wk, L1_xattn_Wv, L1_xattn_lambda_q1, L1_xattn_lambda_q2, L1_xattn_lambda_k1, L1_xattn_lambda_k2, L1_attn_Wq, L1_attn_bq, L1_attn_Wk, L1_attn_bk, L1_attn_Wv, L1_attn_bv, L1_attn_Wo, L1_attn_bo, L1_attn_g1, L1_attn_be1, L1_attn_W1, L1_attn_b1, L1_attn_W2, L1_attn_b2, L1_attn_g2, L1_attn_be2, L1_ffn_Wg, L1_ffn_W_gate_up, L1_ffn_W_down, L1_ffn_Ws_gate_up, L1_ffn_Ws_down):
    import jax
    import jax.numpy as jnp

    def _L0_xattn_ref(query, key, value, Wq, Wk, Wv, mask):
        import jax, jax.numpy as jnp
        import numpy as np
        MASK_FILL = -99999.0
        q = jnp.einsum('bsh,oh->bso', query, Wq)
        k = jnp.einsum('bsh,oh->bso', key, Wk)
        v = jnp.einsum('bsh,oh->bso', value, Wv)
        score = jnp.einsum('bqh,bkh->bqk', q, k)
        m = mask[:, None, :]
        score = jnp.where(m == 0, jnp.float32(MASK_FILL), score)
        attn = jax.nn.softmax(score, axis=-1)
        context = jnp.einsum('bqk,bkh->bqh', attn, v)
        return context

    def _L0_attn_ref(x, kernel, WO):
        import jax, jax.numpy as jnp
        import numpy as np
        B, S, D_IN = (2, 256, 128)
        H, D_HEAD = (16, 64)
        b, s, _ = x.shape
        h, d = (kernel.shape[1], kernel.shape[3])
        q = jnp.einsum('bsm,hmd->bhsd', x, kernel[0])
        k = jnp.einsum('bsm,hmd->bhsd', x, kernel[1])
        v = jnp.einsum('bsm,hmd->bhsd', x, kernel[2])
        scale = jnp.float32(1.0 / (d * d * h))
        scores = jnp.einsum('bhsd,bhtd->bhst', q, k) * scale
        attn = jax.nn.softmax(scores, axis=-1)
        out = jnp.einsum('bhst,bhtd->bhsd', attn, v)
        out = jnp.transpose(out, (0, 2, 3, 1)).reshape(b, s, d * h)
        out = jnp.einsum('bsf,fm->bsm', out, WO[0])
        return out

    def _L0_ffn_ref(x, gate_w, gate_b, w1, b1, w2, b2):
        import jax, jax.numpy as jnp
        import numpy as np
        B, T, C = (4, 256, 128)
        E, H, K = (8, 256, 2)
        b, t, c = x.shape
        xf = x.reshape(b * t, c)
        logits = xf @ gate_w + gate_b
        probs = jax.nn.softmax(logits, axis=-1)
        gates, expert_idx = jax.lax.top_k(probs, K)
        h = jax.nn.relu(jnp.einsum('nc,ech->neh', xf, w1) + b1)
        expert_out = jnp.einsum('neh,ehc->nec', h, w2) + b2
        onehot = jax.nn.one_hot(expert_idx, E, dtype=xf.dtype)
        weights = jnp.einsum('nk,nke->ne', gates, onehot)
        out = jnp.einsum('ne,nec->nc', weights, expert_out)
        return out.reshape(b, t, c)

    def _L1_xattn_ref(encoder_feature, decoder_feature, Wq, Wk, Wv, lambda_q1, lambda_q2, lambda_k1, lambda_k2):
        import jax, jax.numpy as jnp
        import numpy as np
        B, N, T = (2, 256, 256)
        ENC, DEC, HID = (128, 128, 128)
        HEADS = 16
        DH = HID // HEADS
        HALF = DH // 2
        LAMBDA_INIT = 0.8
        b, n, _ = encoder_feature.shape
        _, t, _ = decoder_feature.shape
        hid = Wq.shape[0]
        dh = hid // HEADS
        half = dh // 2
        q = decoder_feature @ Wq.T
        k = encoder_feature @ Wk.T
        v = encoder_feature @ Wv.T
        q = q.reshape(b, t, 2 * HEADS, half).transpose(0, 2, 1, 3)
        k = k.reshape(b, n, 2 * HEADS, half).transpose(0, 2, 1, 3)
        v = v.reshape(b, n, HEADS, dh).transpose(0, 2, 1, 3)
        lam = jnp.exp(jnp.sum(lambda_q1 * lambda_k1)) - jnp.exp(jnp.sum(lambda_q2 * lambda_k2)) + LAMBDA_INIT
        scale = 1.0 / jnp.sqrt(jnp.float32(half))
        att = jax.nn.softmax(jnp.einsum('bhtd,bhnd->bhtn', q, k) * scale, axis=-1)
        att = att.reshape(b, HEADS, 2, t, n)
        att = att[:, :, 0] - lam * att[:, :, 1]
        out = jnp.einsum('bhtn,bhnd->bhtd', att, v)
        return out.transpose(0, 2, 1, 3).reshape(b, t, hid)

    def _L1_attn_ref(x, Wq, bq, Wk, bk, Wv, bv, Wo, bo, g1, be1, W1, b1, W2, b2, g2, be2):
        import math
        import jax, jax.numpy as jnp
        import numpy as np
        H = 128
        NH = 16
        HD = H // NH
        FF = 512
        EPS = 1e-12

        def _lin(key, fan_in, fan_out):
            k1, k2 = jax.random.split(key)
            bound = 1.0 / math.sqrt(fan_in)
            W = jax.random.uniform(k1, (fan_in, fan_out), jnp.float32, -bound, bound)
            b = jax.random.uniform(k2, (fan_out,), jnp.float32, -bound, bound)
            return (W, b)

        def _layernorm(x, g, b):
            mu = jnp.mean(x, axis=-1, keepdims=True)
            var = jnp.mean((x - mu) ** 2, axis=-1, keepdims=True)
            return (x - mu) * jax.lax.rsqrt(var + EPS) * g + b

        def _gelu(x):
            return x * 0.5 * (1.0 + jax.lax.erf(x / jnp.sqrt(jnp.float32(2.0))))
        B, S, _ = x.shape

        def heads(W, b):
            return (x @ W + b).reshape(B, S, NH, HD).transpose(0, 2, 1, 3)
        q, k, v = (heads(Wq, bq), heads(Wk, bk), heads(Wv, bv))
        eq = jax.nn.elu(q)
        ek = jax.nn.elu(k)
        qn = eq / jnp.linalg.norm(eq, axis=-1, keepdims=True)
        kn = ek / jnp.linalg.norm(ek, axis=-1, keepdims=True)
        kv = jnp.einsum('bhsd,bhse->bhde', kn, v)
        ctx = jnp.einsum('bhsd,bhde->bhse', qn, kv) / jnp.float32(math.sqrt(HD))
        ctx = ctx.transpose(0, 2, 1, 3).reshape(B, S, H)
        attn_out = _layernorm(ctx @ Wo + bo + x, g1, be1)
        h = _gelu(attn_out @ W1 + b1)
        out = _layernorm(h @ W2 + b2 + attn_out, g2, be2)
        return out

    def _L1_ffn_ref(x, Wg, W_gate_up, W_down, Ws_gate_up, Ws_down):
        import jax, jax.numpy as jnp
        import numpy as np
        B, S = (2, 256)
        H = 128
        I = 32
        E = 32
        K = 8
        G = 8
        TG = 4
        NS = 2

        def _mlp(x, w_gu, w_d):
            gu = x @ w_gu
            g, u = (gu[..., :I], gu[..., I:])
            return jax.nn.silu(g) * u @ w_d
        b, s, h = x.shape
        xf = x.reshape(-1, h)
        n = xf.shape[0]
        shared = (_mlp(xf, Ws_gate_up[0], Ws_down[0]) + _mlp(xf, Ws_gate_up[1], Ws_down[1])) / NS
        logits = xf @ Wg.T
        gsize = E // G
        gl = logits.reshape(n, G, gsize)
        g_top_l, g_top_i = jax.lax.top_k(gl, TG)
        cand_l = g_top_l.reshape(n, G * TG)
        cand_i = g_top_i.reshape(n, G * TG)
        top_l, pos = jax.lax.top_k(cand_l, K)
        topk_idx = pos // TG * gsize + jnp.take_along_axis(cand_i, pos, axis=1)
        topk_w = jax.nn.softmax(top_l, axis=-1)
        flat_idx = topk_idx.reshape(-1)
        flat_w = topk_w.reshape(-1)
        order = jnp.argsort(flat_idx)
        tok = order // K
        xs = xf[tok]
        gsz = jnp.bincount(flat_idx, length=E).astype(jnp.int32)
        gu = jax.lax.ragged_dot(xs, W_gate_up, gsz)
        hmid = jax.nn.silu(gu[:, :I]) * gu[:, I:]
        yo = jax.lax.ragged_dot(hmid, W_down, gsz)
        yo = yo * flat_w[order][:, None]
        routed = jnp.zeros_like(xf).at[tok].add(yo)
        return (shared + routed).reshape(b, s, h)
    x = x + _L0_xattn_ref(_layernorm(x, axis=-1), ctx_1024, ctx_1024, L0_xattn_Wq, L0_xattn_Wk, L0_xattn_Wv, mask_BxS2_ik1)
    x = x + _L0_attn_ref(_layernorm(x, axis=-1), L0_attn_kernel, L0_attn_WO)
    x = x + _L0_ffn_ref(_layernorm(x, axis=-1), L0_ffn_gate_w, L0_ffn_gate_b, L0_ffn_w1, L0_ffn_b1, L0_ffn_w2, L0_ffn_b2)
    x = x + _L1_xattn_ref(ctx_1024, _layernorm(x, axis=-1), L1_xattn_Wq, L1_xattn_Wk, L1_xattn_Wv, L1_xattn_lambda_q1, L1_xattn_lambda_q2, L1_xattn_lambda_k1, L1_xattn_lambda_k2)
    x = x + _L1_attn_ref(_layernorm(x, axis=-1), L1_attn_Wq, L1_attn_bq, L1_attn_Wk, L1_attn_bk, L1_attn_Wv, L1_attn_bv, L1_attn_Wo, L1_attn_bo, L1_attn_g1, L1_attn_be1, L1_attn_W1, L1_attn_b1, L1_attn_W2, L1_attn_b2, L1_attn_g2, L1_attn_be2)
    x = x + _L1_ffn_ref(_layernorm(x, axis=-1), L1_ffn_Wg, L1_ffn_W_gate_up, L1_ffn_W_down, L1_ffn_Ws_gate_up, L1_ffn_Ws_down)
    return x

_drawn_inputs = setup_inputs


def setup_inputs(seed=0):
    import zlib

    import numpy as np

    out = dict(_drawn_inputs(seed))
    spreads = {'L0_ffn_gate_b': (0.0, 0.353),
     'L1_attn_g1': (1.0, 0.2),
     'L1_attn_be1': (0.0, 0.1),
     'L1_attn_g2': (1.0, 0.2),
     'L1_attn_be2': (0.0, 0.1)}
    factors = {'L0_ffn_b1': 8.0,
     'L0_ffn_b2': 4.696,
     'L1_xattn_Wq': 8.0,
     'L1_xattn_Wk': 8.0,
     'L1_xattn_lambda_q1': 8.0,
     'L1_xattn_lambda_q2': 8.0,
     'L1_xattn_lambda_k1': 8.0,
     'L1_xattn_lambda_k2': 8.0,
     'L1_attn_bo': 3.564,
     'L1_attn_b1': 6.494,
     'L1_attn_b2': 5.377,
     'L1_ffn_Wg': 8.0,
     'L1_ffn_W_gate_up': 8.0,
     'L1_ffn_W_down': 8.0,
     'L1_ffn_Ws_gate_up': 8.0,
     'L1_ffn_Ws_down': 8.0}
    for name, (base, spread) in spreads.items():
        noise = np.random.default_rng([zlib.crc32(name.encode()), seed]).standard_normal(out[name].shape)
        drawn = base * np.exp(spread * noise) if base else spread * noise
        out[name] = jnp.asarray(drawn.astype(out[name].dtype))
    for name, factor in factors.items():
        out[name] = (out[name] * factor).astype(out[name].dtype)
    return out
```

```python
from contextlib import ExitStack

import concourse.bass as bass
from concourse import mybir

ALU = mybir.AluOpType
ACT = mybir.ActivationFunctionType
AX = mybir.AxisListType
F32 = mybir.dt.float32
BF16 = mybir.dt.bfloat16
I32 = mybir.dt.int32

NAMES = ['x', 'ctx_1024', 'mask_BxS2_ik1', 'L0_xattn_Wq', 'L0_xattn_Wk', 'L0_xattn_Wv', 'L0_attn_kernel',
         'L0_attn_WO', 'L0_ffn_gate_w', 'L0_ffn_gate_b', 'L0_ffn_w1', 'L0_ffn_b1', 'L0_ffn_w2', 'L0_ffn_b2',
         'L1_xattn_Wq', 'L1_xattn_Wk', 'L1_xattn_Wv', 'L1_xattn_lambda_q1', 'L1_xattn_lambda_q2',
         'L1_xattn_lambda_k1', 'L1_xattn_lambda_k2', 'L1_attn_Wq', 'L1_attn_bq', 'L1_attn_Wk', 'L1_attn_bk',
         'L1_attn_Wv', 'L1_attn_bv', 'L1_attn_Wo', 'L1_attn_bo', 'L1_attn_g1', 'L1_attn_be1', 'L1_attn_W1',
         'L1_attn_b1', 'L1_attn_W2', 'L1_attn_b2', 'L1_attn_g2', 'L1_attn_be2', 'L1_ffn_Wg',
         'L1_ffn_W_gate_up', 'L1_ffn_W_down', 'L1_ffn_Ws_gate_up', 'L1_ffn_Ws_down']


def build_program(nc, t, out):
    P = 128
    B, S, D = t['x'].shape
    T = B * S
    KEYS = t['ctx_1024'].shape[1]
    KC = KEYS // P
    NCHUNK = B * KC
    BANK = 512
    GROUPS = NCHUNK * P // BANK
    GB = KEYS // BANK
    assert S == P and D == P

    with ExitStack() as ctx:
        def sb(name, shape, dt=F32):
            return ctx.enter_context(nc.sbuf_tensor(name, shape, dt))

        def sem(name):
            return ctx.enter_context(nc.semaphore(name))

        ps = ctx.enter_context(nc.psum_tensor("ps", [P, 8, BANK], F32))
        x = sb("x_res", [P, B, D])
        xn = sb("xn", [P, B, D])
        xn_t = sb("xn_t", [P, T])
        aux_t = sb("aux_t", [P, T])
        ident = sb("ident", [P, P])
        ident_h = sb("ident_h", [P, P], BF16)
        stats = sb("stats", [P, B, 6])
        mean_var = sb("mean_var", [P, B, 2])
        var_eps = sb("var_eps", [P, B])
        rstd = sb("rstd", [P, B])
        minus_half = sb("minus_half", [P, 64])
        small_w = sb("small_w", [P, 5, D])
        wqk0, wv0_t, wk1_t, wv1_t, wq1_t = (small_w[:, i, :] for i in range(5))

        wide = sb("wide", [P, 16384])
        work = sb("work", [P, 8192])
        weights = sb("weights", [P, 4096])
        k_parts = sb("k_parts", [P, 3, NCHUNK * P], BF16)
        v1 = sb("v1", [P, NCHUNK, D])

        ctx_sb = wide[:, 0:8192].rearrange("p (c f) -> p c f", f=D)
        ctx_t = wide[:, 8192:16384]
        scores0 = [work[:, 2048 * i:2048 * (i + 1)] for i in range(2)]
        probs0_t = work[:, 4096:6144].rearrange("p (c s) -> p c s", s=S)
        mask_sb = work[:, 6144:8192].bitcast(I32)
        raw_w = k_parts[:, 2, 6144:8192].bitcast(F32)[:, 0:768].rearrange("p (i f) -> p i f", f=D)
        k_left = weights[:, 0:2 * BANK].rearrange("p (i c) -> p i c", i=2)
        nmax0 = sb("nmax0", [P, B])
        sum0 = sb("sum0", [P, B])
        rsum0 = sb("rsum0", [P, B])
        o1_t = xn[:, 0, :]

        HEADS, DH = t['L0_attn_kernel'].shape[1], t['L0_attn_kernel'].shape[3]
        PAIRS = HEADS // 2
        SCALE0 = 1.0 / (DH * DH * HEADS)
        w_qkv = weights[:, 0:3 * HEADS * DH].rearrange("p (c n) -> p c n", c=3)
        w_out0 = weights[:, 3 * HEADS * DH:4096].rearrange("p (i m) -> p i m", i=PAIRS)
        q0_t = wide[:, 0:4096].rearrange("p (i c) -> p i c", i=PAIRS)
        k0_t = wide[:, 4096:8192].rearrange("p (i c) -> p i c", i=PAIRS)
        v0 = wide[:, 8192:12288].rearrange("p (b n) -> p b n", b=B)
        heads_t = wide[:, 12288:16384].rearrange("p (i c) -> p i c", i=PAIRS)
        probs1 = [work[:, 2048 * i:2048 * (i + 1)].rearrange("p (h c) -> p h c", h=HEADS) for i in range(2)]
        probs1_t = [work[:, 4096 + 2048 * i:6144 + 2048 * i] for i in range(2)]
        max1 = sb("max1", [P, B, HEADS])
        nmax1 = sb("nmax1", [P, B, HEADS])
        sum1 = sb("sum1", [P, B, HEADS])
        rsum1 = sb("rsum1", [P, B, HEADS])

        E0 = t['L0_ffn_gate_w'].shape[1]
        HC0 = t['L0_ffn_w1'].shape[2] // P
        NEVER = 3.0e38
        ROW_LOADS = 16 * (5 + 4)
        w1_0 = wide[:, 4096:6144].rearrange("p (e k c) -> p e k c", e=E0, k=HC0)
        w2_0 = wide[:, 6144:8192].rearrange("p (e k c) -> p e k c", e=E0, k=HC0)
        h0_t = wide[:, 8192:16384].rearrange("p (i c) -> p i c", i=E0 * HC0)
        lam_load = sb("lam_load", [P, 4, 4])
        ones_row = sb("ones_row", [1, P])
        gate_w = sb("gate_w", [P, E0])
        gate_b = sb("gate_b", [1, E0])
        b2_0 = sb("b2_0", [E0, D])
        BR0, BR1 = E0 * HC0, 4
        b1_rows = sb("b1_rows", [BR0 + BR1, P])
        b1_cols = sb("b1_cols", [P, BR0 + BR1])
        logits0 = sb("logits0", [P, B, 2 * E0])
        top0 = sb("top0", [P, B, 8])
        picks0 = sb("picks0", [P, B, 8])
        struck0 = sb("struck0", [P, B, 2 * E0])
        ntop0 = sb("ntop0", [P, B])
        gate_e = sb("gate_e", [P, B, E0])
        gate_sum = sb("gate_sum", [P, B])
        gate_r = sb("gate_r", [P, B])
        gates0 = sb("gates0", [P, B, E0])
        gates0_t = aux_t[0:E0, :]
        HH = 32
        HG = HH // 4
        ITEMS = B * HG
        PAIRS_QK = ((0, 0), (0, 1), (1, 0), (1, 1), (0, 2), (2, 0))
        KROWS = 16 * len(PAIRS_QK)
        ROWS = KROWS + 12
        SCALE1 = 0.5
        UNITS = ((0, 3), (3, 3), (6, 2), (8, 3), (11, 3), (14, 2))
        NU = len(UNITS)
        QUADS = KC // 4
        QUAD_OF = [(c + n - 1) // 4 for c, n in UNITS]
        UNIT_OF = [max(k for k, (c, n) in enumerate(UNITS) if c <= 4 * w + 3) for w in range(QUADS)]
        SLOTS = 4
        VCOLS = 9
        LIMIT = 64.0
        probs_d = (wide[:, 0:4096], weights[:, 0:4096])
        k_square = wide[:, 0:4096].bitcast(BF16)
        q_rows = wide[:, 4096:12288].bitcast(BF16)
        acc_sb = wide[:, 12288:13312].rearrange("p (i c) -> p i c", i=2)
        heads_d = wide[:, 13312:14464].rearrange("p (i v) -> p i v", v=VCOLS)
        q_parts = wide[:, 14464:15232].bitcast(BF16).rearrange("p (i c) -> p i c", i=3)
        shift_parts = wide[:, 15232:15424].bitcast(BF16).rearrange("p (i g c) -> p i g c", i=ITEMS, g=3)
        key_ring = work[:, 0:4096].bitcast(BF16).rearrange("p (i c) -> p i c", i=SLOTS)
        q_masked = work[:, 4096:7168].bitcast(BF16).rearrange("p (i b j c) -> p i b j c", i=3, b=B, j=4)
        v_stage = work[:, 7168:8192].rearrange("p (i c v) -> p i c v", i=2, c=KC)
        small_d = small_w.rearrange("p i f -> p (i f)")
        fold = small_d[:, 0:32]
        of_half = small_d[:, 32:64]
        of_half_h = small_d[:, 64:80].bitcast(BF16)
        of_j = small_d[:, 80:84]
        of_j12 = small_d[:, 84:88]
        lam_prod = small_d[:, 104:112].rearrange("p (a f) -> p a f", a=2)
        lam_sum = small_d[:, 112:114]
        lam_exp = small_d[:, 114:116]
        neg_lam = small_d[:, 116:117]
        k_norms = small_d[0:HH, 120:136]
        k_norm = small_d[0:HH, 136:137]
        q_norm = small_d[0:HH, 137:138]
        bound_h = small_d[0:HH, 138:139]
        bound = small_d[0:1, 139:140]
        safe = small_d[0:1, 140:141].bitcast(I32)
        shift_max = small_d[:, 144:272]
        shift_left = small_d[:, 272:400]
        den_r = small_d[:, 144:272]
        HEADS1 = 16
        DH1 = D // HEADS1
        FC = t['L1_attn_W1'].shape[1] // P
        w_qkv1 = work[:, 4096:4480]
        w_out1 = work[:, 4480:4608]
        w1_1 = work[:, 4608:5120]
        w2_1 = work[:, 5120:5632].rearrange("p (k c) -> p k c", k=FC)
        w_gate = work[0:32, 5632:5760]
        b_qkv1 = work[0:1, 5760:6144]
        b_out1 = work[0:1, 6144:6272]
        b2_1 = work[0:1, 6272:6400]
        affine = aux_t[:].rearrange("p (i f) -> p i f", i=4)
        qk1 = wide[:, 0:1024].rearrange("p (b n) -> p b n", b=B)
        v1s = wide[:, 1024:1536].rearrange("p (b n) -> p b n", b=B)
        qk_low = wide[:, 1536:2560].rearrange("p (b n) -> p b n", b=B)
        qk_sq = wide[:, 2560:3584].rearrange("p (b n) -> p b n", b=B)
        qk_norm = wide[:, 3584:3712]
        of_eight = wide[:, 3712:3728]
        kv_diag = wide[:, 3728:4240].rearrange("p (b n) -> p b n", b=B)
        qn_t = wide[:, 4240:4752]
        lin_t = wide[:, 4752:5264]
        res1 = wide[:, 5264:5776].rearrange("p (b n) -> p b n", b=B)
        attn1 = wide[:, 5776:6288].rearrange("p (b n) -> p b n", b=B)
        attn1_t = wide[:, 6288:6800]
        h1_t = wide[:, 6800:8848].rearrange("p (k c) -> p k c", k=FC)
        qk_rs = wide[:, 8848:8976]
        qk_res = qk1.rearrange("p b n -> p (b n)")[:, 0:512].rearrange("p (b n) -> p b n", b=B)

        E1, I1 = t['L1_ffn_W_down'].shape[0:2]
        NS = t['L1_ffn_Ws_down'].shape[0]
        EC = E1 * I1 // P
        EPC = P // I1
        gate_up = weights[:, 0:(E1 + NS) * 2 * I1].rearrange("p (i n) -> p i n", i=2)
        down = weights[:, 2304:2304 + (EC + 1) * D].rearrange("p (m c) -> p m c", c=D)
        wg_t = wide[:, 9216:9216 + E1]
        spread = wide[0:E1, 9728:9728 + E1 * I1]
        logits1 = wide[:, 10752:10880].rearrange("p (b e) -> p b e", b=B)
        struck1 = wide[:, 10880:11008].rearrange("p (b e) -> p b e", b=B)
        gate1 = wide[:, 11008:11136].rearrange("p (b e) -> p b e", b=B)
        top1 = wide[:, 11136:11168].rearrange("p (b e) -> p b e", b=B)
        ntop1 = wide[:, 11168:11172]
        gsum1 = wide[:, 11172:11176]
        grec1 = wide[:, 11176:11180]
        gate1_t = wide[0:E1, 11264:11776]
        silu = [wide[:, 11776 + 512 * i:12288 + 512 * i] for i in range(2)]
        hid1_t = work[:, 0:(EC + 1) * T]
        x_loaded = sem("x_loaded")
        raw_loaded = sem("raw_loaded")
        ctx_loaded = [sem(f"ctx_loaded{b}") for b in range(B)]
        mask_loaded = sem("mask_loaded")
        ident_zero = sem("ident_zero")
        ident_ready = sem("ident_ready")
        half_ready = sem("half_ready")
        ln_step = sem("ln_step")
        ln_rstd = sem("ln_rstd")
        ln_xn = sem("ln_xn")
        ln_trans = sem("ln_trans")
        ln_done = sem("ln_done")
        small_mm = sem("small_mm")
        small_ready = sem("small_ready")
        qk_mm = sem("qk_mm")
        qk_ready = sem("qk_ready")
        ct_trans = sem("ct_trans")
        ct_ready = sem("ct_ready")
        k_mm = sem("k_mm")
        v_mm = sem("v_mm")
        k_first = sem("k_first")
        k_left1 = sem("k_left1")
        k_second = sem("k_second")
        k_third = sem("k_third")
        v_ready = sem("v_ready")
        s0_mm = sem("s0_mm")
        s0_fill = sem("s0_fill")
        s0_masked = sem("s0_masked")
        s0_max = sem("s0_max")
        s0_exp = sem("s0_exp")
        s0_rsum = sem("s0_rsum")
        p0_trans = sem("p0_trans")
        p0_ready = sem("p0_ready")
        o1_mm = sem("o1_mm")
        o1_ready = sem("o1_ready")
        y0_mm = sem("y0_mm")
        x_done = sem("x_done")
        stored = sem("stored")

        attn0_loaded = sem("attn0_loaded")
        q0_mm = sem("q0_mm")
        k0_mm = sem("k0_mm")
        v0_mm = sem("v0_mm")
        q0_ready = sem("q0_ready")
        k0_ready = sem("k0_ready")
        v0_ready_s = sem("v0_ready_s")
        v0_ready_v = sem("v0_ready_v")
        s1_mm = sem("s1_mm")
        s1_max = sem("s1_max")
        s1_exp = sem("s1_exp")
        s1_norm = sem("s1_norm")
        p1_trans = sem("p1_trans")
        p1_ready = sem("p1_ready")
        h1_mm = sem("h1_mm")
        h1_ready = sem("h1_ready")
        y1_mm = sem("y1_mm")
        rows_loaded = sem("rows_loaded")
        consts = sem("consts")
        cols_mm = sem("cols_mm")
        cols_ready = sem("cols_ready")
        ffn0_loaded = sem("ffn0_loaded")
        lg0_mm = sem("lg0_mm")
        picks0_step = sem("picks0_step")
        gate_exp = sem("gate_exp")
        gate_step = sem("gate_step")
        g0_trans = sem("g0_trans")
        g0_ready = sem("g0_ready")
        b2_mm = sem("b2_mm")
        h0_mm = sem("h0_mm")
        h0_even = sem("h0_even")
        h0_odd = sem("h0_odd")
        e0_mm = sem("e0_mm")
        x_moe = sem("x_moe")
        consts_d = sem("consts_d")
        ksq_ready = sem("ksq_ready")
        kn_mm = sem("kn_mm")
        kn_max = sem("kn_max")
        kn_all = sem("kn_all")
        lam_step = sem("lam_step")
        lam_expd = sem("lam_expd")
        q1_mm = sem("q1_mm")
        q1_part = sem("q1_part")
        q1_left = sem("q1_left")
        q1_square = sem("q1_square")
        qn_mm = sem("qn_mm")
        bound_step = sem("bound_step")
        bound_trans = sem("bound_trans")
        safe_ready = sem("safe_ready")
        q_masked_ready = sem("q_masked_ready")
        q_rows_zero = sem("q_rows_zero")
        q_rows_loaded = sem("q_rows_loaded")
        ring_ones = sem("ring_ones")
        stage_set = sem("stage_set")
        shift_loaded = [sem(f"shift_loaded{i}") for i in range(SLOTS)]
        shift_mm = sem("shift_mm")
        shift_maxed = sem("shift_maxed")
        shift_step = sem("shift_step")
        shift_trans = sem("shift_trans")
        shift_rows = sem("shift_rows")
        ring_loaded = [sem(f"ring_loaded{i}") for i in range(SLOTS)]
        scores_mm = sem("scores_mm")
        exp_done = sem("exp_done")
        pv_done = sem("pv_done")
        acc_copied = sem("acc_copied")
        staged = sem("staged")
        fold_mm = sem("fold_mm")
        folded = sem("folded")
        comb_step = sem("comb_step")
        x_diff = sem("x_diff")
        f2_res = sem("f2_res")
        x_lin = sem("x_lin")
        spread_ready = sem("spread_ready")
        top1_ready = sem("top1_ready")
        hid_half = sem("hid_half")
        lin_loaded = sem("lin_loaded")
        moe1_loaded = sem("moe1_loaded")
        wg_trans = sem("wg_trans")
        wg_ready = sem("wg_ready")
        lin_mm = sem("lin_mm")
        lin_step = sem("lin_step")
        lin_exp = sem("lin_exp")
        lin_v = sem("lin_v")
        lin_sq = sem("lin_sq")
        lin_pow = sem("lin_pow")
        kv_mm = sem("kv_mm")
        kv_ready = sem("kv_ready")
        qn_trans = sem("qn_trans")
        qn_ready = sem("qn_ready")
        lc_mm = sem("lc_mm")
        lc_ready = sem("lc_ready")
        lo_mm = sem("lo_mm")
        a1_trans = sem("a1_trans")
        a1_ready = sem("a1_ready")
        f1_mm = sem("f1_mm")
        f1_ready = sem("f1_ready")
        f2_mm = sem("f2_mm")
        lg1_mm = sem("lg1_mm")
        g1_step = sem("g1_step")
        g1_exp = sem("g1_exp")
        g1_trans = sem("g1_trans")
        g1_ready = sem("g1_ready")
        gu_mm = sem("gu_mm")
        silu_ready = sem("silu_ready")
        hid_step = sem("hid_step")
        down_mm = sem("down_mm")
        x_final = sem("x_final")
        block = ctx.enter_context(nc.Block())
        LN_BANK = 6

        def norm_vector(dve, n, eps, src=x, dst=xn):
            for b in range(B):
                st = nc.vector.bn_stats(stats[:, b, :], src[:, b, :])
            st.then_inc(ln_step, 1)
            dve.wait_ge(ln_step, 3 * n + 1)
            for b in range(B):
                ag = nc.vector.bn_aggr(mean_var[:, b, :], stats[:, b, :])
            ag.then_inc(ln_step, 1)
            dve.wait_ge(ln_step, 3 * n + 2)
            nc.vector.tensor_scalar_add(var_eps[:], mean_var[:, :, 1], eps).then_inc(ln_step, 1)
            dve.wait_ge(ln_rstd, n + 1)
            for b in range(B):
                nc.vector.tensor_scalar(dst[:, b, :], src[:, b, :], mean_var[:, b, 0:1], rstd[:, b:b + 1],
                                        ALU.subtract, ALU.mult).then_inc(ln_xn, 1)

        def norm_gpsimd(pool, n):
            pool.wait_ge(ln_step, 3 * n + 3)
            nc.gpsimd.tensor_tensor(rstd[:], var_eps[:], minus_half[:, 0:B], ALU.pow).then_inc(ln_rstd, 1)

        def norm_tensor(pe, n, src=xn):
            for b in range(B):
                pe.wait_ge(ln_xn, B * n + b + 1)
                tr = nc.tensor.transpose(ps[:, LN_BANK, b * S:(b + 1) * S], src[:, b, :], ident[:])
            tr.then_inc(ln_trans, 1)

        def norm_scalar(act, n):
            act.wait_ge(ln_trans, n + 1)
            nc.scalar.copy(xn_t[:], ps[:, LN_BANK, :]).then_inc(ln_done, 1)

        @block.sync
        def _(sp):
            sp.dma_start(x[:], t['x'].rearrange("b s f -> s b f")).then_inc(x_loaded, 16)
            ctx_d = t['ctx_1024'].rearrange("b (c p) f -> b p c f", p=P)
            for b in range(B):
                sp.dma_start(ctx_sb[:, b * KC:(b + 1) * KC, :], ctx_d[b]).then_inc(ctx_loaded[b], 16)
                if b >= 1:
                    sp.wait_ge(s0_masked, b)
                sp.dma_start(mask_sb, t['mask_BxS2_ik1'][b:b + 1, :].broadcast_to([P, KEYS]))\
                  .then_inc(mask_loaded, 16)
            sp.wait_ge(k_third, GROUPS)
            sp.dma_start(w_qkv.rearrange("p c (h d) -> p c h d", h=HEADS),
                         t['L0_attn_kernel'].rearrange("c h m d -> m c h d")).then_inc(attn0_loaded, 16)
            wo_d = t['L0_attn_WO'][0].rearrange("(d i two) m -> two d i m", i=PAIRS, two=2)
            for i in range(2):
                sp.dma_start(w_out0[DH * i:DH * (i + 1), :, :], wo_d[i]).then_inc(attn0_loaded, 16)
            sp.wait_ge(s1_mm, B)
            sp.dma_start(w1_0.rearrange("p e k c -> p e (k c)"), t['L0_ffn_w1'].rearrange("e c h -> c e h"))\
              .then_inc(ffn0_loaded, 16)
            sp.dma_start(w2_0, t['L0_ffn_w2'].rearrange("e (k p) c -> p e k c", p=P)).then_inc(ffn0_loaded, 16)
            sp.wait_ge(q_masked_ready, 4)
            for g in range(HG):
                for r, (part, _) in enumerate(PAIRS_QK):
                    dst = q_rows[16 * r:16 * (r + 1), :].rearrange("p (b g c) -> p b g c", b=B, g=HG)[:, :, g, :]
                    src = q_masked[16 * g:16 * (g + 1), part, :, :, :].rearrange("p b j c -> p b (j c)")
                    sp.dma_start(dst, src).then_inc(q_rows_loaded, 16)

            def load_keys(b, g, loaded):
                for r, (_, part) in enumerate(PAIRS_QK):
                    sp.dma_start(key_ring[16 * r:16 * (r + 1), g % SLOTS, :],
                                 k_parts[16 * g:16 * (g + 1), part, bass.ds(b * KEYS, KEYS)])\
                      .then_inc(loaded[g % SLOTS], 16)

            sp.wait_ge(safe_ready, 1)
            is_safe = sp.value_load(safe)
            with sp.If(is_safe < 1):
                with sp.Fori(0, B) as b:
                    for g in range(HG):
                        sp.wait_ge(shift_mm, b * HH + (4 * g + 4))
                        load_keys(b, g, shift_loaded)
                sp.wait_ge(shift_mm, B * HH + 4 * SLOTS)
            with sp.Fori(0, B) as b:
                for g in range(HG):
                    sp.wait_ge(scores_mm, b * (HG * NU) + (g + 1) * NU)
                    load_keys(b, g, ring_loaded)
            for dst, name in ((w_qkv1[:, 0:D], 'Wq'), (w_qkv1[:, D:2 * D], 'Wk'), (w_qkv1[:, 2 * D:3 * D], 'Wv'),
                              (w_out1, 'Wo'), (w1_1, 'W1')):
                sp.dma_start(dst, t['L1_attn_' + name]).then_inc(lin_loaded, 16)
            sp.dma_start(w2_1, t['L1_attn_W2'].rearrange("(k p) c -> p k c", p=P)).then_inc(lin_loaded, 16)
            for dst, name in ((b_qkv1[:, 0:D], 'bq'), (b_qkv1[:, D:2 * D], 'bk'), (b_qkv1[:, 2 * D:3 * D], 'bv'),
                              (b_out1, 'bo'), (b2_1, 'b2')):
                sp.dma_start(dst, t['L1_attn_' + name].rearrange("(a f) -> a f", a=1)).then_inc(lin_loaded, 16)
            for i, name in enumerate(('g1', 'be1', 'g2', 'be2')):
                sp.dma_start(affine[:, i, :], t['L1_attn_' + name].rearrange("(a f) -> a f", a=1).broadcast_to([P, D]))\
                  .then_inc(lin_loaded, 16)
            sp.dma_start(w_gate, t['L1_ffn_Wg']).then_inc(lin_loaded, 16)
            sp.wait_ge(pv_done, (ITEMS + 2) * QUADS)
            for i in range(2):
                half = gate_up[:, i, :].rearrange("p (e n) -> p e n", n=I1)
                cols = slice(I1 * i, I1 * (i + 1))
                sp.dma_start(half[:, 0:E1, :], t['L1_ffn_W_gate_up'][:, :, cols].rearrange("e c n -> c e n"))                  .then_inc(moe1_loaded, 16)
                sp.dma_start(half[:, E1:E1 + NS, :], t['L1_ffn_Ws_gate_up'][:, :, cols].rearrange("e c n -> c e n"))                  .then_inc(moe1_loaded, 16)
            sp.dma_start(down[:, 0:EC, :], t['L1_ffn_W_down'].rearrange("(m e) i c -> (e i) m c", m=EC)).then_inc(moe1_loaded, 16)
            sp.dma_start(down[0:NS * I1, EC, :], t['L1_ffn_Ws_down'].rearrange("e i c -> (e i) c")).then_inc(moe1_loaded, 16)
            sp.wait_ge(x_final, B)
            sp.dma_start(out.rearrange("b s f -> s b f"), x[:]).then_inc(stored, 16)
            sp.wait_ge(stored, 16)

        @block.gpsimd
        def _(pool):
            nc.gpsimd.memset(ident[:], 0.0).then_inc(ident_zero, 1)
            nc.gpsimd.memset(ident_h[:], 0.0).then_inc(ident_zero, 1)
            nc.gpsimd.memset(minus_half[:], -0.5).then_inc(half_ready, 1)
            pool.wait_ge(ident_zero, 2)
            for m in (ident, ident_h):
                nc.gpsimd.affine_select(out=m[:], in_=m[:], compare_op=ALU.not_equal, fill=1.0, base=0,
                                        pattern=[[-1, P]], channel_multiplier=1).then_inc(ident_ready, 1)
            pool.wait_ge(half_ready, 1)
            norm_gpsimd(pool, 0)
            for n in range(GROUPS):
                pool.wait_ge(k_left1, n + 1)
                nc.gpsimd.tensor_copy(k_parts[:, 1, n * BANK:(n + 1) * BANK], k_left[:, n % 2, :])\
                  .then_inc(k_second, 1)
                pool.wait_ge(k_second, n + 1)
                nc.gpsimd.tensor_tensor(k_parts[:, 2, n * BANK:(n + 1) * BANK], k_left[:, n % 2, :],
                                        k_parts[:, 1, n * BANK:(n + 1) * BANK], ALU.subtract)\
                  .then_inc(k_third, 1)
                if n % GB == 0:
                    b = n // GB
                    if b >= 2:
                        pool.wait_ge(p0_trans, b - 1)
                    nc.gpsimd.memset(scores0[b % 2], -99999.0).then_inc(s0_fill, 1)
            nc.gpsimd.memset(ones_row[:], 1.0).then_inc(consts, 1)
            nc.gpsimd.memset(logits0[:], -NEVER).then_inc(consts, 1)
            nc.gpsimd.memset(picks0[:], -NEVER).then_inc(consts, 1)
            norm_gpsimd(pool, 1)
            norm_gpsimd(pool, 2)
            pool.wait_ge(x_done, 2 * B)
            pool.wait_ge(ln_rstd, 3)
            nc.gpsimd.memset(key_ring[KROWS:ROWS, :, :], 1.0).then_inc(ring_ones, 1)
            pool.wait_ge(ring_ones, 1)
            nc.gpsimd.memset(v_stage, 0.0).then_inc(stage_set, 1)
            pool.wait_ge(stage_set, 1)
            for i in range(2):
                nc.gpsimd.memset(v_stage[:, :, :, VCOLS * i + 8:VCOLS * i + 9], 1.0).then_inc(stage_set, 1)
            norm_gpsimd(pool, 3)
            pool.wait_ge(x_moe, B * (E0 + 1))
            pool.wait_ge(ln_rstd, 4)
            pool.wait_ge(stage_set, 3)
            nc.gpsimd.memset(q_rows[KROWS:ROWS, :], 0.0).then_inc(q_rows_zero, 1)
            pool.wait_ge(q_rows_zero, 1)
            with pool.Fori(0, B) as b:
                for g in range(HG):
                    pool.wait_ge(pv_done, b * (HG * QUADS) + (g + 1) * QUADS)
                    nc.gpsimd.tensor_copy(
                        v_stage[:, g % 2, :, 0:2 * VCOLS].rearrange("p c (i v) -> p c i v", i=2)[:, :, :, 0:8],
                        v1[:, bass.ds(b * KC, KC), 16 * g:16 * (g + 1)].rearrange("p c (i v) -> p c i v", i=2))\
                      .then_inc(staged, 1)
            norm_gpsimd(pool, 4)
            pool.wait_ge(lin_step, 5)
            for i in range(2):
                nc.gpsimd.tensor_tensor(qk_rs[:, 64 * i:64 * (i + 1)], qk_norm[:, 64 * i:64 * (i + 1)], minus_half[:],
                                        ALU.pow).then_inc(lin_pow, 1)
            norm_gpsimd(pool, 5)
            norm_gpsimd(pool, 6)
            norm_gpsimd(pool, 7)

        @block.scalar
        def _(act):
            for i, name in enumerate(('L0_xattn_Wq', 'L0_xattn_Wk', 'L0_xattn_Wv', 'L1_xattn_Wk',
                                      'L1_xattn_Wv', 'L1_xattn_Wq')):
                act.dma_start(raw_w[:, i, :], t[name]).then_inc(raw_loaded, 16)
            act.dma_start(b1_rows[0:BR0, :], t['L0_ffn_b1'].rearrange("e (k p) -> (e k) p", p=P)).then_inc(rows_loaded, 16)
            act.dma_start(b1_rows[BR0:BR0 + BR1, :], t['L1_attn_b1'].rearrange("(k p) -> k p", p=P)).then_inc(rows_loaded, 16)
            act.dma_start(gate_w[:], t['L0_ffn_gate_w']).then_inc(rows_loaded, 16)
            act.dma_start(gate_b[:], t['L0_ffn_gate_b'].rearrange("(a e) -> a e", a=1)).then_inc(rows_loaded, 16)
            act.dma_start(b2_0[:], t['L0_ffn_b2']).then_inc(rows_loaded, 16)
            for i, name in enumerate(('q1', 'k1', 'q2', 'k2')):
                act.dma_start(lam_load[:, i, :], t['L1_xattn_lambda_' + name].rearrange("(a f) -> a f", a=1)
                              .broadcast_to([P, 4])).then_inc(rows_loaded, 16)
            act.wait_ge(small_mm, 1)
            nc.scalar.copy(small_w[:, 0:4, :], ps[:, 0, :].rearrange("p (i f) -> p i f", f=D))\
              .then_inc(small_ready, 1)
            nc.scalar.copy(small_w[:, 4, :], ps[:, 1, 0:D]).then_inc(small_ready, 1)
            norm_scalar(act, 0)

            def keys_values(n):
                act.wait_ge(k_mm, n + 1)
                nc.scalar.copy(k_parts[:, 0, n * BANK:(n + 1) * BANK], ps[:, 2, :]).then_inc(k_first, 1)
                act.wait_ge(v_mm, n + 1)
                nc.scalar.copy(v1[:, 4 * n:4 * n + 4, :], ps[:, 3, :].rearrange("p (c f) -> p c f", f=D))\
                  .then_inc(v_ready, 1)

            def exps(b):
                act.wait_ge(s0_max, b + 1)
                nc.scalar.activation(scores0[b % 2], scores0[b % 2], ACT.Exp, bias=nmax0[:, b:b + 1],
                                     accum_out=sum0[:, b:b + 1]).then_inc(s0_exp, 1)

            def probs_out(b):
                act.wait_ge(p0_trans, b + 1)
                if b >= 1:
                    act.wait_ge(o1_mm, b)
                nc.scalar.copy(probs0_t.rearrange("p c s -> p (c s)"),
                               ps[:, 4:8, :].rearrange("p k c -> p (k c)")).then_inc(p0_ready, 1)

            def context_out(b):
                act.wait_ge(o1_mm, b + 1)
                nc.scalar.copy(o1_t, ps[:, 3, 0:S]).then_inc(o1_ready, 1)

            for b in range(B + 1):
                if b < B:
                    for j in range(GB):
                        keys_values(GB * b + j)
                        if j == 1 and b >= 1:
                            exps(b - 1)
                else:
                    exps(b - 1)
                if b >= 1:
                    probs_out(b - 1)
                    context_out(b - 1)
            act.wait_ge(cols_mm, 1)
            nc.scalar.copy(b1_cols[:], ps[:, 1, 0:BR0 + BR1]).then_inc(cols_ready, 1)
            norm_scalar(act, 1)
            for i in range(PAIRS):
                act.wait_ge(q0_mm, i + 1)
                nc.scalar.copy(q0_t[:, i, :], ps[:, i % 2, :]).then_inc(q0_ready, 1)
            for b in range(B):
                act.wait_ge(v0_mm, 2 * b + 1)
                nc.scalar.copy(v0[:, b, 0:BANK], ps[:, 4, :]).then_inc(v0_ready_s, 1)

            def probs1_out(b):
                for j in range(4):
                    act.wait_ge(p1_trans, 4 * b + j + 1)
                    nc.scalar.copy(probs1_t[b % 2][:, j * BANK:(j + 1) * BANK], ps[:, 4 + j % 2, :])\
                      .then_inc(p1_ready, 1)

            for b in range(B):
                act.wait_ge(s1_max, 2 * b + 2)
                if b >= 2:
                    act.wait_ge(p1_trans, 4 * (b - 1))
                for h in range(HEADS):
                    ex = nc.scalar.activation(probs1[b % 2][:, h, :], ps[:, h // 4, (h % 4) * S:(h % 4 + 1) * S],
                                              ACT.Exp, bias=nmax1[:, b, h:h + 1], scale=SCALE0,
                                              accum_out=sum1[:, b, h:h + 1])
                ex.then_inc(s1_exp, 1)
                if b >= 1:
                    probs1_out(b - 1)
            probs1_out(B - 1)

            act.wait_ge(s1_mm, B)
            nc.scalar.activation(k_square, k_parts[:, 0, :], ACT.Square).then_inc(ksq_ready, 1)

            norm_scalar(act, 2)

            def relu_even(i):
                act.wait_ge(h0_mm, i + 1)
                nc.scalar.activation(h0_t[:, i, :], ps[:, 1 + i % 3, :], ACT.Relu, bias=b1_cols[:, i:i + 1])\
                  .then_inc(h0_even, 1)

            relu_even(0)
            relu_even(2)
            act.wait_ge(gate_step, 1)
            for b in range(B):
                ex = nc.scalar.activation(gate_e[:, b, :], logits0[:, b, 0:E0], ACT.Exp, bias=ntop0[:, b:b + 1],
                                          accum_out=gate_sum[:, b:b + 1])
            ex.then_inc(gate_exp, 1)
            relu_even(4)
            act.wait_ge(g0_trans, 1)
            nc.scalar.copy(gates0_t, ps[0:E0, 7, :]).then_inc(g0_ready, 1)
            for i in range(6, E0 * HC0, 2):
                relu_even(i)
            act.wait_ge(lam_step, 2)
            nc.scalar.activation(lam_exp, lam_sum, ACT.Exp).then_inc(lam_expd, 1)
            norm_scalar(act, 3)
            act.wait_ge(q1_mm, 1)
            nc.scalar.copy(q_parts[:, 0, :], ps[:, 0, :]).then_inc(q1_part, 1)
            nc.scalar.activation(aux_t[:], ps[:, 0, :], ACT.Square).then_inc(q1_square, 1)
            with act.Fori(0, B) as b:
                for g in range(HG):
                    for k, (c, n) in enumerate(UNITS):
                        act.wait_ge(scores_mm, b * (HG * NU) + (NU * (g + SLOTS) + k + 1))
                        act.wait_ge(pv_done, b * (HG * QUADS) + (QUADS * (g + 1) + QUAD_OF[k] + 1))
                        half = probs_d[c // 8]
                        nc.scalar.activation(half[:, (c % 8) * BANK:(c % 8 + n) * BANK],
                                             ps[:, 3 * (k % 2):3 * (k % 2) + n, :].rearrange("p k c -> p (k c)"),
                                             ACT.Exp, scale=SCALE1).then_inc(exp_done, 1)
            norm_scalar(act, 4)
            act.wait_ge(wg_trans, 1)
            nc.scalar.copy(wg_t, ps[:, 7, 0:E1]).then_inc(wg_ready, 1)
            act.wait_ge(lin_step, 1)
            nc.scalar.activation(qk_low, qk_low, ACT.Exp).then_inc(lin_exp, 1)
            act.wait_ge(lin_step, 3)
            nc.scalar.copy(v1s, ps[:, 0:4, 2 * D:3 * D]).then_inc(lin_v, 1)
            nc.scalar.activation(qk_sq, qk1, ACT.Square).then_inc(lin_sq, 1)
            act.wait_ge(qn_trans, 1)
            nc.scalar.copy(qn_t, ps[:, 5, :]).then_inc(qn_ready, 1)
            act.wait_ge(lc_mm, 1)
            nc.scalar.copy(lin_t, ps[:, 6, :]).then_inc(lc_ready, 1)
            act.wait_ge(a1_trans, 1)
            nc.scalar.copy(attn1_t, ps[:, 5, :]).then_inc(a1_ready, 1)
            for k in range(FC):
                act.wait_ge(f1_mm, k + 1)
                nc.scalar.activation(h1_t[:, k, :], ps[:, k, :], ACT.Gelu, bias=b1_cols[:, BR0 + k:BR0 + k + 1])\
                  .then_inc(f1_ready, 1)

            norm_scalar(act, 5)
            act.wait_ge(g1_step, 2)
            for b in range(B):
                ex = nc.scalar.activation(gate1[:, b, :], logits1[:, b, :], ACT.Exp, bias=ntop1[:, b:b + 1])
            ex.then_inc(g1_exp, 1)
            act.wait_ge(g1_trans, 1)
            nc.scalar.copy(gate1_t, ps[0:E1, 1, :]).then_inc(g1_ready, 1)
            for m in range(EC + 1):
                rows = P if m < EC else NS * I1
                act.wait_ge(gu_mm, m + 1)
                if m >= 2:
                    act.wait_ge(hid_step, m - 1)
                nc.scalar.activation(silu[m % 2][0:rows, :], ps[0:rows, 2 + 3 * (m % 2), :], ACT.Silu)\
                  .then_inc(silu_ready, 1)

        @block.vector
        def _(dve):
            dve.wait_ge(x_loaded, 16)
            norm_vector(dve, 0, 1e-5)
            dve.wait_ge(qk_mm, 1)
            nc.vector.tensor_copy(aux_t[:], ps[:, 4, :]).then_inc(qk_ready, 1)

            def context_group(n):
                dve.wait_ge(ct_trans, n + 1)
                nc.vector.tensor_copy(ctx_t[:, n * BANK:(n + 1) * BANK], ps[:, n % 2, :]).then_inc(ct_ready, 1)

            def keys_left(n):
                dve.wait_ge(k_first, n + 1)
                if n >= 2:
                    dve.wait_ge(k_third, n - 1)
                nc.vector.tensor_tensor(k_left[:, n % 2, :], ps[:, 2, :],
                                        k_parts[:, 0, n * BANK:(n + 1) * BANK], ALU.subtract)\
                  .then_inc(k_left1, 1)

            def mask_max(b):
                dve.wait_ge(s0_mm, b + 1)
                dve.wait_ge(s0_fill, b + 1)
                dve.wait_ge(mask_loaded, 16 * (b + 1))
                nc.vector.copy_predicated(scores0[b % 2], mask_sb, ps[:, 4:8, :].rearrange("p k c -> p (k c)"))\
                  .then_inc(s0_masked, 1)
                dve.wait_ge(s0_masked, b + 1)
                nc.vector.tensor_reduce(nmax0[:, b:b + 1], scores0[b % 2], AX.X, ALU.max, negate=True)\
                  .then_inc(s0_max, 1)

            def add_context(b):
                dve.wait_ge(s0_exp, b + 1)
                nc.vector.reciprocal(rsum0[:, b:b + 1], sum0[:, b:b + 1]).then_inc(s0_rsum, 1)
                dve.wait_ge(s0_rsum, b + 1)
                dve.wait_ge(y0_mm, b + 1)
                nc.vector.scalar_tensor_tensor(x[:, b, :], ps[:, 2, 0:D], rsum0[:, b:b + 1], x[:, b, :],
                                               ALU.mult, ALU.add).then_inc(x_done, 1)

            for b in range(B + 1):
                if b < B:
                    for j in range(GB):
                        n = GB * b + j
                        context_group(n)
                        if j >= 1:
                            keys_left(n - 1)
                        if j == 1 and b >= 1:
                            mask_max(b - 1)
                    keys_left(n)
                else:
                    mask_max(b - 1)
                if b >= 1:
                    add_context(b - 1)
            dve.wait_ge(x_done, B)
            nc.vector.tensor_reduce(fold, ident[:].rearrange("p (a r) -> p r a", r=32), AX.X, ALU.add)
            nc.vector.tensor_reduce(of_half, ident[:].rearrange("p (h c) -> p h c", c=4), AX.X, ALU.add)
            nc.vector.tensor_reduce(of_half_h, ident[:].rearrange("p (h c) -> p h c", c=4), AX.X, ALU.max)
            nc.vector.tensor_reduce(of_j, ident[:].rearrange("p (a j c) -> p j a c", j=4, c=4), AX.XY, ALU.add)
            nc.vector.tensor_reduce(of_j12, ident[:, 0:12].rearrange("p (a j) -> p j a", j=4), AX.X, ALU.add)\
              .then_inc(consts_d, 1)
            dve.wait_ge(rows_loaded, ROW_LOADS)
            nc.vector.tensor_tensor(lam_prod, lam_load[:, 0:4:2, :], lam_load[:, 1:4:2, :], ALU.mult).then_inc(lam_step, 1)
            dve.wait_ge(lam_step, 1)
            nc.vector.tensor_reduce(lam_sum, lam_prod, AX.X, ALU.add).then_inc(lam_step, 1)

            norm_vector(dve, 1, 1e-5)
            for i in range(PAIRS):
                dve.wait_ge(k0_mm, i + 1)
                nc.vector.tensor_copy(k0_t[:, i, :], ps[:, 2 + i % 2, :]).then_inc(k0_ready, 1)

            def max_heads(b):
                dve.wait_ge(s1_mm, b + 1)
                nc.vector.tensor_reduce(max1[:, b, :], ps[:, 0:4, :].rearrange("p k (h c) -> p (k h) c", c=S),
                                        AX.X, ALU.max).then_inc(s1_max, 1)
                dve.wait_ge(s1_max, 2 * b + 1)
                nc.vector.tensor_scalar_mul(nmax1[:, b, :], max1[:, b, :], -SCALE0).then_inc(s1_max, 1)

            def normalise(b):
                dve.wait_ge(s1_exp, b + 1)
                nc.vector.reciprocal(rsum1[:, b, :], sum1[:, b, :]).then_inc(s1_norm, 1)
                dve.wait_ge(s1_norm, 2 * b + 1)
                nc.vector.tensor_tensor(probs1[b % 2], probs1[b % 2],
                                        rsum1[:, b, :].unsqueeze(2).to_broadcast([P, HEADS, S]), ALU.mult)\
                  .then_inc(s1_norm, 1)

            def heads_out(b):
                dve.wait_ge(h1_mm, b + 1)
                nc.vector.tensor_copy(heads_t[:, :, b * S:(b + 1) * S],
                                      ps[:, 6:8, :].rearrange("p k (i c) -> p (k i) c", c=S)).then_inc(h1_ready, 1)

            max_heads(0)
            for b in range(B):
                dve.wait_ge(v0_mm, 2 * b + 2)
                nc.vector.tensor_copy(v0[:, b, BANK:2 * BANK], ps[:, 5, :]).then_inc(v0_ready_v, 1)
            for b in range(B):
                normalise(b)
                if b + 1 < B:
                    max_heads(b + 1)
                heads_out(b)
            for b in range(B):
                dve.wait_ge(y1_mm, b + 1)
                nc.vector.tensor_tensor(x[:, b, :], x[:, b, :], ps[:, b, 0:D], ALU.add).then_inc(x_done, 1)

            dve.wait_ge(x_done, 2 * B)
            norm_vector(dve, 2, 1e-5)
            dve.wait_ge(consts, 3)
            dve.wait_ge(lg0_mm, 1)
            nc.vector.tensor_copy(logits0[:, :, 0:E0], ps[:, 0, 0:B * E0].rearrange("p (b e) -> p b e", b=B))\
              .then_inc(picks0_step, 1)

            def relu_odd(i):
                dve.wait_ge(h0_mm, i + 1)
                nc.vector.tensor_scalar(h0_t[:, i, :], ps[:, 1 + i % 3, :], b1_cols[:, i:i + 1], 0.0,
                                        ALU.add, ALU.max).then_inc(h0_odd, 1)

            dve.wait_ge(picks0_step, 1)
            for b in range(B):
                mx = nc.vector.max(top0[:, b, :], logits0[:, b, 0:E0])
            mx.then_inc(picks0_step, 1)
            dve.wait_ge(cols_ready, 1)
            relu_odd(1)
            dve.wait_ge(picks0_step, 2)
            nc.vector.tensor_scalar_mul(ntop0[:], top0[:, :, 0], -1.0).then_inc(gate_step, 1)
            nc.vector.tensor_copy(picks0[:, :, 0:2], top0[:, :, 0:2]).then_inc(picks0_step, 1)
            dve.wait_ge(picks0_step, 3)
            for b in range(B):
                mr = nc.vector.match_replace(struck0[:, b, :], picks0[:, b, :], logits0[:, b, :], NEVER)
            mr.then_inc(picks0_step, 1)
            relu_odd(3)
            dve.wait_ge(picks0_step, 4)
            nc.vector.tensor_tensor(gates0[:], struck0[:, :, 0:E0], logits0[:, :, 0:E0], ALU.not_equal)\
              .then_inc(gate_step, 1)
            dve.wait_ge(gate_exp, 1)
            nc.vector.reciprocal(gate_r[:], gate_sum[:]).then_inc(gate_step, 1)
            dve.wait_ge(gate_step, 3)
            nc.vector.tensor_tensor(gate_e[:], gate_e[:], gates0[:], ALU.mult).then_inc(gate_step, 1)
            dve.wait_ge(gate_step, 4)
            nc.vector.tensor_tensor(gates0[:], gate_e[:], gate_r[:].unsqueeze(2).to_broadcast([P, B, E0]), ALU.mult)\
              .then_inc(gate_step, 1)
            relu_odd(5)
            dve.wait_ge(gate_step, 5)
            dve.wait_ge(b2_mm, 1)
            for b in range(B):
                nc.vector.tensor_tensor(x[:, b, :], x[:, b, :], ps[:, 7, b * D:(b + 1) * D], ALU.add).then_inc(x_moe, 1)
            for e in range(E0):
                if 2 * e + 7 < E0 * HC0:
                    relu_odd(2 * e + 7)
                dve.wait_ge(e0_mm, e + 1)
                for b in range(B):
                    dve.wait_ge(x_moe, B * e + b + 1)
                    nc.vector.scalar_tensor_tensor(x[:, b, :], ps[:, 4 + e % 2, b * D:(b + 1) * D],
                                                   gates0[:, b, e:e + 1], x[:, b, :], ALU.mult, ALU.add)\
                      .then_inc(x_moe, 1)
                for i in (0, 1):
                    dve.wait_ge(kn_mm, 2 * e + i + 1)
                    nc.vector.tensor_reduce(k_norms[:, 2 * e + i:2 * e + i + 1], ps[0:HH, 6 * i, :], AX.X, ALU.max)\
                      .then_inc(kn_max, 1)
            dve.wait_ge(kn_max, GROUPS)
            nc.vector.reduce_max(k_norm, k_norms, AX.X).then_inc(kn_all, 1)
            dve.wait_ge(lam_expd, 1)
            nc.vector.scalar_tensor_tensor(neg_lam, lam_exp[:, 0:1], -1.0, lam_exp[:, 1:2], ALU.mult, ALU.add)\
              .then_inc(lam_step, 1)
            dve.wait_ge(lam_step, 3)
            nc.vector.tensor_scalar_add(neg_lam, neg_lam, -0.8).then_inc(lam_step, 1)
            dve.wait_ge(x_moe, B * (E0 + 1))
            norm_vector(dve, 3, 1e-5)
            dve.wait_ge(q1_part, 1)
            dve.wait_ge(q1_square, 1)
            dve.wait_ge(ln_trans, 4)
            left = xn[:].rearrange("p b f -> p (b f)")
            nc.vector.tensor_tensor(left, ps[:, 0, :], q_parts[:, 0, :], ALU.subtract).then_inc(q1_left, 1)
            dve.wait_ge(q1_left, 1)
            nc.vector.tensor_copy(q_parts[:, 1, :], left).then_inc(q1_left, 1)
            dve.wait_ge(q1_left, 2)
            nc.vector.tensor_tensor(q_parts[:, 2, :], left, q_parts[:, 1, :], ALU.subtract).then_inc(q1_left, 1)
            dve.wait_ge(q1_left, 3)
            for j in range(4):
                nc.vector.tensor_scalar(q_masked[:, :, :, j, :], q_parts.rearrange("p i (b c) -> p i b c", b=B),
                                        of_j[:, j:j + 1], None, ALU.mult).then_inc(q_masked_ready, 1)
            dve.wait_ge(qn_mm, 1)
            nc.vector.reduce_max(q_norm, ps[0:HH, 1, :], AX.X).then_inc(bound_step, 1)
            dve.wait_ge(kn_all, 1)
            dve.wait_ge(bound_step, 1)
            nc.vector.tensor_tensor(bound_h, q_norm, k_norm, ALU.mult).then_inc(bound_step, 1)
            dve.wait_ge(bound_trans, 1)
            nc.vector.reduce_max(bound, ps[0:1, 2, 0:HH], AX.X).then_inc(bound_step, 1)
            dve.wait_ge(bound_step, 3)
            nc.vector.tensor_scalar(safe, bound, (LIMIT / SCALE1) ** 2 / 1.02, None, ALU.is_le).then_inc(safe_ready, 1)

            dve.wait_ge(safe_ready, 1)
            is_safe = dve.value_load(safe)
            with dve.If(is_safe < 1):
                with dve.Fori(0, B) as b:
                    for h in range(HH):
                        dve.wait_ge(shift_mm, b * HH + (h + 1 + 4 * SLOTS))
                        nc.vector.tensor_reduce(shift_max[:, bass.ds(b * HH + h, 1)],
                                                ps[:, 4 * (h % 2):4 * (h % 2) + 4, :].rearrange("p k c -> p (k c)"),
                                                AX.X, ALU.max, negate=True).then_inc(shift_maxed, 1)
                dve.wait_ge(shift_maxed, B * HH + 2)
                m_v = shift_max.rearrange("p (i j) -> p i j", j=4)
                l_v = shift_left.rearrange("p (i j) -> p i j", j=4)
                nc.vector.tensor_copy(shift_parts[:, :, 0, :], m_v).then_inc(shift_step, 1)
                dve.wait_ge(shift_step, 1)
                nc.vector.tensor_tensor(l_v, m_v, shift_parts[:, :, 0, :], ALU.subtract).then_inc(shift_step, 1)
                dve.wait_ge(shift_step, 2)
                nc.vector.tensor_copy(shift_parts[:, :, 1, :], l_v).then_inc(shift_step, 1)
                dve.wait_ge(shift_step, 3)
                nc.vector.tensor_tensor(shift_parts[:, :, 2, :], l_v, shift_parts[:, :, 1, :], ALU.subtract)\
                  .then_inc(shift_step, 1)
                dve.wait_ge(q_rows_zero, 1)
                for n in range(ITEMS):
                    dve.wait_ge(shift_trans, n + 1)
                    nc.vector.tensor_tensor(
                        q_rows[KROWS:ROWS, n * BANK:(n + 1) * BANK].rearrange("p (j c) -> p j c", j=4),
                        ps[0:12, n % 2, 0:S].unsqueeze(1).to_broadcast([12, 4, S]),
                        of_j12[0:12, :].unsqueeze(2).to_broadcast([12, 4, S]), ALU.mult).then_inc(shift_rows, 1)

            with dve.Fori(0, B) as b:
                for g in range(HG):
                    dve.wait_ge(pv_done, b * (HG * QUADS) + QUADS * (g + 3))
                    nc.vector.tensor_copy(acc_sb[:, g % 2, :], ps[:, 6, :]).then_inc(acc_copied, 1)
                    dve.wait_ge(fold_mm, b * HG + (g + 1))
                    nc.vector.tensor_copy(heads_d[:, bass.ds(b * HH + 4 * g, 4), :],
                                          ps[:, 7, 0:4 * VCOLS].rearrange("p (j v) -> p j v", j=4)).then_inc(folded, 1)
            dve.wait_ge(folded, ITEMS + 1)
            num = heads_d[:, :, 0:8]
            nc.vector.reciprocal(den_r, heads_d[:, :, 8]).then_inc(comb_step, 1)
            dve.wait_ge(comb_step, 1)
            nc.vector.tensor_tensor(num, num, den_r.unsqueeze(2).to_broadcast([P, B * HH, 8]), ALU.mult)\
              .then_inc(comb_step, 1)
            dve.wait_ge(comb_step, 2)
            by_head = x[:].rearrange("p b (h v) -> p (b h) v", v=8)
            nc.vector.scalar_tensor_tensor(by_head, heads_d[:, 1:B * HH:2, 0:8], neg_lam, by_head, ALU.mult, ALU.add)\
              .then_inc(comb_step, 1)
            dve.wait_ge(comb_step, 3)
            nc.vector.tensor_tensor(by_head, heads_d[:, 0:B * HH:2, 0:8], by_head, ALU.add).then_inc(x_diff, 1)
            dve.wait_ge(x_diff, 1)
            norm_vector(dve, 4, 1e-5)
            nc.vector.tensor_reduce(of_eight, ident[:].rearrange("p (h c) -> p h c", c=DH1), AX.X, ALU.add)\
              .then_inc(kv_ready, 1)
            dve.wait_ge(kv_ready, 1)
            nc.vector.tensor_scalar_mul(of_eight, of_eight, DH1 ** -0.5).then_inc(kv_ready, 1)
            dve.wait_ge(lin_mm, 1)
            q_k = ps[:, 0:4, 0:2 * D]
            nc.vector.tensor_scalar(qk_low, q_k, 0.0, None, ALU.min).then_inc(lin_step, 1)
            dve.wait_ge(lin_exp, 1)
            nc.vector.tensor_scalar_add(qk_low, qk_low, -1.0).then_inc(lin_step, 1)
            dve.wait_ge(lin_step, 2)
            nc.vector.scalar_tensor_tensor(qk1, q_k, 0.0, qk_low, ALU.max, ALU.add).then_inc(lin_step, 1)
            dve.wait_ge(lin_sq, 1)
            by_head = "p b (h c) -> p (b h) c"
            nc.vector.tensor_reduce(qk_norm, qk_sq.rearrange(by_head, c=DH1), AX.X, ALU.add).then_inc(lin_step, 2)
            dve.wait_ge(lin_pow, 2)
            nc.vector.tensor_tensor(qk1.rearrange(by_head, c=DH1), qk1.rearrange(by_head, c=DH1),
                                    qk_rs.unsqueeze(2).to_broadcast([P, 2 * B * HEADS1, DH1]), ALU.mult).then_inc(lin_step, 1)
            dve.wait_ge(kv_mm, 1)
            dve.wait_ge(kv_ready, 2)
            nc.vector.tensor_tensor(kv_diag.rearrange("p b (h c) -> p b h c", c=DH1),
                                    ps[:, 4, :].rearrange("p (b h c) -> p b h c", b=B, c=DH1),
                                    of_eight.unsqueeze(1).unsqueeze(3).to_broadcast([P, B, HEADS1, DH1]), ALU.mult)\
              .then_inc(kv_ready, 1)
            dve.wait_ge(lo_mm, 1)
            nc.vector.tensor_tensor(res1, xn[:], ps[:, 7, :].rearrange("p (b n) -> p b n", b=B), ALU.add).then_inc(lin_step, 1)
            dve.wait_ge(lin_step, 7)
            norm_vector(dve, 5, 1e-12, res1, attn1)

            def affine_vector(n, i):
                dve.wait_ge(ln_xn, B * (n + 1))
                nc.vector.tensor_tensor(attn1 if i == 0 else res1, attn1 if i == 0 else res1,
                                        affine[:, i, :].unsqueeze(1).to_broadcast([P, B, D]), ALU.mult).then_inc(lin_step, 1)
                dve.wait_ge(lin_step, 8 + i)
                nc.vector.tensor_tensor(attn1 if i == 0 else res1, attn1 if i == 0 else res1,
                                        affine[:, i + 1, :].unsqueeze(1).to_broadcast([P, B, D]), ALU.add).then_inc(lin_step, 1)

            affine_vector(5, 0)
            dve.wait_ge(lin_step, 9)
            dve.wait_ge(f2_mm, 1)
            nc.vector.tensor_tensor(qk_res, attn1, ps[:, 4, :].rearrange("p (b n) -> p b n", b=B), ALU.add).then_inc(f2_res, 1)
            dve.wait_ge(f2_res, 1)
            norm_vector(dve, 6, 1e-12, qk_res, res1)
            affine_vector(6, 2)
            dve.wait_ge(lin_step, 11)
            nc.vector.tensor_tensor(x[:], x[:], res1, ALU.add).then_inc(x_lin, 1)

            dve.wait_ge(x_lin, 1)
            norm_vector(dve, 7, 1e-5)
            nc.vector.tensor_copy(spread.rearrange("p (e i) -> p e i", i=I1),
                                  ident[0:E1, 0:E1].unsqueeze(2).to_broadcast([E1, E1, I1])).then_inc(spread_ready, 1)
            dve.wait_ge(lg1_mm, 1)
            nc.vector.tensor_copy(logits1, ps[:, 0, 0:B * E1].rearrange("p (b e) -> p b e", b=B)).then_inc(g1_step, 1)
            dve.wait_ge(g1_step, 1)
            for b in range(B):
                mx = nc.vector.max(top1[:, b, :], logits1[:, b, :])
            mx.then_inc(top1_ready, 1)
            dve.wait_ge(top1_ready, 1)
            nc.vector.tensor_scalar_mul(ntop1, top1[:, :, 0], -1.0).then_inc(g1_step, 1)
            for b in range(B):
                mr = nc.vector.match_replace(struck1[:, b, :], top1[:, b, :], logits1[:, b, :], NEVER)
            mr.then_inc(g1_step, 1)
            dve.wait_ge(g1_step, 3)
            nc.vector.tensor_tensor(struck1, struck1, logits1, ALU.not_equal).then_inc(g1_step, 1)
            dve.wait_ge(g1_step, 4)
            dve.wait_ge(g1_exp, 1)
            nc.vector.tensor_tensor(gate1, gate1, struck1, ALU.mult).then_inc(g1_step, 1)
            dve.wait_ge(g1_step, 5)
            nc.vector.tensor_reduce(gsum1, gate1, AX.X, ALU.add).then_inc(g1_step, 1)
            dve.wait_ge(g1_step, 6)
            nc.vector.reciprocal(grec1, gsum1).then_inc(g1_step, 1)
            dve.wait_ge(g1_step, 7)
            nc.vector.tensor_tensor(gate1, gate1, grec1.unsqueeze(2).to_broadcast([P, B, E1]), ALU.mult).then_inc(g1_step, 1)
            for m in range(EC + 1):
                rows = P if m < EC else NS * I1
                dve.wait_ge(silu_ready, m + 1)
                dst = hid1_t[0:rows, m * T:(m + 1) * T]
                if m < EC:
                    nc.vector.tensor_tensor(silu[m % 2], silu[m % 2], ps[:, 3 + 3 * (m % 2), :], ALU.mult).then_inc(hid_half, 1)
                    dve.wait_ge(hid_half, m + 1)
                    nc.vector.tensor_tensor(dst, silu[m % 2], ps[:, 4 + 3 * (m % 2), :], ALU.mult).then_inc(hid_step, 1)
                else:
                    nc.vector.scalar_tensor_tensor(dst, silu[m % 2][0:rows, :], 1.0 / NS, ps[0:rows, 3 + 3 * (m % 2), :],
                                                   ALU.mult, ALU.mult).then_inc(hid_step, 1)
            for b in range(B):
                dve.wait_ge(down_mm, b + 1)
                nc.vector.tensor_tensor(x[:, b, :], x[:, b, :], ps[:, b, 0:D], ALU.add).then_inc(x_final, 1)

        @block.tensor
        def _(pe):
            pe.wait_ge(ident_ready, 2)
            pe.wait_ge(raw_loaded, 96)
            nc.tensor.matmul(ps[:, 0, 0:D], raw_w[:, 0, :], raw_w[:, 1, :], start=True, stop=True)
            for i in range(3):
                nc.tensor.transpose(ps[:, 0, (i + 1) * D:(i + 2) * D], raw_w[:, 2 + i, :] if i == 0 else
                                    raw_w[:, 2 + i, :], ident[:])
            nc.tensor.transpose(ps[:, 1, 0:D], raw_w[:, 5, :], ident[:]).then_inc(small_mm, 1)
            norm_tensor(pe, 0)
            pe.wait_ge(small_ready, 2)
            pe.wait_ge(ln_done, 1)
            nc.tensor.matmul(ps[:, 4, :], wqk0, xn_t[:], start=True, stop=True).then_inc(qk_mm, 1)

            def transpose_group(n):
                if n % GB == 0:
                    pe.wait_ge(ctx_loaded[n // GB], 16)
                if n >= 2:
                    pe.wait_ge(ct_ready, n - 1)
                for c in range(4):
                    tr = nc.tensor.transpose(ps[:, n % 2, c * P:(c + 1) * P], ctx_sb[:, 4 * n + c, :], ident[:])
                tr.then_inc(ct_trans, 1)

            def project_group(n):
                pe.wait_ge(ct_ready, n + 1)
                if n >= 1:
                    pe.wait_ge(k_left1, n)
                nc.tensor.matmul(ps[:, 2, :], wk1_t, ctx_t[:, n * BANK:(n + 1) * BANK], start=True, stop=True)\
                  .then_inc(k_mm, 1)
                if n >= 1:
                    pe.wait_ge(v_ready, n)
                for c in range(4):
                    mm = nc.tensor.matmul(ps[:, 3, c * P:(c + 1) * P], ctx_t[:, (4 * n + c) * P:(4 * n + c + 1) * P],
                                          wv1_t, start=True, stop=True)
                mm.then_inc(v_mm, 1)

            def scores(b):
                if b >= 1:
                    pe.wait_ge(p0_ready, b)
                pe.wait_ge(ct_ready, GB * (b + 1))
                for j in range(GB):
                    key0 = (GB * b + j) * BANK
                    mm = nc.tensor.matmul(ps[:, 4 + j, :], aux_t[:, b * S:(b + 1) * S], ctx_t[:, key0:key0 + BANK],
                                          start=True, stop=True)
                mm.then_inc(s0_mm, 1)

            def transpose_probs(b):
                pe.wait_ge(s0_exp, b + 1)
                for c in range(KC):
                    tr = nc.tensor.transpose(ps[:, 4 + c // 4, (c % 4) * S:(c % 4 + 1) * S],
                                             scores0[b % 2][:, c * P:(c + 1) * P], ident[:])
                tr.then_inc(p0_trans, 1)

            def attend(b):
                pe.wait_ge(p0_ready, b + 1)
                pe.wait_ge(v_ready, min(GB * (b + 2), GROUPS))
                for c in range(KC):
                    mm = nc.tensor.matmul(ps[:, 3, 0:S], ctx_sb[:, b * KC + c, :], probs0_t[:, c, :],
                                          start=(c == 0), stop=(c == KC - 1))
                mm.then_inc(o1_mm, 1)
                pe.wait_ge(o1_ready, b + 1)
                pe.wait_ge(k_left1, min(GB * (b + 2), GROUPS))
                nc.tensor.matmul(ps[:, 2, 0:D], o1_t, wv0_t, start=True, stop=True).then_inc(y0_mm, 1)

            pe.wait_ge(qk_ready, 1)
            for b in range(B + 1):
                if b < B:
                    for j in range(GB):
                        n = GB * b + j
                        transpose_group(n)
                        if j >= 1:
                            if j == 1 and b >= 2:
                                pe.wait_ge(x_done, b - 1)
                            project_group(n - 1)
                    project_group(n)
                if b >= 1:
                    transpose_probs(b - 1)
                if b < B:
                    scores(b)
                if b >= 1:
                    attend(b - 1)
            pe.wait_ge(rows_loaded, ROW_LOADS)
            nc.tensor.transpose(ps[:, 1, 0:BR0 + BR1], b1_rows[:], ident[0:BR0 + BR1, 0:BR0 + BR1]).then_inc(cols_mm, 1)
            norm_tensor(pe, 1)
            pe.wait_ge(attn0_loaded, 48)
            pe.wait_ge(cols_ready, 1)
            pe.wait_ge(ln_done, 2)
            for i in range(PAIRS):
                if i >= 2:
                    pe.wait_ge(q0_ready, i - 1)
                nc.tensor.matmul(ps[:, i % 2, :], w_qkv[:, 0, 2 * DH * i:2 * DH * (i + 1)], xn_t[:],
                                 start=True, stop=True).then_inc(q0_mm, 1)
                if i >= 2:
                    pe.wait_ge(k0_ready, i - 1)
                nc.tensor.matmul(ps[:, 2 + i % 2, :], w_qkv[:, 1, 2 * DH * i:2 * DH * (i + 1)], xn_t[:],
                                 start=True, stop=True).then_inc(k0_mm, 1)

            def scores_heads(b):
                for i in range(PAIRS):
                    for odd in range(2):
                        rows = slice(DH * odd, DH * (odd + 1))
                        mm = nc.tensor.matmul(ps[:, 2 * odd + i // 4, (i % 4) * S:(i % 4 + 1) * S],
                                              q0_t[rows, i, b * S:(b + 1) * S], k0_t[rows, i, b * S:(b + 1) * S],
                                              start=True, stop=True)
                mm.then_inc(s1_mm, 1)

            pe.wait_ge(q0_ready, PAIRS)
            pe.wait_ge(k0_ready, PAIRS)
            scores_heads(0)
            for b in range(B):
                if b >= 1:
                    pe.wait_ge(v0_ready_s, b)
                nc.tensor.matmul(ps[:, 4, :], xn_t[:, b * S:(b + 1) * S], w_qkv[:, 2, 0:BANK],
                                 start=True, stop=True).then_inc(v0_mm, 1)
                if b >= 1:
                    pe.wait_ge(v0_ready_v, b)
                nc.tensor.matmul(ps[:, 5, :], xn_t[:, b * S:(b + 1) * S], w_qkv[:, 2, BANK:2 * BANK],
                                 start=True, stop=True).then_inc(v0_mm, 1)
            pe.wait_ge(v0_ready_s, B)
            pe.wait_ge(v0_ready_v, B)
            for b in range(B):
                if b + 1 < B:
                    pe.wait_ge(s1_exp, b + 1)
                    scores_heads(b + 1)
                pe.wait_ge(s1_norm, 2 * b + 2)
                for j in range(4):
                    n = 4 * b + j
                    if n >= 2:
                        pe.wait_ge(p1_ready, n - 1)
                    for c in range(4):
                        tr = nc.tensor.transpose(ps[:, 4 + j % 2, c * S:(c + 1) * S], probs1[b % 2][:, 4 * j + c, :],
                                                 ident[:])
                    tr.then_inc(p1_trans, 1)
                pe.wait_ge(p1_ready, 4 * (b + 1))
                if b >= 1:
                    pe.wait_ge(h1_ready, b)
                for i in range(PAIRS):
                    for odd in range(2):
                        at = (PAIRS * odd + i) * S
                        head = 2 * i + odd
                        mm = nc.tensor.matmul(ps[DH * odd:DH * (odd + 1), 6 + i // 4, (i % 4) * S:(i % 4 + 1) * S],
                                              v0[:, b, head * DH:(head + 1) * DH], probs1_t[b % 2][:, at:at + S],
                                              start=True, stop=True)
                mm.then_inc(h1_mm, 1)
            pe.wait_ge(s1_exp, B)
            for b in range(B):
                pe.wait_ge(h1_ready, b + 1)
                for i in range(PAIRS):
                    mm = nc.tensor.matmul(ps[:, b, 0:D], heads_t[:, i, b * S:(b + 1) * S], w_out0[:, i, :],
                                          start=(i == 0), stop=(i == PAIRS - 1))
                mm.then_inc(y1_mm, 1)

            norm_tensor(pe, 2)
            pe.wait_ge(consts, 1)
            pe.wait_ge(ln_done, 3)
            for b in range(B):
                nc.tensor.matmul(ps[:, 0, b * E0:(b + 1) * E0], xn_t[:, b * S:(b + 1) * S], gate_w[:],
                                 start=True, stop=False)
                mm = nc.tensor.matmul(ps[:, 0, b * E0:(b + 1) * E0], ones_row[:], gate_b[:], start=False, stop=True)
            mm.then_inc(lg0_mm, 1)
            pe.wait_ge(ffn0_loaded, 32)

            def hidden(i):
                if i >= 3:
                    last = i - 3
                    pe.wait_ge(h0_even if last % 2 == 0 else h0_odd, last // 2 + 1)
                nc.tensor.matmul(ps[:, 1 + i % 3, :], w1_0[:, i // HC0, i % HC0, :], xn_t[:], start=True, stop=True)\
                  .then_inc(h0_mm, 1)

            def expert(e):
                pe.wait_ge(h0_even, e + 1)
                pe.wait_ge(h0_odd, e + 1)
                if e >= 2:
                    pe.wait_ge(x_moe, B * e)
                for b in range(B):
                    for k in range(HC0):
                        mm = nc.tensor.matmul(ps[:, 4 + e % 2, b * D:(b + 1) * D], h0_t[:, HC0 * e + k, b * S:(b + 1) * S],
                                              w2_0[:, e, k, :], start=(k == 0), stop=(k == HC0 - 1))
                mm.then_inc(e0_mm, 1)

            def key_norms(e):
                for i in (0, 1):
                    n = 2 * e + i
                    if n >= 2:
                        pe.wait_ge(kn_max, n - 1)
                    nc.tensor.matmul(ps[0:HH, 6 * i, :], of_half_h, k_square[:, n * BANK:(n + 1) * BANK],
                                     start=True, stop=True).then_inc(kn_mm, 1)

            for i in range(6):
                hidden(i)
            pe.wait_ge(gate_step, 5)
            for b in range(B):
                tr = nc.tensor.transpose(ps[0:E0, 7, b * S:(b + 1) * S], gates0[:, b, :], ident[:])
            tr.then_inc(g0_trans, 1)
            pe.wait_ge(g0_ready, 1)
            for b in range(B):
                mm = nc.tensor.matmul(ps[:, 7, b * D:(b + 1) * D], gates0_t[:, b * S:(b + 1) * S], b2_0[:],
                                      start=True, stop=True)
            mm.then_inc(b2_mm, 1)
            for e in range(E0):
                for i in (2 * e + 6, 2 * e + 7):
                    if i < E0 * HC0:
                        hidden(i)
                expert(e)
                if e == 0:
                    pe.wait_ge(consts_d, 1)
                    pe.wait_ge(ksq_ready, 1)
                key_norms(e)
            pe.wait_ge(kn_max, GROUPS)
            norm_tensor(pe, 3)
            pe.wait_ge(ln_done, 4)
            nc.tensor.matmul(ps[:, 0, :], wq1_t, xn_t[:], start=True, stop=True).then_inc(q1_mm, 1)
            pe.wait_ge(q1_square, 1)
            nc.tensor.matmul(ps[0:HH, 1, :], of_half, aux_t[:], start=True, stop=True).then_inc(qn_mm, 1)
            pe.wait_ge(bound_step, 2)
            nc.tensor.transpose(ps[0:1, 2, 0:HH], bound_h, ident[0:HH, 0:HH]).then_inc(bound_trans, 1)
            pe.wait_ge(q_rows_zero, 1)
            pe.wait_ge(q_rows_loaded, 16 * HG * len(PAIRS_QK))
            pe.wait_ge(ring_ones, 1)
            pe.wait_ge(safe_ready, 1)
            is_safe = pe.value_load(safe)
            with pe.If(is_safe < 1):
                pe.sem_inc(shift_maxed, 2)
                pe.sem_inc(shift_mm, 4 * SLOTS)
                with pe.Fori(0, B) as b:
                    for g in range(HG):
                        pe.wait_ge(shift_loaded[g % SLOTS], (b * (HG // SLOTS) + (g // SLOTS + 1)) * (16 * len(PAIRS_QK)))
                        for j in range(4):
                            h = 4 * g + j
                            pe.wait_ge(shift_maxed, b * HH + (h + 1))
                            for n in range(4):
                                mm = nc.tensor.matmul(ps[:, 4 * (h % 2) + n, :],
                                                      q_rows[0:KROWS, bass.ds(b * (HG * BANK) + (g * BANK + j * S), S)],
                                                      key_ring[0:KROWS, g % SLOTS, n * BANK:(n + 1) * BANK],
                                                      start=True, stop=True)
                            mm.then_inc(shift_mm, 1)
                pe.wait_ge(shift_step, 4)
                for n in range(ITEMS):
                    if n >= 2:
                        pe.wait_ge(shift_rows, n - 1)
                    nc.tensor.matmul(ps[0:12, n % 2, 0:S], shift_parts[:, n, :, :].rearrange("p g c -> p (g c)"),
                                     ident_h[:], start=True, stop=True).then_inc(shift_trans, 1)
                pe.wait_ge(shift_rows, ITEMS)

            pe.sem_inc(scores_mm, NU * SLOTS)
            pe.sem_inc(exp_done, 2)
            pe.sem_inc(pv_done, 2 * QUADS)
            pe.sem_inc(acc_copied, 1)
            pe.sem_inc(folded, 1)

            def score_unit(b, g, k):
                if k == 0:
                    pe.wait_ge(ring_loaded[g % SLOTS], (b * (HG // SLOTS) + (g // SLOTS + 1)) * (16 * len(PAIRS_QK)))
                pe.wait_ge(exp_done, b * (HG * NU) + (NU * g + k + 1))
                c, n = UNITS[k]
                for i in range(n):
                    mm = nc.tensor.matmul(ps[:, 3 * (k % 2) + i, :], key_ring[0:ROWS, g % SLOTS, (c + i) * P:(c + i + 1) * P],
                                          q_rows[0:ROWS, bass.ds(b * (HG * BANK) + g * BANK, BANK)],
                                          start=True, stop=True)
                mm.then_inc(scores_mm, 1)

            def weigh_quad(b, g, w):
                if w == 0:
                    pe.wait_ge(acc_copied, b * HG + (g + 1))
                    pe.wait_ge(staged, b * HG + (g + 1))
                pe.wait_ge(exp_done, b * (HG * NU) + (NU * g + UNIT_OF[w] + 3))
                for n in range(4):
                    c = 4 * w + n
                    mm = nc.tensor.matmul(ps[32 * n:32 * (n + 1), 6, :], v_stage[:, g % 2, c, :],
                                          probs_d[c // 8][:, (c % 8) * BANK:(c % 8 + 1) * BANK],
                                          start=(w == 0), stop=(w == QUADS - 1))
                mm.then_inc(pv_done, 1)

            def fold_item(b, g):
                pe.wait_ge(acc_copied, b * HG + (g + 2))
                pe.wait_ge(folded, b * HG + (g + 1))
                for j in range(4):
                    mm = nc.tensor.matmul(ps[:, 7, VCOLS * j:VCOLS * (j + 1)], acc_sb[:, g % 2, j * S:(j + 1) * S],
                                          fold[:, VCOLS * (j // 2):VCOLS * (j // 2 + 1)], start=True, stop=True)
                mm.then_inc(fold_mm, 1)

            def items(b, last):
                for g in range(HG):
                    more = g + 1 < HG
                    score_unit(b, g, 2)
                    if g >= 1:
                        fold_item(b, g - 1)
                    score_unit(b, g, 3)
                    weigh_quad(b, g, 0)
                    score_unit(b, g, 4)
                    weigh_quad(b, g, 1)
                    score_unit(b, g, 5)
                    for k in (0, 1):
                        if more:
                            score_unit(b, g + 1, k)
                        elif not last:
                            score_unit(b + 1, 0, k)
                        weigh_quad(b, g, 2 + k)
                fold_item(b, HG - 1)

            score_unit(0, 0, 0)
            score_unit(0, 0, 1)
            with pe.Fori(0, B - 1) as b:
                items(b, False)
            items(B - 1, True)
            pe.wait_ge(lin_loaded, 16 * 16)
            pe.wait_ge(folded, ITEMS + 1)
            norm_tensor(pe, 4)
            nc.tensor.transpose(ps[:, 7, 0:E1], w_gate, ident[0:E1, 0:E1]).then_inc(wg_trans, 1)
            pe.wait_ge(ln_done, 5)
            for b in range(B):
                nc.tensor.matmul(ps[:, b, 0:3 * D], xn_t[:, b * S:(b + 1) * S], w_qkv1, start=True, stop=False)
                mm = nc.tensor.matmul(ps[:, b, 0:3 * D], ones_row[:], b_qkv1, start=False, stop=True)
            mm.then_inc(lin_mm, 1)
            pe.wait_ge(lin_step, 6)
            for b in range(B):
                tr = nc.tensor.transpose(ps[:, 5, b * S:(b + 1) * S], qk1[:, b, 0:D], ident[:])
            tr.then_inc(qn_trans, 1)
            pe.wait_ge(lin_v, 1)
            for b in range(B):
                mm = nc.tensor.matmul(ps[:, 4, b * D:(b + 1) * D], qk1[:, b, D:2 * D], v1s[:, b, :], start=True, stop=True)
            mm.then_inc(kv_mm, 1)
            pe.wait_ge(qn_ready, 1)
            pe.wait_ge(kv_ready, 3)
            for b in range(B):
                mm = nc.tensor.matmul(ps[:, 6, b * S:(b + 1) * S], kv_diag[:, b, :], qn_t[:, b * S:(b + 1) * S],
                                      start=True, stop=True)
            mm.then_inc(lc_mm, 1)
            pe.wait_ge(wg_ready, 1)
            pe.wait_ge(lc_ready, 1)
            for b in range(B):
                nc.tensor.matmul(ps[:, 7, b * D:(b + 1) * D], lin_t[:, b * S:(b + 1) * S], w_out1, start=True, stop=False)
                mm = nc.tensor.matmul(ps[:, 7, b * D:(b + 1) * D], ones_row[:], b_out1, start=False, stop=True)
            mm.then_inc(lo_mm, 1)
            pe.wait_ge(lin_step, 9)
            for b in range(B):
                tr = nc.tensor.transpose(ps[:, 5, b * S:(b + 1) * S], attn1[:, b, :], ident[:])
            tr.then_inc(a1_trans, 1)
            pe.wait_ge(a1_ready, 1)
            for k in range(FC):
                nc.tensor.matmul(ps[:, k, :], w1_1[:, k * P:(k + 1) * P], attn1_t, start=True, stop=True).then_inc(f1_mm, 1)
            pe.wait_ge(f1_ready, FC)
            for b in range(B):
                for k in range(FC):
                    nc.tensor.matmul(ps[:, 4, b * D:(b + 1) * D], h1_t[:, k, b * S:(b + 1) * S], w2_1[:, k, :],
                                     start=(k == 0), stop=False)
                mm = nc.tensor.matmul(ps[:, 4, b * D:(b + 1) * D], ones_row[:], b2_1, start=False, stop=True)
            mm.then_inc(f2_mm, 1)

            norm_tensor(pe, 7)
            pe.wait_ge(moe1_loaded, 96)
            pe.wait_ge(ln_done, 6)
            for b in range(B):
                mm = nc.tensor.matmul(ps[:, 0, b * E1:(b + 1) * E1], xn_t[:, b * S:(b + 1) * S], wg_t, start=True, stop=True)
            mm.then_inc(lg1_mm, 1)

            def gate_and_up(m):
                rows = P if m < EC else NS * I1
                if m >= 2:
                    pe.wait_ge(hid_step, m - 1)
                for i in range(2):
                    mm = nc.tensor.matmul(ps[0:rows, 2 + i + 3 * (m % 2), :], gate_up[:, i, m * P:m * P + rows],
                                          xn_t[:], start=True, stop=True)
                return mm

            def weights_of(m):
                return nc.tensor.matmul(ps[:, 4 + 3 * (m % 2), :], spread[:, m * P:(m + 1) * P], gate1_t,
                                        start=True, stop=True)

            gate_and_up(0)
            gate_and_up(1)
            pe.wait_ge(g1_step, 8)
            for b in range(B):
                tr = nc.tensor.transpose(ps[0:E1, 1, b * S:(b + 1) * S], gate1[:, b, :], ident[:])
            tr.then_inc(g1_trans, 1)
            pe.wait_ge(g1_ready, 1)
            pe.wait_ge(spread_ready, 1)
            weights_of(0).then_inc(gu_mm, 1)
            weights_of(1).then_inc(gu_mm, 1)
            for m in range(2, EC):
                gate_and_up(m)
                weights_of(m).then_inc(gu_mm, 1)
            gate_and_up(EC).then_inc(gu_mm, 1)
            pe.wait_ge(hid_step, EC + 1)
            for b in range(B):
                for m in range(EC + 1):
                    rows = P if m < EC else NS * I1
                    mm = nc.tensor.matmul(ps[:, b, 0:D], hid1_t[0:rows, m * T + b * S:m * T + (b + 1) * S],
                                          down[0:rows, m, :], start=(m == 0), stop=(m == EC))
                mm.then_inc(down_mm, 1)


def kernel(**inputs):
    import numpy as np
    import concourse.bacc as bacc
    from concourse.bass_utils import run_bass_kernel_spmd

    nc = bacc.Bacc("TRN2", target_bir_lowering=False, num_devices=1)
    arrays, tensors = {}, {}
    for name in NAMES:
        a = np.ascontiguousarray(inputs[name])
        arrays["in_" + name] = a
        tensors[name] = nc.dram_tensor("in_" + name, a.shape, mybir.dt.from_np(a.dtype), kind="ExternalInput").ap()
    out = nc.dram_tensor("out_x", inputs['x'].shape, F32, kind="ExternalOutput").ap()
    build_program(nc, tensors, out)
    r = run_bass_kernel_spmd(nc, [arrays], core_ids=[0])
    return r.results[0]["out_x"]
```

```python
from contextlib import ExitStack

import concourse.bass as bass
from concourse import mybir

ALU = mybir.AluOpType
ACT = mybir.ActivationFunctionType
AX = mybir.AxisListType
F32 = mybir.dt.float32
BF16 = mybir.dt.bfloat16
I32 = mybir.dt.int32

NAMES = ['x', 'ctx_1024', 'mask_BxS2_ik1', 'L0_xattn_Wq', 'L0_xattn_Wk', 'L0_xattn_Wv', 'L0_attn_kernel',
         'L0_attn_WO', 'L0_ffn_gate_w', 'L0_ffn_gate_b', 'L0_ffn_w1', 'L0_ffn_b1', 'L0_ffn_w2', 'L0_ffn_b2',
         'L1_xattn_Wq', 'L1_xattn_Wk', 'L1_xattn_Wv', 'L1_xattn_lambda_q1', 'L1_xattn_lambda_q2',
         'L1_xattn_lambda_k1', 'L1_xattn_lambda_k2', 'L1_attn_Wq', 'L1_attn_bq', 'L1_attn_Wk', 'L1_attn_bk',
         'L1_attn_Wv', 'L1_attn_bv', 'L1_attn_Wo', 'L1_attn_bo', 'L1_attn_g1', 'L1_attn_be1', 'L1_attn_W1',
         'L1_attn_b1', 'L1_attn_W2', 'L1_attn_b2', 'L1_attn_g2', 'L1_attn_be2', 'L1_ffn_Wg',
         'L1_ffn_W_gate_up', 'L1_ffn_W_down', 'L1_ffn_Ws_gate_up', 'L1_ffn_Ws_down']


def build_program(nc, t, out):
    P = 128
    B, S, D = t['x'].shape
    T = B * S
    KEYS = t['ctx_1024'].shape[1]
    KC = KEYS // P
    NCHUNK = B * KC
    BANK = 512
    GROUPS = NCHUNK * P // BANK
    GB = KEYS // BANK
    assert S == P and D == P

    with ExitStack() as ctx:
        def sb(name, shape, dt=F32):
            return ctx.enter_context(nc.sbuf_tensor(name, shape, dt))

        def sem(name):
            return ctx.enter_context(nc.semaphore(name))

        ps = ctx.enter_context(nc.psum_tensor("ps", [P, 8, BANK], F32))
        x = sb("x_res", [P, B, D])
        xn = sb("xn", [P, B, D])
        xn_t = sb("xn_t", [P, T])
        aux_t = sb("aux_t", [P, T])
        ident = sb("ident", [P, P])
        ident_h = sb("ident_h", [P, P], BF16)
        stats = sb("stats", [P, B, 6])
        mean_var = sb("mean_var", [P, B, 2])
        var_eps = sb("var_eps", [P, B])
        rstd = sb("rstd", [P, B])
        minus_half = sb("minus_half", [P, 64])
        small_w = sb("small_w", [P, 5, D])
        wqk0, wv0_t, wk1_t, wv1_t, wq1_t = (small_w[:, i, :] for i in range(5))

        wide = sb("wide", [P, 16384])
        work = sb("work", [P, 8192])
        weights = sb("weights", [P, 4096])
        k_parts = sb("k_parts", [P, 3, NCHUNK * P], BF16)
        v1 = sb("v1", [P, NCHUNK, D])

        ctx_sb = wide[:, 0:8192].rearrange("p (c f) -> p c f", f=D)
        ctx_t = wide[:, 8192:16384]
        scores0 = [work[:, 2048 * i:2048 * (i + 1)] for i in range(2)]
        probs0_t = work[:, 4096:6144].rearrange("p (c s) -> p c s", s=S)
        mask_sb = work[:, 6144:8192].bitcast(I32)
        raw_w = k_parts[:, 2, 6144:8192].bitcast(F32)[:, 0:768].rearrange("p (i f) -> p i f", f=D)
        max0 = sb("max0", [P, B, 2])
        nmax0 = sb("nmax0", [P, B])
        sum0 = sb("sum0", [P, B, 2])
        rsum0 = sb("rsum0", [P, B])
        o1_t = xn[:, 0, :]

        HEADS, DH = t['L0_attn_kernel'].shape[1], t['L0_attn_kernel'].shape[3]
        PAIRS = HEADS // 2
        SCALE0 = 1.0 / (DH * DH * HEADS)
        w_qkv = weights[:, 0:3 * HEADS * DH].rearrange("p (c n) -> p c n", c=3)
        w_out0 = weights[:, 3 * HEADS * DH:4096].rearrange("p (i m) -> p i m", i=PAIRS)
        k_left = weights[:, 3 * HEADS * DH:4096].rearrange("p (i c) -> p i c", i=2)
        q0_t = wide[:, 0:4096].rearrange("p (i c) -> p i c", i=PAIRS)
        k0_t = wide[:, 4096:8192].rearrange("p (i c) -> p i c", i=PAIRS)
        v0 = wide[:, 8192:12288].rearrange("p (b n) -> p b n", b=B)
        heads_t = wide[:, 12288:16384].rearrange("p (i c) -> p i c", i=PAIRS)
        probs1 = [work[:, 2048 * i:2048 * (i + 1)].rearrange("p (h c) -> p h c", h=HEADS) for i in range(2)]
        probs1_t = [work[:, 4096 + 2048 * i:6144 + 2048 * i] for i in range(2)]
        max1 = sb("max1", [P, B, HEADS])
        nmax1 = sb("nmax1", [P, B, HEADS])
        sum1 = sb("sum1", [P, B, HEADS])
        rsum1 = sb("rsum1", [P, B, HEADS])

        E0 = t['L0_ffn_gate_w'].shape[1]
        HC0 = t['L0_ffn_w1'].shape[2] // P
        NEVER = 3.0e38
        ROW_LOADS = 16 * (5 + 4)
        w1_0 = wide[:, 4096:6144].rearrange("p (e k c) -> p e k c", e=E0, k=HC0)
        w2_0 = wide[:, 6144:8192].rearrange("p (e k c) -> p e k c", e=E0, k=HC0)
        h0_t = wide[:, 8192:16384].rearrange("p (i c) -> p i c", i=E0 * HC0)
        lam_load = sb("lam_load", [P, 4, 4])
        ones_row = sb("ones_row", [1, P])
        gate_w = sb("gate_w", [P, E0])
        gate_b = sb("gate_b", [P, E0])
        b2_0 = sb("b2_0", [E0, D])
        BR0, BR1 = E0 * HC0, 4
        b1_rows = sb("b1_rows", [BR0 + BR1, P])
        b1_cols = sb("b1_cols", [P, BR0 + BR1])
        logits0 = sb("logits0", [P, B, 2 * E0])
        top0 = sb("top0", [P, B, 8])
        picks0 = sb("picks0", [P, B, 8])
        struck0 = sb("struck0", [P, B, 2 * E0])
        ntop0 = sb("ntop0", [P, B])
        gate_e = sb("gate_e", [P, B, E0])
        gate_sum = sb("gate_sum", [P, B])
        gate_r = sb("gate_r", [P, B])
        gates0 = sb("gates0", [P, B, E0])
        gates0_t = aux_t[0:E0, :]
        HH = 32
        HG = HH // 4
        ITEMS = B * HG
        PAIRS_QK = ((0, 0), (0, 1), (0, 2), (1, 0), (1, 1), (2, 0))
        KROWS = 16 * len(PAIRS_QK)
        ROWS = KROWS + 12
        RING_LOADS = 16 * len(PAIRS_QK)
        SCALE1 = 0.5
        UNIT = 2
        NBUF = 3
        UNITS = []
        for g in range(HG):
            UNITS.append([(c, UNIT) for c in range(0, KC, UNIT)])
            if g % 4 == 3:
                UNITS[g][-1:] = [(KC - 2, 1), (KC - 1, 1)]
        UNIT0 = [sum(len(u) for u in UNITS[:g]) for g in range(HG + 1)]
        NU = UNIT0[HG]
        QUADS = KC // 4
        GI = 4
        SLOTS = 4
        VCOLS = 9
        LIMIT = 64.0
        probs_d = (wide[:, 0:4096], weights[:, 0:4096])
        k_square = wide[:, 0:4096].bitcast(BF16)
        q_rows = wide[:, 4096:12288].bitcast(BF16)
        acc_sb = wide[:, 12288:13312].rearrange("p (i c) -> p i c", i=2)
        heads_d = wide[:, 13312:14464].rearrange("p (i v) -> p i v", v=VCOLS)
        q_parts = wide[:, 14464:15232].bitcast(BF16).rearrange("p (i c) -> p i c", i=3)
        shift_parts = wide[:, 15232:15424].bitcast(BF16).rearrange("p (i g c) -> p i g c", i=ITEMS, g=3)
        key_ring = work[:, 0:4096].bitcast(BF16).rearrange("p (i c) -> p i c", i=SLOTS)
        q_masked = work[:, 4096:7168].bitcast(BF16).rearrange("p (i b j c) -> p i b j c", i=3, b=B, j=4)
        v_stage = work[:, 7168:8192].rearrange("p (i c v) -> p i c v", i=2, c=KC)
        small_d = small_w.rearrange("p i f -> p (i f)")
        of_half = small_d[:, 32:64]
        of_half_h = small_d[:, 64:80].bitcast(BF16)
        of_j = small_d[:, 80:84]
        of_j12 = small_d[:, 84:88]
        lam_prod = small_d[:, 104:112].rearrange("p (a f) -> p a f", a=2)
        lam_sum = small_d[:, 112:114]
        lam_exp = small_d[:, 114:116]
        neg_lam = small_d[:, 116:117]
        k_norms = small_d[0:HH, 120:136]
        k_norm = small_d[0:HH, 136:137]
        q_norm = small_d[0:HH, 137:138]
        bound_h = small_d[0:HH, 138:139]
        bound = small_d[0:1, 139:140]
        safe = small_d[0:1, 140:141].bitcast(I32)
        shift_max = small_d[:, 144:272]
        shift_left = small_d[:, 272:400]
        den_r = small_d[:, 144:272]
        HEADS1 = 16
        DH1 = D // HEADS1
        FC = t['L1_attn_W1'].shape[1] // P
        w_qkv1 = work[:, 4096:4480]
        w_out1 = work[:, 4480:4608]
        w1_1 = work[:, 4608:5120]
        w2_1 = work[:, 5120:5632].rearrange("p (k c) -> p k c", k=FC)
        w_gate = work[0:32, 5632:5760]
        b_qkv1 = work[0:1, 5760:6144]
        b_out1 = work[0:1, 6144:6272]
        b2_1 = work[0:1, 6272:6400]
        affine = aux_t[:].rearrange("p (i f) -> p i f", i=4)
        qk1 = wide[:, 0:1024].rearrange("p (b n) -> p b n", b=B)
        v1s = wide[:, 1024:1536].rearrange("p (b n) -> p b n", b=B)
        qk_low = wide[:, 1536:2560].rearrange("p (b n) -> p b n", b=B)
        qk_sq = wide[:, 2560:3584].rearrange("p (b n) -> p b n", b=B)
        qk_norm = wide[:, 3584:3712]
        of_eight = wide[:, 3712:3728]
        kv_diag = wide[:, 3728:4240].rearrange("p (b n) -> p b n", b=B)
        qn_t = wide[:, 4240:4752]
        lin_t = wide[:, 4752:5264]
        res1 = wide[:, 5264:5776].rearrange("p (b n) -> p b n", b=B)
        attn1 = wide[:, 5776:6288].rearrange("p (b n) -> p b n", b=B)
        attn1_t = wide[:, 6288:6800]
        h1_t = wide[:, 6800:8848].rearrange("p (k c) -> p k c", k=FC)
        qk_rs = wide[:, 8848:8976]
        qk_root = wide[:, 8976:9104]
        qk_res = qk1.rearrange("p b n -> p (b n)")[:, 0:512].rearrange("p (b n) -> p b n", b=B)

        E1, I1 = t['L1_ffn_W_down'].shape[0:2]
        NS = t['L1_ffn_Ws_down'].shape[0]
        EC = E1 * I1 // P
        EPC = P // I1
        gate_up = weights[:, 0:(E1 + NS) * 2 * I1].rearrange("p (i n) -> p i n", i=2)
        down = weights[:, 2304:2304 + (EC + 1) * D].rearrange("p (m c) -> p m c", c=D)
        wg_t = wide[:, 9216:9216 + E1]
        spread = wide[0:E1, 9728:9728 + E1 * I1]
        logits1 = wide[:, 10752:10880].rearrange("p (b e) -> p b e", b=B)
        struck1 = wide[:, 10880:11008].rearrange("p (b e) -> p b e", b=B)
        gate1 = wide[:, 11008:11136].rearrange("p (b e) -> p b e", b=B)
        top1 = wide[:, 11136:11168].rearrange("p (b e) -> p b e", b=B)
        ntop1 = wide[:, 11168:11172]
        gsum1 = wide[:, 11172:11176]
        grec1 = wide[:, 11176:11180]
        gate1_t = wide[0:E1, 11264:11776]
        silu = [wide[:, 11776 + 512 * i:12288 + 512 * i] for i in range(2)]
        hid1_t = work[:, 0:(EC + 1) * T]
        x_loaded = sem("x_loaded")
        raw_loaded = sem("raw_loaded")
        ctx_loaded = [sem(f"ctx_loaded{b}") for b in range(B)]
        mask_loaded = sem("mask_loaded")
        ident_zero = sem("ident_zero")
        ident_ready = sem("ident_ready")
        half_ready = sem("half_ready")
        ln_step = sem("ln_step")
        ln_rstd = sem("ln_rstd")
        ln_xn = sem("ln_xn")
        ln_trans = sem("ln_trans")
        ln_done = sem("ln_done")
        small_mm = sem("small_mm")
        small_ready = sem("small_ready")
        qk_mm = sem("qk_mm")
        qk_ready = sem("qk_ready")
        ct_trans = sem("ct_trans")
        ct_ready = sem("ct_ready")
        k_mm = sem("k_mm")
        v_mm = sem("v_mm")
        k_first = sem("k_first")
        k_left1 = sem("k_left1")
        k_second = sem("k_second")
        k_third = sem("k_third")
        v_ready = sem("v_ready")
        s0_mm = sem("s0_mm")
        s0_fill = sem("s0_fill")
        s0_masked = sem("s0_masked")
        s0_max = sem("s0_max")
        s0_exp = sem("s0_exp")
        s0_rsum = sem("s0_rsum")
        p0_trans = sem("p0_trans")
        p0_ready = sem("p0_ready")
        o1_mm = sem("o1_mm")
        o1_ready = sem("o1_ready")
        y0_mm = sem("y0_mm")
        x_done = sem("x_done")
        stored = sem("stored")

        qkv0_loaded = sem("qkv0_loaded")
        attn0_loaded = sem("attn0_loaded")
        q0_mm = sem("q0_mm")
        k0_mm = sem("k0_mm")
        v0_mm = sem("v0_mm")
        q0_ready = sem("q0_ready")
        k0_ready = sem("k0_ready")
        v0_ready = sem("v0_ready")
        s1_mm = sem("s1_mm")
        s1_max = sem("s1_max")
        s1_exp = sem("s1_exp")
        s1_norm = sem("s1_norm")
        p1_trans = sem("p1_trans")
        p1_ready = sem("p1_ready")
        h1_mm = sem("h1_mm")
        h1_ready = sem("h1_ready")
        y1_mm = sem("y1_mm")
        rows_loaded = sem("rows_loaded")
        consts = sem("consts")
        cols_mm = sem("cols_mm")
        cols_ready = sem("cols_ready")
        ffn0_loaded = sem("ffn0_loaded")
        lg0_mm = sem("lg0_mm")
        picks0_step = sem("picks0_step")
        gate_exp = sem("gate_exp")
        gate_step = sem("gate_step")
        g0_trans = sem("g0_trans")
        g0_ready = sem("g0_ready")
        b2_mm = sem("b2_mm")
        h0_mm = sem("h0_mm")
        h0_relu = sem("h0_relu")
        e0_mm = sem("e0_mm")
        x_moe = sem("x_moe")
        consts_d = sem("consts_d")
        ksq_ready = sem("ksq_ready")
        kn_mm = sem("kn_mm")
        kn_max = sem("kn_max")
        kn_all = sem("kn_all")
        lam_step = sem("lam_step")
        lam_expd = sem("lam_expd")
        q1_mm = sem("q1_mm")
        q1_part = sem("q1_part")
        q1_left = sem("q1_left")
        q1_square = sem("q1_square")
        qn_mm = sem("qn_mm")
        bound_step = sem("bound_step")
        bound_trans = sem("bound_trans")
        safe_ready = sem("safe_ready")
        q_masked_ready = sem("q_masked_ready")
        q_rows_zero = sem("q_rows_zero")
        q_rows_loaded = [sem(f"q_rows_loaded{i}") for i in range(SLOTS)]
        ring_ones = sem("ring_ones")
        stage_set = sem("stage_set")
        shift_loaded = [sem(f"shift_loaded{i}") for i in range(SLOTS)]
        shift_mm = sem("shift_mm")
        shift_maxed = sem("shift_maxed")
        shift_step = sem("shift_step")
        shift_trans = sem("shift_trans")
        shift_rows = sem("shift_rows")
        ring_loaded = [sem(f"ring_loaded{i}") for i in range(SLOTS)]
        scores_mm = sem("scores_mm")
        exp_done = sem("exp_done")
        pv_done = sem("pv_done")
        acc_added = sem("acc_added")
        staged = sem("staged")
        fold_mm = sem("fold_mm")
        folded = sem("folded")
        comb_step = sem("comb_step")
        x_diff = sem("x_diff")
        f2_res = sem("f2_res")
        x_lin = sem("x_lin")
        spread_ready = sem("spread_ready")
        top1_ready = sem("top1_ready")
        hid_half = sem("hid_half")
        lin_loaded = sem("lin_loaded")
        moe1_loaded = sem("moe1_loaded")
        wg_trans = sem("wg_trans")
        wg_ready = sem("wg_ready")
        lin_mm = sem("lin_mm")
        lin_step = sem("lin_step")
        lin_exp = sem("lin_exp")
        lin_v = sem("lin_v")
        lin_sq = sem("lin_sq")
        lin_root = sem("lin_root")
        kv_mm = sem("kv_mm")
        kv_ready = sem("kv_ready")
        qn_trans = sem("qn_trans")
        qn_ready = sem("qn_ready")
        lc_mm = sem("lc_mm")
        lc_ready = sem("lc_ready")
        lo_mm = sem("lo_mm")
        a1_trans = sem("a1_trans")
        a1_ready = sem("a1_ready")
        f1_mm = sem("f1_mm")
        f1_ready = sem("f1_ready")
        f2_mm = sem("f2_mm")
        lg1_mm = sem("lg1_mm")
        g1_step = sem("g1_step")
        g1_exp = sem("g1_exp")
        g1_trans = sem("g1_trans")
        g1_ready = sem("g1_ready")
        gu_mm = sem("gu_mm")
        silu_ready = sem("silu_ready")
        hid_step = sem("hid_step")
        down_mm = sem("down_mm")
        x_final = sem("x_final")
        block = ctx.enter_context(nc.Block())
        LN_BANK = 6

        def norm_vector(dve, n, eps, src=x, dst=xn):
            for b in range(B):
                st = nc.vector.bn_stats(stats[:, b, :], src[:, b, :])
            st.then_inc(ln_step, 1)
            dve.wait_ge(ln_step, 3 * n + 1)
            for b in range(B):
                ag = nc.vector.bn_aggr(mean_var[:, b, :], stats[:, b, :])
            ag.then_inc(ln_step, 1)
            dve.wait_ge(ln_step, 3 * n + 2)
            nc.vector.tensor_scalar_add(var_eps[:], mean_var[:, :, 1], eps).then_inc(ln_step, 1)
            dve.wait_ge(ln_rstd, n + 1)
            for b in range(B):
                nc.vector.tensor_scalar(dst[:, b, :], src[:, b, :], mean_var[:, b, 0:1], rstd[:, b:b + 1],
                                        ALU.subtract, ALU.mult).then_inc(ln_xn, 1)

        def norm_gpsimd(pool, n):
            pool.wait_ge(ln_step, 3 * n + 3)
            nc.gpsimd.tensor_tensor(rstd[:], var_eps[:], minus_half[:, 0:B], ALU.pow).then_inc(ln_rstd, 1)

        def norm_tensor(pe, n, src=xn):
            for b in range(B):
                pe.wait_ge(ln_xn, B * n + b + 1)
                tr = nc.tensor.transpose(ps[:, LN_BANK, b * S:(b + 1) * S], src[:, b, :], ident[:])
            tr.then_inc(ln_trans, 1)

        def norm_scalar(act, n):
            act.wait_ge(ln_trans, n + 1)
            nc.scalar.copy(xn_t[:], ps[:, LN_BANK, :]).then_inc(ln_done, 1)

        def ct_bank(n):
            return 3 * (n % 2) if n < GB else 0

        @block.sync
        def _(sp):
            sp.dma_start(x[:], t['x'].rearrange("b s f -> s b f")).then_inc(x_loaded, 16)
            for i, name in enumerate(('L0_xattn_Wq', 'L0_xattn_Wk', 'L0_xattn_Wv', 'L1_xattn_Wk',
                                      'L1_xattn_Wv', 'L1_xattn_Wq')):
                sp.dma_start(raw_w[:, i, :], t[name]).then_inc(raw_loaded, 16)
            ctx_d = t['ctx_1024'].rearrange("b (c p) f -> b p c f", p=P)
            for b in range(B):
                sp.dma_start(ctx_sb[:, b * KC:(b + 1) * KC, :], ctx_d[b]).then_inc(ctx_loaded[b], 16)
                if b >= 1:
                    sp.wait_ge(s0_masked, 2 * b)
                sp.dma_start(mask_sb, t['mask_BxS2_ik1'][b:b + 1, :].broadcast_to([P, KEYS]))\
                  .then_inc(mask_loaded, 16)
                if b == 1:
                    sp.dma_start(b1_rows[0:BR0, :], t['L0_ffn_b1'].rearrange("e (k p) -> (e k) p", p=P)).then_inc(rows_loaded, 16)
                    sp.dma_start(b1_rows[BR0:BR0 + BR1, :], t['L1_attn_b1'].rearrange("(k p) -> k p", p=P)).then_inc(rows_loaded, 16)
                    sp.dma_start(gate_w[:], t['L0_ffn_gate_w']).then_inc(rows_loaded, 16)
                    sp.dma_start(gate_b[:], t['L0_ffn_gate_b'].rearrange("(a e) -> a e", a=1).broadcast_to([P, E0])).then_inc(rows_loaded, 16)
                    sp.dma_start(b2_0[:], t['L0_ffn_b2']).then_inc(rows_loaded, 16)
                    for i, name in enumerate(('q1', 'k1', 'q2', 'k2')):
                        sp.dma_start(lam_load[:, i, :], t['L1_xattn_lambda_' + name].rearrange("(a f) -> a f", a=1)
                                      .broadcast_to([P, 4])).then_inc(rows_loaded, 16)
            sp.dma_start(w_qkv.rearrange("p c (h d) -> p c h d", h=HEADS),
                         t['L0_attn_kernel'].rearrange("c h m d -> m c h d")).then_inc(qkv0_loaded, 16)
            sp.wait_ge(k_third, GROUPS)
            wo_d = t['L0_attn_WO'][0].rearrange("(d i two) m -> two d i m", i=PAIRS, two=2)
            for i in range(2):
                sp.dma_start(w_out0[DH * i:DH * (i + 1), :, :], wo_d[i]).then_inc(attn0_loaded, 16)
            sp.wait_ge(s1_mm, B)
            sp.dma_start(w1_0.rearrange("p e k c -> p e (k c)"), t['L0_ffn_w1'].rearrange("e c h -> c e h"))\
              .then_inc(ffn0_loaded, 16)
            sp.dma_start(w2_0, t['L0_ffn_w2'].rearrange("e (k p) c -> p e k c", p=P)).then_inc(ffn0_loaded, 16)
            def load_keys(b, g, loaded):
                for r, (_, part) in enumerate(PAIRS_QK):
                    sp.dma_start(key_ring[16 * r:16 * (r + 1), g % SLOTS, :],
                                 k_parts[16 * g:16 * (g + 1), part, bass.ds(b * KEYS, KEYS)])\
                      .then_inc(loaded[g % SLOTS], 16)

            sp.wait_ge(x_done, 2 * B)
            for g in range(SLOTS):
                load_keys(0, g, ring_loaded)
            for g in range(HG):
                if g >= SLOTS:
                    sp.wait_ge(q_rows_loaded[g % SLOTS], RING_LOADS)
                for r, (part, _) in enumerate(PAIRS_QK):
                    if g == 0:
                        sp.wait_ge(q_masked_ready, 4 * (part + 1))
                    dst = q_rows[16 * r:16 * (r + 1), :].rearrange("p (b g c) -> p b g c", b=B, g=HG)[:, :, g, :]
                    src = q_masked[16 * g:16 * (g + 1), part, :, :, :].rearrange("p b j c -> p b (j c)")
                    sp.dma_start(dst, src).then_inc(q_rows_loaded[g % SLOTS], 16)

            sp.wait_ge(safe_ready, 1)
            is_safe = sp.value_load(safe)
            with sp.If(is_safe < 1):
                for i in range(SLOTS):
                    sp.wait_ge(ring_loaded[i], RING_LOADS)
                with sp.Fori(0, B) as b:
                    for g in range(HG):
                        sp.wait_ge(shift_mm, b * HH + (4 * g + 4))
                        load_keys(b, g, shift_loaded)
                for g in range(SLOTS):
                    sp.wait_ge(shift_mm, B * HH + 4 * (g + 1))
                    load_keys(0, g, shift_loaded)
            for g in range(SLOTS, HG):
                sp.wait_ge(scores_mm, UNIT0[g - SLOTS + 1])
                load_keys(0, g, ring_loaded)
            with sp.Fori(1, B) as b:
                for g in range(HG):
                    if g < SLOTS:
                        sp.wait_ge(scores_mm, (b - 1) * NU + UNIT0[g - SLOTS + 1 + HG])
                    else:
                        sp.wait_ge(scores_mm, b * NU + UNIT0[g - SLOTS + 1])
                    load_keys(b, g, ring_loaded)
            for dst, name in ((w_qkv1[:, 0:D], 'Wq'), (w_qkv1[:, D:2 * D], 'Wk'), (w_qkv1[:, 2 * D:3 * D], 'Wv'),
                              (w_out1, 'Wo'), (w1_1, 'W1')):
                sp.dma_start(dst, t['L1_attn_' + name]).then_inc(lin_loaded, 16)
            sp.dma_start(w2_1, t['L1_attn_W2'].rearrange("(k p) c -> p k c", p=P)).then_inc(lin_loaded, 16)
            for dst, name in ((b_qkv1[:, 0:D], 'bq'), (b_qkv1[:, D:2 * D], 'bk'), (b_qkv1[:, 2 * D:3 * D], 'bv'),
                              (b_out1, 'bo'), (b2_1, 'b2')):
                sp.dma_start(dst, t['L1_attn_' + name].rearrange("(a f) -> a f", a=1)).then_inc(lin_loaded, 16)
            for i, name in enumerate(('g1', 'be1', 'g2', 'be2')):
                sp.dma_start(affine[:, i, :], t['L1_attn_' + name].rearrange("(a f) -> a f", a=1).broadcast_to([P, D]))\
                  .then_inc(lin_loaded, 16)
            sp.dma_start(w_gate, t['L1_ffn_Wg']).then_inc(lin_loaded, 16)
            sp.wait_ge(pv_done, (ITEMS + 2) * QUADS)
            for i in range(2):
                half = gate_up[:, i, :].rearrange("p (e n) -> p e n", n=I1)
                cols = slice(I1 * i, I1 * (i + 1))
                sp.dma_start(half[:, 0:E1, :], t['L1_ffn_W_gate_up'][:, :, cols].rearrange("e c n -> c e n"))                  .then_inc(moe1_loaded, 16)
                sp.dma_start(half[:, E1:E1 + NS, :], t['L1_ffn_Ws_gate_up'][:, :, cols].rearrange("e c n -> c e n"))                  .then_inc(moe1_loaded, 16)
            sp.dma_start(down[:, 0:EC, :], t['L1_ffn_W_down'].rearrange("(m e) i c -> (e i) m c", m=EC)).then_inc(moe1_loaded, 16)
            sp.dma_start(down[0:NS * I1, EC, :], t['L1_ffn_Ws_down'].rearrange("e i c -> (e i) c")).then_inc(moe1_loaded, 16)
            sp.wait_ge(x_final, B)
            sp.dma_start(out.rearrange("b s f -> s b f"), x[:]).then_inc(stored, 16)
            sp.wait_ge(stored, 16)

        @block.gpsimd
        def _(pool):
            nc.gpsimd.memset(ident[:], 0.0).then_inc(ident_zero, 1)
            nc.gpsimd.memset(ident_h[:], 0.0).then_inc(ident_zero, 1)
            nc.gpsimd.memset(minus_half[:], -0.5).then_inc(half_ready, 1)
            pool.wait_ge(ident_zero, 2)
            for m in (ident, ident_h):
                nc.gpsimd.affine_select(out=m[:], in_=m[:], compare_op=ALU.not_equal, fill=1.0, base=0,
                                        pattern=[[-1, P]], channel_multiplier=1).then_inc(ident_ready, 1)
            pool.wait_ge(half_ready, 1)
            norm_gpsimd(pool, 0)
            for b in range(2):
                nc.gpsimd.memset(scores0[b], -99999.0).then_inc(s0_fill, 1)
            for n in range(GROUPS):
                pool.wait_ge(k_left1, n + 1)
                nc.gpsimd.tensor_copy(k_parts[:, 1, n * BANK:(n + 1) * BANK], k_left[:, n % 2, :])\
                  .then_inc(k_second, 1)
                pool.wait_ge(k_second, n + 1)
                nc.gpsimd.tensor_tensor(k_parts[:, 2, n * BANK:(n + 1) * BANK], k_left[:, n % 2, :],
                                        k_parts[:, 1, n * BANK:(n + 1) * BANK], ALU.subtract)\
                  .then_inc(k_third, 1)
                if n % GB == 0 and 2 <= n // GB + 1 < B:
                    b = n // GB + 1
                    pool.wait_ge(p0_trans, 4 * (b - 1))
                    nc.gpsimd.memset(scores0[b % 2], -99999.0).then_inc(s0_fill, 1)
            nc.gpsimd.memset(ones_row[:], 1.0).then_inc(consts, 1)
            nc.gpsimd.memset(logits0[:], -NEVER).then_inc(consts, 1)
            nc.gpsimd.memset(picks0[:], -NEVER).then_inc(consts, 1)
            norm_gpsimd(pool, 1)
            norm_gpsimd(pool, 2)
            pool.wait_ge(x_done, 2 * B)
            pool.wait_ge(ln_rstd, 3)
            nc.gpsimd.memset(key_ring[KROWS:ROWS, :, :], 1.0).then_inc(ring_ones, 1)
            pool.wait_ge(ring_ones, 1)
            nc.gpsimd.memset(v_stage, 0.0).then_inc(stage_set, 1)
            pool.wait_ge(stage_set, 1)
            for i in range(2):
                nc.gpsimd.memset(v_stage[:, :, :, VCOLS * i + 8:VCOLS * i + 9], 1.0).then_inc(stage_set, 1)
            norm_gpsimd(pool, 3)
            pool.wait_ge(x_moe, B * (E0 + 1))
            pool.wait_ge(ln_rstd, 4)
            pool.wait_ge(stage_set, 3)
            nc.gpsimd.memset(wide[KROWS:ROWS, 4096:8192], 0.0).then_inc(stage_set, 1)
            pool.wait_ge(stage_set, 4)
            with pool.Fori(0, B) as b:
                for g in range(HG):
                    pool.wait_ge(pv_done, b * (HG * QUADS) + (g + 1) * QUADS)
                    nc.gpsimd.tensor_copy(
                        v_stage[:, g % 2, :, 0:2 * VCOLS].rearrange("p c (i v) -> p c i v", i=2)[:, :, :, 0:8],
                        v1[:, bass.ds(b * KC, KC), 16 * g:16 * (g + 1)].rearrange("p c (i v) -> p c i v", i=2))\
                      .then_inc(staged, 1)
            norm_gpsimd(pool, 4)
            norm_gpsimd(pool, 5)
            norm_gpsimd(pool, 6)
            norm_gpsimd(pool, 7)

        @block.scalar
        def _(act):
            act.wait_ge(small_mm, 1)
            nc.scalar.copy(small_w[:, 0:4, :], ps[:, 0, :].rearrange("p (i f) -> p i f", f=D))\
              .then_inc(small_ready, 1)
            nc.scalar.copy(small_w[:, 4, :], ps[:, 1, 0:D]).then_inc(small_ready, 1)
            norm_scalar(act, 0)

            def context_group(n):
                act.wait_ge(ct_trans, n + 1)
                nc.scalar.copy(ctx_t[:, n * BANK:(n + 1) * BANK], ps[:, ct_bank(n), :]).then_inc(ct_ready, 1)

            def keys_values(n):
                act.wait_ge(k_mm, n + 1)
                nc.scalar.copy(k_parts[:, 0, n * BANK:(n + 1) * BANK], ps[:, 1 + n % 2, :]).then_inc(k_first, 1)
                act.wait_ge(v_mm, n + 1)
                nc.scalar.copy(v1[:, 4 * n:4 * n + 4, :], ps[:, 3, :].rearrange("p (c f) -> p c f", f=D))\
                  .then_inc(v_ready, 1)

            def exps(b, i):
                half = scores0[b % 2][:, KEYS // 2 * i:KEYS // 2 * (i + 1)]
                act.wait_ge(s0_max, 3 * b + 3)
                nc.scalar.activation(half, half, ACT.Exp, bias=nmax0[:, b:b + 1],
                                     accum_out=sum0[:, b, i:i + 1]).then_inc(s0_exp, 1)

            def probs_out(b):
                if b >= 1:
                    act.wait_ge(o1_mm, b)
                for j in range(4):
                    act.wait_ge(p0_trans, 4 * b + j + 1)
                    nc.scalar.copy(probs0_t[:, 4 * j:4 * j + 4, :], ps[:, 4 + j, :].rearrange("p (c s) -> p c s", s=S))\
                      .then_inc(p0_ready, 1)

            def context_out(b):
                act.wait_ge(o1_mm, b + 1)
                nc.scalar.copy(o1_t, ps[:, 3, 0:S]).then_inc(o1_ready, 1)

            for j in range(GB):
                context_group(j)
            for b in range(B):
                for j in range(GB):
                    if b + 1 < B:
                        context_group(GB * (b + 1) + j)
                    if j >= 2:
                        exps(b, j - 2)
                    keys_values(GB * b + j)
                probs_out(b)
                context_out(b)
            act.wait_ge(cols_mm, 1)
            nc.scalar.copy(b1_cols[:], ps[:, 1, 0:BR0 + BR1]).then_inc(cols_ready, 1)
            norm_scalar(act, 1)
            for i in range(PAIRS):
                act.wait_ge(q0_mm, i + 1)
                nc.scalar.copy(q0_t[:, i, :], ps[:, i % 2, :]).then_inc(q0_ready, 1)
            def probs1_out(b):
                for j in range(4):
                    act.wait_ge(p1_trans, 4 * b + j + 1)
                    nc.scalar.copy(probs1_t[b % 2][:, j * BANK:(j + 1) * BANK], ps[:, 4 + j % 2, :])\
                      .then_inc(p1_ready, 1)

            for b in range(B):
                if b >= 1:
                    probs1_out(b - 1)
                act.wait_ge(s1_max, 2 * b + 2)
                if b >= 2:
                    act.wait_ge(p1_trans, 4 * (b - 1))
                for h in range(HEADS):
                    ex = nc.scalar.activation(probs1[b % 2][:, h, :], ps[:, h // 4, (h % 4) * S:(h % 4 + 1) * S],
                                              ACT.Exp, bias=nmax1[:, b, h:h + 1], scale=SCALE0,
                                              accum_out=sum1[:, b, h:h + 1])
                ex.then_inc(s1_exp, 1)
            probs1_out(B - 1)

            act.wait_ge(s1_mm, B)
            nc.scalar.activation(k_square, k_parts[:, 0, :], ACT.Square).then_inc(ksq_ready, 1)

            norm_scalar(act, 2)

            def relu(i):
                act.wait_ge(h0_mm, i + 1)
                nc.scalar.activation(h0_t[:, i, :], ps[:, 1 + i % 3, :], ACT.Relu, bias=b1_cols[:, i:i + 1])\
                  .then_inc(h0_relu, 1)

            for i in range(3):
                relu(i)
            act.wait_ge(gate_step, 1)
            for b in range(B):
                ex = nc.scalar.activation(gate_e[:, b, :], logits0[:, b, 0:E0], ACT.Exp, bias=ntop0[:, b:b + 1],
                                          accum_out=gate_sum[:, b:b + 1])
            ex.then_inc(gate_exp, 1)
            act.wait_ge(lam_step, 2)
            nc.scalar.activation(lam_exp, lam_sum, ACT.Exp).then_inc(lam_expd, 1)
            for i in range(3, 6):
                relu(i)
            act.wait_ge(g0_trans, 1)
            nc.scalar.copy(gates0_t, ps[0:E0, 7, :]).then_inc(g0_ready, 1)
            for i in range(6, E0 * HC0):
                relu(i)
            norm_scalar(act, 3)
            act.wait_ge(q1_mm, 1)
            nc.scalar.copy(q_parts[:, 0, :], ps[:, 0, :]).then_inc(q1_part, 1)
            nc.scalar.activation(aux_t[:], ps[:, 0, :], ACT.Square).then_inc(q1_square, 1)
            with act.Fori(0, B) as b:
                for g in range(HG):
                    for k, (c, n) in enumerate(UNITS[g]):
                        u = UNIT0[g] + k
                        act.wait_ge(scores_mm, b * NU + (u + 1))
                        if c % 4 == 0:
                            act.wait_ge(pv_done, b * (HG * QUADS) + (QUADS * (g + 1) + c // 4 + 1))
                        bank = UNIT * (u % NBUF)
                        half = probs_d[c // 8]
                        nc.scalar.activation(half[:, (c % 8) * BANK:(c % 8 + n) * BANK],
                                             ps[:, bank:bank + n, :].rearrange("p k c -> p (k c)"),
                                             ACT.Exp, scale=SCALE1).then_inc(exp_done, 1)
            norm_scalar(act, 4)
            act.wait_ge(wg_trans, 1)
            nc.scalar.copy(wg_t, ps[:, 7, 0:E1]).then_inc(wg_ready, 1)
            act.wait_ge(lin_step, 1)
            nc.scalar.activation(qk_low, qk_low, ACT.Exp).then_inc(lin_exp, 1)
            act.wait_ge(lin_step, 3)
            nc.scalar.copy(v1s, ps[:, 0:4, 2 * D:3 * D]).then_inc(lin_v, 1)
            nc.scalar.activation(qk_sq, qk1, ACT.Square).then_inc(lin_sq, 1)
            act.wait_ge(lin_step, 5)
            nc.scalar.activation(qk_root, qk_norm, ACT.Sqrt).then_inc(lin_root, 1)
            act.wait_ge(qn_trans, 1)
            nc.scalar.copy(qn_t, ps[:, 5, :]).then_inc(qn_ready, 1)
            act.wait_ge(lc_mm, 1)
            nc.scalar.copy(lin_t, ps[:, 6, :]).then_inc(lc_ready, 1)
            act.wait_ge(a1_trans, 1)
            nc.scalar.copy(attn1_t, ps[:, 5, :]).then_inc(a1_ready, 1)
            for k in range(FC):
                act.wait_ge(f1_mm, k + 1)
                nc.scalar.activation(h1_t[:, k, :], ps[:, k, :], ACT.Gelu, bias=b1_cols[:, BR0 + k:BR0 + k + 1])\
                  .then_inc(f1_ready, 1)

            norm_scalar(act, 5)
            act.wait_ge(g1_step, 2)
            for b in range(B):
                ex = nc.scalar.activation(gate1[:, b, :], logits1[:, b, :], ACT.Exp, bias=ntop1[:, b:b + 1])
            ex.then_inc(g1_exp, 1)
            act.wait_ge(g1_trans, 1)
            nc.scalar.copy(gate1_t, ps[0:E1, 1, :]).then_inc(g1_ready, 1)
            for m in range(EC + 1):
                rows = P if m < EC else NS * I1
                act.wait_ge(gu_mm, m + 1)
                if m >= 2:
                    act.wait_ge(hid_step, m - 1)
                nc.scalar.activation(silu[m % 2][0:rows, :], ps[0:rows, 2 + 3 * (m % 2), :], ACT.Silu)\
                  .then_inc(silu_ready, 1)

        @block.vector
        def _(dve):
            dve.wait_ge(x_loaded, 16)
            norm_vector(dve, 0, 1e-5)
            dve.wait_ge(qk_mm, 1)
            nc.vector.tensor_copy(aux_t[:], ps[:, 4, :]).then_inc(qk_ready, 1)

            def keys_left(n):
                dve.wait_ge(k_first, n + 1)
                if n >= 2:
                    dve.wait_ge(k_third, n - 1)
                nc.vector.tensor_tensor(k_left[:, n % 2, :], ps[:, 1 + n % 2, :],
                                        k_parts[:, 0, n * BANK:(n + 1) * BANK], ALU.subtract)\
                  .then_inc(k_left1, 1)

            def mask_half(b, i):
                half = slice(KEYS // 2 * i, KEYS // 2 * (i + 1))
                dve.wait_ge(s0_mm, 2 * b + i + 1)
                dve.wait_ge(s0_fill, b + 1)
                dve.wait_ge(mask_loaded, 16 * (b + 1))
                nc.vector.copy_predicated(scores0[b % 2][:, half], mask_sb[:, half],
                                          ps[:, 4 + 2 * i:6 + 2 * i, :].rearrange("p k c -> p (k c)")).then_inc(s0_masked, 1)

            def max_half(b, i):
                dve.wait_ge(s0_masked, 2 * b + i + 1)
                nc.vector.tensor_reduce(max0[:, b, i:i + 1], scores0[b % 2][:, KEYS // 2 * i:KEYS // 2 * (i + 1)],
                                        AX.X, ALU.max).then_inc(s0_max, 1)

            def max_row(b):
                dve.wait_ge(s0_max, 3 * b + 2)
                nc.vector.tensor_reduce(nmax0[:, b:b + 1], max0[:, b, :], AX.X, ALU.max, negate=True).then_inc(s0_max, 1)

            def add_context(b):
                dve.wait_ge(s0_exp, 2 * b + 2)
                nc.vector.tensor_reduce(rsum0[:, b:b + 1], sum0[:, b, :], AX.X, ALU.add).then_inc(s0_rsum, 1)
                dve.wait_ge(s0_rsum, 2 * b + 1)
                nc.vector.reciprocal(rsum0[:, b:b + 1], rsum0[:, b:b + 1]).then_inc(s0_rsum, 1)
                dve.wait_ge(s0_rsum, 2 * b + 2)
                dve.wait_ge(y0_mm, b + 1)
                nc.vector.scalar_tensor_tensor(x[:, b, :], ps[:, 2, 0:D], rsum0[:, b:b + 1], x[:, b, :],
                                               ALU.mult, ALU.add).then_inc(x_done, 1)

            for b in range(B + 1):
                for j in range(GB if b else 0):
                    if j == 0:
                        if b >= 2:
                            add_context(b - 2)
                        mask_half(b - 1, 0)
                        keys_left(GB * (b - 1) + j)
                        mask_half(b - 1, 1)
                    elif j == 1:
                        max_half(b - 1, 0)
                        keys_left(GB * (b - 1) + j)
                        max_half(b - 1, 1)
                        max_row(b - 1)
                    else:
                        keys_left(GB * (b - 1) + j)
            add_context(B - 1)
            dve.wait_ge(x_done, B)
            nc.vector.tensor_reduce(of_half, ident[:].rearrange("p (h c) -> p h c", c=4), AX.X, ALU.add)
            nc.vector.tensor_reduce(of_half_h, ident[:].rearrange("p (h c) -> p h c", c=4), AX.X, ALU.max)
            nc.vector.tensor_reduce(of_j, ident[:].rearrange("p (a j c) -> p j a c", j=4, c=4), AX.XY, ALU.add)
            nc.vector.tensor_reduce(of_j12, ident[:, 0:12].rearrange("p (a j) -> p j a", j=4), AX.X, ALU.add)\
              .then_inc(consts_d, 1)
            dve.wait_ge(rows_loaded, ROW_LOADS)
            nc.vector.tensor_tensor(lam_prod, lam_load[:, 0:4:2, :], lam_load[:, 1:4:2, :], ALU.mult).then_inc(lam_step, 1)
            dve.wait_ge(lam_step, 1)
            nc.vector.tensor_reduce(lam_sum, lam_prod, AX.X, ALU.add).then_inc(lam_step, 1)

            norm_vector(dve, 1, 1e-5)
            for i in range(PAIRS):
                dve.wait_ge(k0_mm, i + 1)
                nc.vector.tensor_copy(k0_t[:, i, :], ps[:, 2 + i % 2, :]).then_inc(k0_ready, 1)

            def max_heads(b):
                dve.wait_ge(s1_mm, b + 1)
                nc.vector.tensor_reduce(max1[:, b, :], ps[:, 0:4, :].rearrange("p k (h c) -> p (k h) c", c=S),
                                        AX.X, ALU.max).then_inc(s1_max, 1)
                dve.wait_ge(s1_max, 2 * b + 1)
                nc.vector.tensor_scalar_mul(nmax1[:, b, :], max1[:, b, :], -SCALE0).then_inc(s1_max, 1)

            def normalise(b):
                dve.wait_ge(s1_exp, b + 1)
                nc.vector.reciprocal(rsum1[:, b, :], sum1[:, b, :]).then_inc(s1_norm, 1)
                dve.wait_ge(s1_norm, 2 * b + 1)
                nc.vector.tensor_tensor(probs1[b % 2], probs1[b % 2],
                                        rsum1[:, b, :].unsqueeze(2).to_broadcast([P, HEADS, S]), ALU.mult)\
                  .then_inc(s1_norm, 1)

            def heads_out(b):
                dve.wait_ge(h1_mm, b + 1)
                nc.vector.tensor_copy(heads_t[:, :, b * S:(b + 1) * S],
                                      ps[:, 6:8, :].rearrange("p k (i c) -> p (k i) c", c=S)).then_inc(h1_ready, 1)

            max_heads(0)
            for b in range(B):
                for i in range(2):
                    dve.wait_ge(v0_mm, 2 * b + i + 1)
                    nc.vector.tensor_copy(v0[:, b, BANK * i:BANK * (i + 1)], ps[:, 4 + i, :]).then_inc(v0_ready, 1)
            def add_heads(b):
                dve.wait_ge(y1_mm, b + 1)
                nc.vector.tensor_tensor(x[:, b, :], x[:, b, :], ps[:, 4, 0:D], ALU.add).then_inc(x_done, 1)

            for b in range(B):
                if b >= 1:
                    add_heads(b - 1)
                normalise(b)
                if b + 1 < B:
                    max_heads(b + 1)
                heads_out(b)
            add_heads(B - 1)

            dve.wait_ge(x_done, 2 * B)
            norm_vector(dve, 2, 1e-5)
            dve.wait_ge(consts, 3)
            dve.wait_ge(lg0_mm, 1)
            nc.vector.tensor_tensor(logits0[:, :, 0:E0], ps[:, 0, 0:B * E0].rearrange("p (b e) -> p b e", b=B),
                                    gate_b[:].unsqueeze(1).to_broadcast([P, B, E0]), ALU.add)\
              .then_inc(picks0_step, 1)

            dve.wait_ge(picks0_step, 1)
            for b in range(B):
                mx = nc.vector.max(top0[:, b, :], logits0[:, b, 0:E0])
            mx.then_inc(picks0_step, 1)
            dve.wait_ge(picks0_step, 2)
            nc.vector.tensor_scalar_mul(ntop0[:], top0[:, :, 0], -1.0).then_inc(gate_step, 1)
            nc.vector.tensor_copy(picks0[:, :, 0:2], top0[:, :, 0:2]).then_inc(picks0_step, 1)
            dve.wait_ge(picks0_step, 3)
            for b in range(B):
                mr = nc.vector.match_replace(struck0[:, b, :], picks0[:, b, :], logits0[:, b, :], NEVER)
            mr.then_inc(picks0_step, 1)
            dve.wait_ge(picks0_step, 4)
            nc.vector.tensor_tensor(gates0[:], struck0[:, :, 0:E0], logits0[:, :, 0:E0], ALU.not_equal)\
              .then_inc(gate_step, 1)
            dve.wait_ge(gate_exp, 1)
            nc.vector.reciprocal(gate_r[:], gate_sum[:]).then_inc(gate_step, 1)
            dve.wait_ge(gate_step, 3)
            nc.vector.tensor_tensor(gate_e[:], gate_e[:], gates0[:], ALU.mult).then_inc(gate_step, 1)
            dve.wait_ge(gate_step, 4)
            nc.vector.tensor_tensor(gates0[:], gate_e[:], gate_r[:].unsqueeze(2).to_broadcast([P, B, E0]), ALU.mult)\
              .then_inc(gate_step, 1)
            dve.wait_ge(gate_step, 5)
            dve.wait_ge(b2_mm, 1)
            for b in range(B):
                nc.vector.tensor_tensor(x[:, b, :], x[:, b, :], ps[:, 7, b * D:(b + 1) * D], ALU.add).then_inc(x_moe, 1)
            def largest_norm(n):
                dve.wait_ge(kn_mm, n + 1)
                nc.vector.tensor_reduce(k_norms[:, n:n + 1], ps[0:HH, 6 * (n % 2), :], AX.X, ALU.max).then_inc(kn_max, 1)

            for e in range(E0):
                for n in range(3 * e, min(3 * e + 2, GROUPS)):
                    largest_norm(n)
                dve.wait_ge(e0_mm, e + 1)
                for b in range(B):
                    dve.wait_ge(x_moe, B * e + b + 1)
                    nc.vector.scalar_tensor_tensor(x[:, b, :], ps[:, 4 + e % 2, b * D:(b + 1) * D],
                                                   gates0[:, b, e:e + 1], x[:, b, :], ALU.mult, ALU.add)\
                      .then_inc(x_moe, 1)
                if 3 * e + 2 < GROUPS:
                    largest_norm(3 * e + 2)
                if e == E0 - 2:
                    dve.wait_ge(kn_max, GROUPS)
                    nc.vector.reduce_max(k_norm, k_norms, AX.X).then_inc(kn_all, 1)
                    dve.wait_ge(lam_expd, 1)
                    nc.vector.scalar_tensor_tensor(neg_lam, lam_exp[:, 0:1], -1.0, lam_exp[:, 1:2], ALU.mult, ALU.add)\
                      .then_inc(lam_step, 1)
                    dve.wait_ge(lam_step, 3)
                    nc.vector.tensor_scalar_add(neg_lam, neg_lam, -0.8).then_inc(lam_step, 1)
            dve.wait_ge(x_moe, B * (E0 + 1))
            norm_vector(dve, 3, 1e-5)
            nc.vector.memset(wide[KROWS:ROWS, 8192:12288], 0.0).then_inc(q_rows_zero, 1)
            def mask_queries(i):
                for j in range(4):
                    nc.vector.tensor_scalar(q_masked[:, i, :, j, :], q_parts[:, i, :].rearrange("p (b c) -> p b c", b=B),
                                            of_j[:, j:j + 1], None, ALU.mult).then_inc(q_masked_ready, 1)

            dve.wait_ge(q1_part, 1)
            mask_queries(0)
            dve.wait_ge(q1_square, 1)
            dve.wait_ge(ln_trans, 4)
            left = xn[:].rearrange("p b f -> p (b f)")
            nc.vector.tensor_tensor(left, ps[:, 0, :], q_parts[:, 0, :], ALU.subtract).then_inc(q1_left, 1)
            dve.wait_ge(q1_left, 1)
            nc.vector.tensor_copy(q_parts[:, 1, :], left).then_inc(q1_left, 1)
            dve.wait_ge(q1_left, 2)
            mask_queries(1)
            nc.vector.tensor_tensor(q_parts[:, 2, :], left, q_parts[:, 1, :], ALU.subtract).then_inc(q1_left, 1)
            dve.wait_ge(q1_left, 3)
            mask_queries(2)
            dve.wait_ge(qn_mm, 1)
            nc.vector.reduce_max(q_norm, ps[0:HH, 1, :], AX.X).then_inc(bound_step, 1)
            dve.wait_ge(kn_all, 1)
            dve.wait_ge(bound_step, 1)
            nc.vector.tensor_tensor(bound_h, q_norm, k_norm, ALU.mult).then_inc(bound_step, 1)
            dve.wait_ge(bound_trans, 1)
            nc.vector.reduce_max(bound, ps[0:1, 2, 0:HH], AX.X).then_inc(bound_step, 1)
            dve.wait_ge(bound_step, 3)
            nc.vector.tensor_scalar(safe, bound, (LIMIT / SCALE1) ** 2 / 1.02, None, ALU.is_le).then_inc(safe_ready, 1)

            dve.wait_ge(safe_ready, 1)
            is_safe = dve.value_load(safe)
            with dve.If(is_safe < 1):
                with dve.Fori(0, B) as b:
                    for h in range(HH):
                        dve.wait_ge(shift_mm, b * HH + (h + 1 + 4 * SLOTS))
                        nc.vector.tensor_reduce(shift_max[:, bass.ds(b * HH + h, 1)],
                                                ps[:, 4 * (h % 2):4 * (h % 2) + 4, :].rearrange("p k c -> p (k c)"),
                                                AX.X, ALU.max, negate=True).then_inc(shift_maxed, 1)
                dve.wait_ge(shift_maxed, B * HH + 2)
                m_v = shift_max.rearrange("p (i j) -> p i j", j=4)
                l_v = shift_left.rearrange("p (i j) -> p i j", j=4)
                nc.vector.tensor_copy(shift_parts[:, :, 0, :], m_v).then_inc(shift_step, 1)
                dve.wait_ge(shift_step, 1)
                nc.vector.tensor_tensor(l_v, m_v, shift_parts[:, :, 0, :], ALU.subtract).then_inc(shift_step, 1)
                dve.wait_ge(shift_step, 2)
                nc.vector.tensor_copy(shift_parts[:, :, 1, :], l_v).then_inc(shift_step, 1)
                dve.wait_ge(shift_step, 3)
                nc.vector.tensor_tensor(shift_parts[:, :, 2, :], l_v, shift_parts[:, :, 1, :], ALU.subtract)\
                  .then_inc(shift_step, 1)
                dve.wait_ge(stage_set, 4)
                for n in range(ITEMS):
                    dve.wait_ge(shift_trans, n + 1)
                    nc.vector.tensor_tensor(
                        q_rows[KROWS:ROWS, n * BANK:(n + 1) * BANK].rearrange("p (j c) -> p j c", j=4),
                        ps[0:12, n % 2, 0:S].unsqueeze(1).to_broadcast([12, 4, S]),
                        of_j12[0:12, :].unsqueeze(2).to_broadcast([12, 4, S]), ALU.mult).then_inc(shift_rows, 1)

            with dve.Fori(0, B) as b:
                for g in range(HG):
                    dve.wait_ge(pv_done, b * (HG * QUADS) + QUADS * (g + 3))
                    acc = acc_sb[32 * (g % GI):32 * (g % GI + 1), g // GI, :]
                    for n in range(4):
                        tile_n = ps[32 * n:32 * (n + 1), 6 + g % 2, :]
                        if n == 0:
                            nc.vector.tensor_copy(acc, tile_n).then_inc(acc_added, 1)
                        else:
                            dve.wait_ge(acc_added, b * (HG * 4) + (4 * (g + 2) + n))
                            nc.vector.tensor_tensor(acc, acc, tile_n, ALU.add).then_inc(acc_added, 1)
                    if g % GI == GI - 1:
                        dve.wait_ge(fold_mm, b * (HG // GI) + (g // GI + 1))
                        nc.vector.tensor_copy(heads_d[:, bass.ds(b * HH + 4 * GI * (g // GI), 4 * GI), :],
                                              ps[:, 7, 0:4 * GI * VCOLS].rearrange("p (h v) -> p h v", v=VCOLS))\
                          .then_inc(folded, 1)
                dve.wait_ge(folded, b * (HG // GI) + (HG // GI + 1))
                heads_b = heads_d[:, bass.ds(b * HH, HH), :]
                den_b = den_r[:, bass.ds(b * HH, HH)]
                nc.vector.reciprocal(den_b, heads_b[:, :, 8]).then_inc(comb_step, 1)
                dve.wait_ge(comb_step, b * 3 + 1)
                nc.vector.tensor_tensor(heads_b[:, :, 0:8], heads_b[:, :, 0:8],
                                        den_b.unsqueeze(2).to_broadcast([P, HH, 8]), ALU.mult).then_inc(comb_step, 1)
                dve.wait_ge(comb_step, b * 3 + 2)
                x_b = x[:, bass.ds(b, 1), :].rearrange("p a (h v) -> p (a h) v", v=8)
                by_half = heads_b[:, :, 0:8].rearrange("p (h i) v -> p h i v", i=2)
                nc.vector.scalar_tensor_tensor(x_b, by_half[:, :, 1, :], neg_lam, x_b, ALU.mult, ALU.add)\
                  .then_inc(comb_step, 1)
                dve.wait_ge(comb_step, b * 3 + 3)
                nc.vector.tensor_tensor(x_b, by_half[:, :, 0, :], x_b, ALU.add).then_inc(x_diff, 1)

            dve.wait_ge(x_diff, B)
            norm_vector(dve, 4, 1e-5)
            nc.vector.tensor_reduce(of_eight, ident[:].rearrange("p (h c) -> p h c", c=DH1), AX.X, ALU.add)\
              .then_inc(kv_ready, 1)
            dve.wait_ge(kv_ready, 1)
            nc.vector.tensor_scalar_mul(of_eight, of_eight, DH1 ** -0.5).then_inc(kv_ready, 1)
            dve.wait_ge(lin_mm, 1)
            q_k = ps[:, 0:4, 0:2 * D]
            nc.vector.tensor_scalar(qk_low, q_k, 0.0, None, ALU.min).then_inc(lin_step, 1)
            dve.wait_ge(lin_exp, 1)
            nc.vector.tensor_scalar_add(qk_low, qk_low, -1.0).then_inc(lin_step, 1)
            dve.wait_ge(lin_step, 2)
            nc.vector.scalar_tensor_tensor(qk1, q_k, 0.0, qk_low, ALU.max, ALU.add).then_inc(lin_step, 1)
            dve.wait_ge(lin_sq, 1)
            by_head = "p b (h c) -> p (b h) c"
            nc.vector.tensor_reduce(qk_norm, qk_sq.rearrange(by_head, c=DH1), AX.X, ALU.add).then_inc(lin_step, 2)
            dve.wait_ge(lin_root, 1)
            nc.vector.reciprocal(qk_rs, qk_root).then_inc(lin_root, 1)
            dve.wait_ge(lin_root, 2)
            nc.vector.scalar_tensor_tensor(qk_root, qk_rs, -0.5, qk_rs, ALU.mult, ALU.mult).then_inc(lin_root, 1)
            dve.wait_ge(lin_root, 3)
            nc.vector.tensor_tensor(qk_root, qk_root, qk_norm, ALU.mult).then_inc(lin_root, 1)
            dve.wait_ge(lin_root, 4)
            nc.vector.scalar_tensor_tensor(qk_rs, qk_root, 1.5, qk_rs, ALU.add, ALU.mult).then_inc(lin_root, 1)
            dve.wait_ge(lin_root, 5)
            nc.vector.tensor_tensor(qk1.rearrange(by_head, c=DH1), qk1.rearrange(by_head, c=DH1),
                                    qk_rs.unsqueeze(2).to_broadcast([P, 2 * B * HEADS1, DH1]), ALU.mult).then_inc(lin_step, 1)
            dve.wait_ge(kv_mm, 1)
            dve.wait_ge(kv_ready, 2)
            nc.vector.tensor_tensor(kv_diag.rearrange("p b (h c) -> p b h c", c=DH1),
                                    ps[:, 4, :].rearrange("p (b h c) -> p b h c", b=B, c=DH1),
                                    of_eight.unsqueeze(1).unsqueeze(3).to_broadcast([P, B, HEADS1, DH1]), ALU.mult)\
              .then_inc(kv_ready, 1)
            dve.wait_ge(lo_mm, 1)
            nc.vector.tensor_tensor(res1, xn[:], ps[:, 7, :].rearrange("p (b n) -> p b n", b=B), ALU.add).then_inc(lin_step, 1)
            dve.wait_ge(lin_step, 7)
            norm_vector(dve, 5, 1e-12, res1, attn1)

            def affine_vector(n, i):
                dve.wait_ge(ln_xn, B * (n + 1))
                nc.vector.tensor_tensor(attn1 if i == 0 else res1, attn1 if i == 0 else res1,
                                        affine[:, i, :].unsqueeze(1).to_broadcast([P, B, D]), ALU.mult).then_inc(lin_step, 1)
                dve.wait_ge(lin_step, 8 + i)
                nc.vector.tensor_tensor(attn1 if i == 0 else res1, attn1 if i == 0 else res1,
                                        affine[:, i + 1, :].unsqueeze(1).to_broadcast([P, B, D]), ALU.add).then_inc(lin_step, 1)

            affine_vector(5, 0)
            dve.wait_ge(lin_step, 9)
            dve.wait_ge(f2_mm, 1)
            nc.vector.tensor_tensor(qk_res, attn1, ps[:, 4, :].rearrange("p (b n) -> p b n", b=B), ALU.add).then_inc(f2_res, 1)
            dve.wait_ge(f2_res, 1)
            norm_vector(dve, 6, 1e-12, qk_res, res1)
            affine_vector(6, 2)
            dve.wait_ge(lin_step, 11)
            nc.vector.tensor_tensor(x[:], x[:], res1, ALU.add).then_inc(x_lin, 1)

            dve.wait_ge(x_lin, 1)
            norm_vector(dve, 7, 1e-5)
            nc.vector.tensor_copy(spread.rearrange("p (e i) -> p e i", i=I1),
                                  ident[0:E1, 0:E1].unsqueeze(2).to_broadcast([E1, E1, I1])).then_inc(spread_ready, 1)
            dve.wait_ge(lg1_mm, 1)
            nc.vector.tensor_copy(logits1, ps[:, 0, 0:B * E1].rearrange("p (b e) -> p b e", b=B)).then_inc(g1_step, 1)
            dve.wait_ge(g1_step, 1)
            for b in range(B):
                mx = nc.vector.max(top1[:, b, :], logits1[:, b, :])
            mx.then_inc(top1_ready, 1)
            dve.wait_ge(top1_ready, 1)
            nc.vector.tensor_scalar_mul(ntop1, top1[:, :, 0], -1.0).then_inc(g1_step, 1)
            for b in range(B):
                mr = nc.vector.match_replace(struck1[:, b, :], top1[:, b, :], logits1[:, b, :], NEVER)
            mr.then_inc(g1_step, 1)
            dve.wait_ge(g1_step, 3)
            nc.vector.tensor_tensor(struck1, struck1, logits1, ALU.not_equal).then_inc(g1_step, 1)
            dve.wait_ge(g1_step, 4)
            dve.wait_ge(g1_exp, 1)
            nc.vector.tensor_tensor(gate1, gate1, struck1, ALU.mult).then_inc(g1_step, 1)
            dve.wait_ge(g1_step, 5)
            nc.vector.tensor_reduce(gsum1, gate1, AX.X, ALU.add).then_inc(g1_step, 1)
            dve.wait_ge(g1_step, 6)
            nc.vector.reciprocal(grec1, gsum1).then_inc(g1_step, 1)
            dve.wait_ge(g1_step, 7)
            nc.vector.tensor_tensor(gate1, gate1, grec1.unsqueeze(2).to_broadcast([P, B, E1]), ALU.mult).then_inc(g1_step, 1)
            for m in range(EC + 1):
                rows = P if m < EC else NS * I1
                dve.wait_ge(silu_ready, m + 1)
                dst = hid1_t[0:rows, m * T:(m + 1) * T]
                if m < EC:
                    nc.vector.tensor_tensor(silu[m % 2], silu[m % 2], ps[:, 3 + 3 * (m % 2), :], ALU.mult).then_inc(hid_half, 1)
                    dve.wait_ge(hid_half, m + 1)
                    nc.vector.tensor_tensor(dst, silu[m % 2], ps[:, 4 + 3 * (m % 2), :], ALU.mult).then_inc(hid_step, 1)
                else:
                    nc.vector.scalar_tensor_tensor(dst, silu[m % 2][0:rows, :], 1.0 / NS, ps[0:rows, 3 + 3 * (m % 2), :],
                                                   ALU.mult, ALU.mult).then_inc(hid_step, 1)
            for b in range(B):
                dve.wait_ge(down_mm, b + 1)
                nc.vector.tensor_tensor(x[:, b, :], x[:, b, :], ps[:, b, 0:D], ALU.add).then_inc(x_final, 1)

        @block.tensor
        def _(pe):
            pe.wait_ge(ident_ready, 2)
            pe.wait_ge(raw_loaded, 96)
            nc.tensor.matmul(ps[:, 0, 0:D], raw_w[:, 0, :], raw_w[:, 1, :], start=True, stop=True)
            for i in range(3):
                nc.tensor.transpose(ps[:, 0, (i + 1) * D:(i + 2) * D], raw_w[:, 2 + i, :] if i == 0 else
                                    raw_w[:, 2 + i, :], ident[:])
            nc.tensor.transpose(ps[:, 1, 0:D], raw_w[:, 5, :], ident[:]).then_inc(small_mm, 1)
            norm_tensor(pe, 0)
            pe.wait_ge(small_ready, 2)
            pe.wait_ge(ln_done, 1)
            nc.tensor.matmul(ps[:, 4, :], wqk0, xn_t[:], start=True, stop=True).then_inc(qk_mm, 1)

            def transpose_group(n):
                if n % GB == 0:
                    pe.wait_ge(ctx_loaded[n // GB], 16)
                if n >= GB:
                    pe.wait_ge(ct_ready, n)
                elif n >= 2:
                    pe.wait_ge(ct_ready, n - 1)
                for c in range(4):
                    tr = nc.tensor.transpose(ps[:, ct_bank(n), c * P:(c + 1) * P], ctx_sb[:, 4 * n + c, :], ident[:])
                tr.then_inc(ct_trans, 1)

            def project_group(n):
                pe.wait_ge(ct_ready, n + 1)
                if n >= 2:
                    pe.wait_ge(k_left1, n - 1)
                if n >= GB and n % GB == 0:
                    pe.wait_ge(x_done, n // GB)
                nc.tensor.matmul(ps[:, 1 + n % 2, :], wk1_t, ctx_t[:, n * BANK:(n + 1) * BANK], start=True, stop=True)\
                  .then_inc(k_mm, 1)
                if n >= 1:
                    pe.wait_ge(v_ready, n)
                for c in range(4):
                    mm = nc.tensor.matmul(ps[:, 3, c * P:(c + 1) * P], ctx_t[:, (4 * n + c) * P:(4 * n + c + 1) * P],
                                          wv1_t, start=True, stop=True)
                mm.then_inc(v_mm, 1)

            def scores(b):
                pe.wait_ge(ct_ready, GB * (b + 1))
                for j in range(GB):
                    if b >= 1:
                        pe.wait_ge(p0_ready, 4 * (b - 1) + j + 1)
                    key0 = (GB * b + j) * BANK
                    mm = nc.tensor.matmul(ps[:, 4 + j, :], aux_t[:, b * S:(b + 1) * S], ctx_t[:, key0:key0 + BANK],
                                          start=True, stop=True)
                    if j % 2 == 1:
                        mm.then_inc(s0_mm, 1)

            def transpose_probs(b):
                for j in range(4):
                    pe.wait_ge(s0_exp, 2 * b + 1 + j // 2)
                    for c in range(4 * j, 4 * j + 4):
                        tr = nc.tensor.transpose(ps[:, 4 + j, (c % 4) * S:(c % 4 + 1) * S],
                                                 scores0[b % 2][:, c * P:(c + 1) * P], ident[:])
                    tr.then_inc(p0_trans, 1)

            def attend(b):
                pe.wait_ge(p0_ready, 4 * (b + 1))
                pe.wait_ge(v_ready, GB * (b + 1))
                for c in range(KC):
                    mm = nc.tensor.matmul(ps[:, 3, 0:S], ctx_sb[:, b * KC + c, :], probs0_t[:, c, :],
                                          start=(c == 0), stop=(c == KC - 1))
                mm.then_inc(o1_mm, 1)
                pe.wait_ge(o1_ready, b + 1)
                pe.wait_ge(k_left1, GB * (b + 1))
                nc.tensor.matmul(ps[:, 2, 0:D], o1_t, wv0_t, start=True, stop=True).then_inc(y0_mm, 1)

            pe.wait_ge(qk_ready, 1)
            for b in range(B + 1):
                for j in range(GB):
                    if b < B:
                        transpose_group(GB * b + j)
                    if b >= 1:
                        project_group(GB * (b - 1) + j)
                if b >= 1:
                    transpose_probs(b - 1)
                if b < B:
                    scores(b)
                if b >= 1:
                    attend(b - 1)
            pe.wait_ge(rows_loaded, ROW_LOADS)
            nc.tensor.transpose(ps[:, 1, 0:BR0 + BR1], b1_rows[:], ident[0:BR0 + BR1, 0:BR0 + BR1]).then_inc(cols_mm, 1)
            norm_tensor(pe, 1)
            pe.wait_ge(qkv0_loaded, 16)
            pe.wait_ge(cols_ready, 1)
            pe.wait_ge(ln_done, 2)
            for i in range(PAIRS):
                if i >= 2:
                    pe.wait_ge(q0_ready, i - 1)
                nc.tensor.matmul(ps[:, i % 2, :], w_qkv[:, 0, 2 * DH * i:2 * DH * (i + 1)], xn_t[:],
                                 start=True, stop=True).then_inc(q0_mm, 1)
                if i >= 2:
                    pe.wait_ge(k0_ready, i - 1)
                nc.tensor.matmul(ps[:, 2 + i % 2, :], w_qkv[:, 1, 2 * DH * i:2 * DH * (i + 1)], xn_t[:],
                                 start=True, stop=True).then_inc(k0_mm, 1)

            def scores_heads(b):
                for i in range(PAIRS):
                    for odd in range(2):
                        rows = slice(DH * odd, DH * (odd + 1))
                        mm = nc.tensor.matmul(ps[:, 2 * odd + i // 4, (i % 4) * S:(i % 4 + 1) * S],
                                              q0_t[rows, i, b * S:(b + 1) * S], k0_t[rows, i, b * S:(b + 1) * S],
                                              start=True, stop=True)
                mm.then_inc(s1_mm, 1)

            pe.wait_ge(q0_ready, PAIRS)
            pe.wait_ge(k0_ready, PAIRS)
            scores_heads(0)
            for b in range(B):
                if b >= 1:
                    pe.wait_ge(v0_ready, 2 * b - 1)
                nc.tensor.matmul(ps[:, 4, :], xn_t[:, b * S:(b + 1) * S], w_qkv[:, 2, 0:BANK],
                                 start=True, stop=True).then_inc(v0_mm, 1)
                if b >= 1:
                    pe.wait_ge(v0_ready, 2 * b)
                nc.tensor.matmul(ps[:, 5, :], xn_t[:, b * S:(b + 1) * S], w_qkv[:, 2, BANK:2 * BANK],
                                 start=True, stop=True).then_inc(v0_mm, 1)
            pe.wait_ge(v0_ready, 2 * B)
            def project_heads(b):
                pe.wait_ge(attn0_loaded, 32)
                pe.wait_ge(h1_ready, b + 1)
                for i in range(PAIRS):
                    mm = nc.tensor.matmul(ps[:, 4, 0:D], heads_t[:, i, b * S:(b + 1) * S], w_out0[:, i, :],
                                          start=(i == 0), stop=(i == PAIRS - 1))
                mm.then_inc(y1_mm, 1)

            for b in range(B):
                if b >= 1:
                    project_heads(b - 1)
                if b + 1 < B:
                    pe.wait_ge(s1_exp, b + 1)
                    scores_heads(b + 1)
                pe.wait_ge(s1_norm, 2 * b + 2)
                if b >= 1:
                    pe.wait_ge(x_done, B + b)
                for j in range(4):
                    n = 4 * b + j
                    if n >= 2:
                        pe.wait_ge(p1_ready, n - 1)
                    for c in range(4):
                        tr = nc.tensor.transpose(ps[:, 4 + j % 2, c * S:(c + 1) * S], probs1[b % 2][:, 4 * j + c, :],
                                                 ident[:])
                    tr.then_inc(p1_trans, 1)
                pe.wait_ge(p1_ready, 4 * (b + 1))
                if b >= 1:
                    pe.wait_ge(h1_ready, b)
                for i in range(PAIRS):
                    for odd in range(2):
                        at = (PAIRS * odd + i) * S
                        head = 2 * i + odd
                        mm = nc.tensor.matmul(ps[DH * odd:DH * (odd + 1), 6 + i // 4, (i % 4) * S:(i % 4 + 1) * S],
                                              v0[:, b, head * DH:(head + 1) * DH], probs1_t[b % 2][:, at:at + S],
                                              start=True, stop=True)
                mm.then_inc(h1_mm, 1)
            project_heads(B - 1)

            norm_tensor(pe, 2)
            pe.wait_ge(ln_done, 3)
            for b in range(B):
                mm = nc.tensor.matmul(ps[:, 0, b * E0:(b + 1) * E0], xn_t[:, b * S:(b + 1) * S], gate_w[:],
                                      start=True, stop=True)
            mm.then_inc(lg0_mm, 1)
            pe.wait_ge(ffn0_loaded, 32)

            def hidden(i):
                if i >= 3:
                    pe.wait_ge(h0_relu, i - 2)
                nc.tensor.matmul(ps[:, 1 + i % 3, :], w1_0[:, i // HC0, i % HC0, :], xn_t[:], start=True, stop=True)\
                  .then_inc(h0_mm, 1)

            def expert(e):
                pe.wait_ge(h0_relu, HC0 * (e + 1))
                if e >= 2:
                    pe.wait_ge(x_moe, B * e)
                for b in range(B):
                    for k in range(HC0):
                        mm = nc.tensor.matmul(ps[:, 4 + e % 2, b * D:(b + 1) * D], h0_t[:, HC0 * e + k, b * S:(b + 1) * S],
                                              w2_0[:, e, k, :], start=(k == 0), stop=(k == HC0 - 1))
                mm.then_inc(e0_mm, 1)

            def key_norm(n):
                if n >= 2:
                    pe.wait_ge(kn_max, n - 1)
                nc.tensor.matmul(ps[0:HH, 6 * (n % 2), :], of_half_h, k_square[:, n * BANK:(n + 1) * BANK],
                                 start=True, stop=True).then_inc(kn_mm, 1)

            for i in range(6):
                hidden(i)
            pe.wait_ge(gate_step, 5)
            for b in range(B):
                tr = nc.tensor.transpose(ps[0:E0, 7, b * S:(b + 1) * S], gates0[:, b, :], ident[:])
            tr.then_inc(g0_trans, 1)
            pe.wait_ge(g0_ready, 1)
            for b in range(B):
                mm = nc.tensor.matmul(ps[:, 7, b * D:(b + 1) * D], gates0_t[:, b * S:(b + 1) * S], b2_0[:],
                                      start=True, stop=True)
            mm.then_inc(b2_mm, 1)
            for e in range(E0):
                if e == 0:
                    pe.wait_ge(consts_d, 1)
                    pe.wait_ge(ksq_ready, 1)
                for i in range(2):
                    if 2 * e + i + 6 < E0 * HC0:
                        hidden(2 * e + i + 6)
                    if 3 * e + i < GROUPS:
                        key_norm(3 * e + i)
                expert(e)
                if 3 * e + 2 < GROUPS:
                    key_norm(3 * e + 2)
            pe.wait_ge(kn_max, GROUPS)
            norm_tensor(pe, 3)
            pe.wait_ge(ln_done, 4)
            nc.tensor.matmul(ps[:, 0, :], wq1_t, xn_t[:], start=True, stop=True).then_inc(q1_mm, 1)
            pe.wait_ge(q1_square, 1)
            nc.tensor.matmul(ps[0:HH, 1, :], of_half, aux_t[:], start=True, stop=True).then_inc(qn_mm, 1)
            pe.wait_ge(bound_step, 2)
            nc.tensor.transpose(ps[0:1, 2, 0:HH], bound_h, ident[0:HH, 0:HH]).then_inc(bound_trans, 1)
            pe.wait_ge(stage_set, 4)
            pe.wait_ge(q_rows_zero, 1)
            pe.wait_ge(ring_ones, 1)
            pe.wait_ge(safe_ready, 1)
            is_safe = pe.value_load(safe)
            with pe.If(is_safe < 1):
                pe.sem_inc(shift_maxed, 2)
                pe.sem_inc(shift_mm, 4 * SLOTS)
                for i in range(SLOTS):
                    pe.wait_ge(q_rows_loaded[i], HG // SLOTS * RING_LOADS)
                with pe.Fori(0, B) as b:
                    for g in range(HG):
                        pe.wait_ge(shift_loaded[g % SLOTS], (b * (HG // SLOTS) + (g // SLOTS + 1)) * RING_LOADS)
                        for j in range(4):
                            h = 4 * g + j
                            pe.wait_ge(shift_maxed, b * HH + (h + 1))
                            for n in range(4):
                                mm = nc.tensor.matmul(ps[:, 4 * (h % 2) + n, :],
                                                      q_rows[0:KROWS, bass.ds(b * (HG * BANK) + (g * BANK + j * S), S)],
                                                      key_ring[0:KROWS, g % SLOTS, n * BANK:(n + 1) * BANK],
                                                      start=True, stop=True)
                            mm.then_inc(shift_mm, 1)
                pe.wait_ge(shift_step, 4)
                for n in range(ITEMS):
                    if n >= 2:
                        pe.wait_ge(shift_rows, n - 1)
                    nc.tensor.matmul(ps[0:12, n % 2, 0:S], shift_parts[:, n, :, :].rearrange("p g c -> p (g c)"),
                                     ident_h[:], start=True, stop=True).then_inc(shift_trans, 1)
                pe.wait_ge(shift_rows, ITEMS)
                for i in range(SLOTS):
                    pe.wait_ge(shift_loaded[i], (B * (HG // SLOTS) + 1) * RING_LOADS)

            pe.sem_inc(exp_done, NBUF)
            pe.sem_inc(pv_done, 2 * QUADS)
            pe.sem_inc(acc_added, 2 * 4)
            pe.sem_inc(folded, 1)

            def score_unit(b, u):
                g = max(i for i in range(HG) if UNIT0[i] <= u)
                c, n = UNITS[g][u - UNIT0[g]]
                if c == 0:
                    pe.wait_ge(q_rows_loaded[g % SLOTS], (g // SLOTS + 1) * RING_LOADS)
                    pe.wait_ge(ring_loaded[g % SLOTS], (b * (HG // SLOTS) + (g // SLOTS + 1)) * RING_LOADS)
                pe.wait_ge(exp_done, b * NU + (u + 1))
                for i in range(n):
                    mm = nc.tensor.matmul(ps[:, UNIT * (u % NBUF) + i, :],
                                          key_ring[0:ROWS, g % SLOTS, (c + i) * P:(c + i + 1) * P],
                                          q_rows[0:ROWS, bass.ds(b * (HG * BANK) + g * BANK, BANK)],
                                          start=True, stop=True)
                mm.then_inc(scores_mm, 1)

            def weigh_quad(b, g, w, u):
                if w == 0:
                    pe.wait_ge(acc_added, b * (HG * 4) + 4 * (g + 1))
                    if g % GI == 1:
                        pe.wait_ge(folded, b * (HG // GI) + (g // GI + 1))
                    pe.wait_ge(staged, b * HG + (g + 1))
                pe.wait_ge(exp_done, b * NU + (u + 1 + NBUF))
                for n in range(4):
                    c = 4 * w + n
                    mm = nc.tensor.matmul(ps[32 * n:32 * (n + 1), 6 + g % 2, :], v_stage[:, g % 2, c, :],
                                          probs_d[c // 8][:, (c % 8) * BANK:(c % 8 + 1) * BANK],
                                          start=(w == 0), stop=(w == QUADS - 1))
                mm.then_inc(pv_done, 1)

            def fold_items(b, q):
                pe.wait_ge(acc_added, b * (HG * 4) + 4 * (GI * (q + 1) + 2))
                for j in range(4):
                    mm = nc.tensor.matmul(
                        ps[:, 7, 0:4 * GI * VCOLS].rearrange("p (i j v) -> p i j v", i=GI, j=4)[:, :, j, :],
                        acc_sb[:, q, j * S:(j + 1) * S],
                        ident[:].rearrange("p (i r) -> p i r", i=GI)[:, :, VCOLS * (j // 2):VCOLS * (j // 2 + 1)],
                        start=True, stop=True)
                mm.then_inc(fold_mm, 1)

            def item(b, g, last, fold=None):
                for k, (c, n) in enumerate(UNITS[g]):
                    u = UNIT0[g] + k
                    if u + NBUF < NU:
                        score_unit(b, u + NBUF)
                    elif not last:
                        score_unit(b + 1, u + NBUF - NU)
                    if (c + n) % 4 == 0:
                        weigh_quad(b, g, c // 4, u)
                    if fold and c == 10:
                        fold_items(*fold)

            def later_items(b, last):
                for g in range(1, HG):
                    item(b, g, last, (b, g // GI - 1) if g % GI == 0 else None)

            for u in range(NBUF):
                score_unit(0, u)
            item(0, 0, False)
            with pe.Fori(0, B - 1) as b:
                later_items(b, False)
                item(b + 1, 0, False, (b, 1))
            later_items(B - 1, True)
            fold_items(B - 1, 1)

            pe.wait_ge(lin_loaded, 16 * 16)
            pe.wait_ge(folded, ITEMS // GI + 1)
            norm_tensor(pe, 4)
            nc.tensor.transpose(ps[:, 7, 0:E1], w_gate, ident[0:E1, 0:E1]).then_inc(wg_trans, 1)
            pe.wait_ge(ln_done, 5)
            for b in range(B):
                nc.tensor.matmul(ps[:, b, 0:3 * D], xn_t[:, b * S:(b + 1) * S], w_qkv1, start=True, stop=False)
                mm = nc.tensor.matmul(ps[:, b, 0:3 * D], ones_row[:], b_qkv1, start=False, stop=True)
            mm.then_inc(lin_mm, 1)
            pe.wait_ge(lin_step, 6)
            for b in range(B):
                tr = nc.tensor.transpose(ps[:, 5, b * S:(b + 1) * S], qk1[:, b, 0:D], ident[:])
            tr.then_inc(qn_trans, 1)
            pe.wait_ge(lin_v, 1)
            for b in range(B):
                mm = nc.tensor.matmul(ps[:, 4, b * D:(b + 1) * D], qk1[:, b, D:2 * D], v1s[:, b, :], start=True, stop=True)
            mm.then_inc(kv_mm, 1)
            pe.wait_ge(qn_ready, 1)
            pe.wait_ge(kv_ready, 3)
            for b in range(B):
                mm = nc.tensor.matmul(ps[:, 6, b * S:(b + 1) * S], kv_diag[:, b, :], qn_t[:, b * S:(b + 1) * S],
                                      start=True, stop=True)
            mm.then_inc(lc_mm, 1)
            pe.wait_ge(wg_ready, 1)
            pe.wait_ge(lc_ready, 1)
            for b in range(B):
                nc.tensor.matmul(ps[:, 7, b * D:(b + 1) * D], lin_t[:, b * S:(b + 1) * S], w_out1, start=True, stop=False)
                mm = nc.tensor.matmul(ps[:, 7, b * D:(b + 1) * D], ones_row[:], b_out1, start=False, stop=True)
            mm.then_inc(lo_mm, 1)
            pe.wait_ge(lin_step, 9)
            for b in range(B):
                tr = nc.tensor.transpose(ps[:, 5, b * S:(b + 1) * S], attn1[:, b, :], ident[:])
            tr.then_inc(a1_trans, 1)
            pe.wait_ge(a1_ready, 1)
            for k in range(FC):
                nc.tensor.matmul(ps[:, k, :], w1_1[:, k * P:(k + 1) * P], attn1_t, start=True, stop=True).then_inc(f1_mm, 1)
            pe.wait_ge(f1_ready, FC)
            for b in range(B):
                for k in range(FC):
                    nc.tensor.matmul(ps[:, 4, b * D:(b + 1) * D], h1_t[:, k, b * S:(b + 1) * S], w2_1[:, k, :],
                                     start=(k == 0), stop=False)
                mm = nc.tensor.matmul(ps[:, 4, b * D:(b + 1) * D], ones_row[:], b2_1, start=False, stop=True)
            mm.then_inc(f2_mm, 1)

            norm_tensor(pe, 7)
            pe.wait_ge(moe1_loaded, 96)
            pe.wait_ge(ln_done, 6)
            for b in range(B):
                mm = nc.tensor.matmul(ps[:, 0, b * E1:(b + 1) * E1], xn_t[:, b * S:(b + 1) * S], wg_t, start=True, stop=True)
            mm.then_inc(lg1_mm, 1)

            def gate_and_up(m):
                rows = P if m < EC else NS * I1
                if m >= 2:
                    pe.wait_ge(hid_step, m - 1)
                for i in range(2):
                    mm = nc.tensor.matmul(ps[0:rows, 2 + i + 3 * (m % 2), :], gate_up[:, i, m * P:m * P + rows],
                                          xn_t[:], start=True, stop=True)
                return mm

            def weights_of(m):
                return nc.tensor.matmul(ps[:, 4 + 3 * (m % 2), :], spread[:, m * P:(m + 1) * P], gate1_t,
                                        start=True, stop=True)

            gate_and_up(0)
            gate_and_up(1)
            pe.wait_ge(g1_step, 8)
            for b in range(B):
                tr = nc.tensor.transpose(ps[0:E1, 1, b * S:(b + 1) * S], gate1[:, b, :], ident[:])
            tr.then_inc(g1_trans, 1)
            pe.wait_ge(g1_ready, 1)
            pe.wait_ge(spread_ready, 1)
            weights_of(0).then_inc(gu_mm, 1)
            weights_of(1).then_inc(gu_mm, 1)
            for m in range(2, EC):
                gate_and_up(m)
                weights_of(m).then_inc(gu_mm, 1)
            gate_and_up(EC).then_inc(gu_mm, 1)
            pe.wait_ge(hid_step, EC + 1)
            for b in range(B):
                for m in range(EC + 1):
                    rows = P if m < EC else NS * I1
                    mm = nc.tensor.matmul(ps[:, b, 0:D], hid1_t[0:rows, m * T + b * S:m * T + (b + 1) * S],
                                          down[0:rows, m, :], start=(m == 0), stop=(m == EC))
                mm.then_inc(down_mm, 1)


def kernel(**inputs):
    import numpy as np
    import concourse.bacc as bacc
    from concourse.bass_utils import run_bass_kernel_spmd

    nc = bacc.Bacc("TRN2", target_bir_lowering=False, num_devices=1)
    arrays, tensors = {}, {}
    for name in NAMES:
        a = np.ascontiguousarray(inputs[name])
        arrays["in_" + name] = a
        tensors[name] = nc.dram_tensor("in_" + name, a.shape, mybir.dt.from_np(a.dtype), kind="ExternalInput").ap()
    out = nc.dram_tensor("out_x", inputs['x'].shape, F32, kind="ExternalOutput").ap()
    build_program(nc, tensors, out)
    r = run_bass_kernel_spmd(nc, [arrays], core_ids=[0])
    return r.results[0]["out_x"]
```

```python
from contextlib import ExitStack

import concourse.bass as bass
from concourse import mybir

ALU = mybir.AluOpType
ACT = mybir.ActivationFunctionType
AX = mybir.AxisListType
F32 = mybir.dt.float32
BF16 = mybir.dt.bfloat16
I32 = mybir.dt.int32

NAMES = ['x', 'ctx_1024', 'mask_BxS2_ik1', 'L0_xattn_Wq', 'L0_xattn_Wk', 'L0_xattn_Wv', 'L0_attn_kernel',
         'L0_attn_WO', 'L0_ffn_gate_w', 'L0_ffn_gate_b', 'L0_ffn_w1', 'L0_ffn_b1', 'L0_ffn_w2', 'L0_ffn_b2',
         'L1_xattn_Wq', 'L1_xattn_Wk', 'L1_xattn_Wv', 'L1_xattn_lambda_q1', 'L1_xattn_lambda_q2',
         'L1_xattn_lambda_k1', 'L1_xattn_lambda_k2', 'L1_attn_Wq', 'L1_attn_bq', 'L1_attn_Wk', 'L1_attn_bk',
         'L1_attn_Wv', 'L1_attn_bv', 'L1_attn_Wo', 'L1_attn_bo', 'L1_attn_g1', 'L1_attn_be1', 'L1_attn_W1',
         'L1_attn_b1', 'L1_attn_W2', 'L1_attn_b2', 'L1_attn_g2', 'L1_attn_be2', 'L1_ffn_Wg',
         'L1_ffn_W_gate_up', 'L1_ffn_W_down', 'L1_ffn_Ws_gate_up', 'L1_ffn_Ws_down']


def build_program(nc, t, out):
    P = 128
    B, S, D = t['x'].shape
    T = B * S
    KEYS = t['ctx_1024'].shape[1]
    KC = KEYS // P
    NCHUNK = B * KC
    BANK = 512
    GROUPS = NCHUNK * P // BANK
    GB = KEYS // BANK
    assert S == P and D == P

    with ExitStack() as ctx:
        def sb(name, shape, dt=F32):
            return ctx.enter_context(nc.sbuf_tensor(name, shape, dt))

        def sem(name):
            return ctx.enter_context(nc.semaphore(name))

        ps = ctx.enter_context(nc.psum_tensor("ps", [P, 8, BANK], F32))
        x = sb("x_res", [P, B, D])
        xn = sb("xn", [P, B, D])
        xn_t = sb("xn_t", [P, T])
        aux_t = sb("aux_t", [P, T])
        ident = sb("ident", [P, P])
        ident_h = sb("ident_h", [P, P], BF16)
        stats = sb("stats", [P, B, 6])
        mean_var = sb("mean_var", [P, B, 2])
        var_eps = sb("var_eps", [P, B])
        rstd = sb("rstd", [P, B])
        minus_half = sb("minus_half", [P, 64])
        small_w = sb("small_w", [P, 5, D])
        wqk0, wv0_t, wk1_t, wv1_t, wq1_t = (small_w[:, i, :] for i in range(5))

        wide = sb("wide", [P, 16384])
        work = sb("work", [P, 8192])
        weights = sb("weights", [P, 4096])
        k_parts = sb("k_parts", [P, 3, NCHUNK * P], BF16)
        v1 = sb("v1", [P, NCHUNK, D])

        ctx_sb = wide[:, 0:8192].rearrange("p (c f) -> p c f", f=D)
        ctx_t = wide[:, 8192:16384]
        scores0 = [work[:, 2048 * i:2048 * (i + 1)] for i in range(2)]
        probs0_t = work[:, 4096:6144].rearrange("p (c s) -> p c s", s=S)
        mask_sb = work[:, 6144:8192].bitcast(I32)
        raw_w = k_parts[:, 2, 6144:8192].bitcast(F32)[:, 0:768].rearrange("p (i f) -> p i f", f=D)
        max0 = sb("max0", [P, B, 2])
        nmax0 = sb("nmax0", [P, B])
        sum0 = sb("sum0", [P, B, 2])
        rsum0 = sb("rsum0", [P, B])
        o1_t = xn[:, 0, :]

        HEADS, DH = t['L0_attn_kernel'].shape[1], t['L0_attn_kernel'].shape[3]
        PAIRS = HEADS // 2
        SCALE0 = 1.0 / (DH * DH * HEADS)
        w_qkv = weights[:, 0:3 * HEADS * DH].rearrange("p (c n) -> p c n", c=3)
        w_out0 = weights[:, 3 * HEADS * DH:4096].rearrange("p (i m) -> p i m", i=PAIRS)
        k_left = weights[:, 3 * HEADS * DH:4096].rearrange("p (i c) -> p i c", i=2)
        q0_t = wide[:, 0:4096].rearrange("p (i c) -> p i c", i=PAIRS)
        k0_t = wide[:, 4096:8192].rearrange("p (i c) -> p i c", i=PAIRS)
        v0 = wide[:, 8192:12288].rearrange("p (b n) -> p b n", b=B)
        heads_t = wide[:, 12288:16384].rearrange("p (i c) -> p i c", i=PAIRS)
        probs1 = [work[:, 2048 * i:2048 * (i + 1)].rearrange("p (h c) -> p h c", h=HEADS) for i in range(2)]
        probs1_t = [work[:, 4096 + 2048 * i:6144 + 2048 * i] for i in range(2)]
        max1 = sb("max1", [P, B, HEADS])
        nmax1 = sb("nmax1", [P, B, HEADS])
        sum1 = sb("sum1", [P, B, HEADS])
        rsum1 = sb("rsum1", [P, B, HEADS])

        E0 = t['L0_ffn_gate_w'].shape[1]
        HC0 = t['L0_ffn_w1'].shape[2] // P
        NEVER = 3.0e38
        ROW_LOADS = 16 * (5 + 4)
        w1_0 = wide[:, 4096:6144].rearrange("p (e k c) -> p e k c", e=E0, k=HC0)
        w2_0 = wide[:, 6144:8192].rearrange("p (e k c) -> p e k c", e=E0, k=HC0)
        h0_t = wide[:, 8192:16384].rearrange("p (i c) -> p i c", i=E0 * HC0)
        lam_load = sb("lam_load", [P, 4, 4])
        gate_w = sb("gate_w", [P, E0])
        gate_b = sb("gate_b", [P, E0])
        b2_0 = sb("b2_0", [E0, D])
        BR0, BR1 = E0 * HC0, 4
        b1_rows = sb("b1_rows", [BR0 + BR1, P])
        b1_cols = sb("b1_cols", [P, BR0 + BR1])
        logits0 = sb("logits0", [P, B, 2 * E0])
        top0 = sb("top0", [P, B, 8])
        picks0 = sb("picks0", [P, B, 8])
        struck0 = sb("struck0", [P, B, 2 * E0])
        ntop0 = sb("ntop0", [P, B])
        gate_e = sb("gate_e", [P, B, E0])
        gate_sum = sb("gate_sum", [P, B])
        gate_r = sb("gate_r", [P, B])
        gates0 = sb("gates0", [P, B, E0])
        gates0_t = aux_t[0:E0, :]
        HH = 32
        HG = HH // 4
        ITEMS = B * HG
        PAIRS_QK = ((0, 0), (0, 1), (0, 2), (1, 0), (1, 1), (2, 0))
        KROWS = 16 * len(PAIRS_QK)
        ROWS = KROWS + 12
        RING_LOADS = 16 * len(PAIRS_QK)
        SCALE1 = 0.5
        UNIT = 2
        NBUF = 3
        UNITS = []
        for g in range(HG):
            UNITS.append([(c, UNIT) for c in range(0, KC, UNIT)])
            if g % 4 == 3:
                UNITS[g][-1:] = [(KC - 2, 1), (KC - 1, 1)]
        UNIT0 = [sum(len(u) for u in UNITS[:g]) for g in range(HG + 1)]
        NU = UNIT0[HG]
        QUADS = KC // 4
        GI = 4
        SLOTS = 4
        VCOLS = 9
        LIMIT = 64.0
        probs_d = (wide[:, 0:4096], weights[:, 0:4096])
        k_square = wide[:, 0:4096].bitcast(BF16)
        q_rows = wide[:, 4096:12288].bitcast(BF16)
        acc_sb = wide[:, 12288:13312].rearrange("p (i c) -> p i c", i=2)
        heads_d = wide[:, 13312:14464].rearrange("p (i v) -> p i v", v=VCOLS)
        q_parts = wide[:, 14464:15232].bitcast(BF16).rearrange("p (i c) -> p i c", i=3)
        shift_parts = wide[:, 15232:15424].bitcast(BF16).rearrange("p (i g c) -> p i g c", i=ITEMS, g=3)
        key_ring = work[:, 0:4096].bitcast(BF16).rearrange("p (i c) -> p i c", i=SLOTS)
        q_masked = work[:, 4096:7168].bitcast(BF16).rearrange("p (i b j c) -> p i b j c", i=3, b=B, j=4)
        v_stage = work[:, 7168:8192].rearrange("p (i c v) -> p i c v", i=2, c=KC)
        small_d = small_w.rearrange("p i f -> p (i f)")
        of_half = small_d[:, 32:64]
        of_half_h = small_d[:, 64:80].bitcast(BF16)
        of_j = small_d[:, 80:84]
        of_j12 = small_d[:, 84:88]
        lam_prod = small_d[:, 104:112].rearrange("p (a f) -> p a f", a=2)
        lam_sum = small_d[:, 112:114]
        lam_exp = small_d[:, 114:116]
        neg_lam = small_d[:, 116:117]
        k_norms = small_d[0:HH, 120:136]
        k_norm = small_d[0:HH, 136:137]
        q_norm = small_d[0:HH, 137:138]
        bound_h = small_d[0:HH, 138:139]
        bound = small_d[0:1, 139:140]
        safe = small_d[0:1, 140:141].bitcast(I32)
        shift_max = small_d[:, 144:272]
        shift_left = small_d[:, 272:400]
        den_r = small_d[:, 144:272]
        HEADS1 = 16
        DH1 = D // HEADS1
        LIN_LOADS = 16 * 16
        FC = t['L1_attn_W1'].shape[1] // P
        w_qkv1 = work[:, 4096:4480]
        w_out1 = work[:, 4480:4608]
        w1_1 = work[:, 4608:5120]
        w2_1 = work[:, 5120:5632].rearrange("p (k c) -> p k c", k=FC)
        w_gate = work[0:32, 5632:5760]
        b_qkv1 = work[:, 5760:6144]
        b_out1 = work[:, 6144:6272]
        b2_1 = work[:, 6272:6400]
        affine = aux_t[:].rearrange("p (i f) -> p i f", i=4)
        qkv1 = wide[:, 0:1536].rearrange("p (b n) -> p b n", b=B)
        qk1 = qkv1[:, :, 0:2 * D]
        v1s = qkv1[:, :, 2 * D:3 * D]
        qk_low = wide[:, 1536:2560].rearrange("p (b n) -> p b n", b=B)
        qk_sq = wide[:, 2560:3584].rearrange("p (b n) -> p b n", b=B)
        qk_norm = wide[:, 3584:3712]
        of_eight = wide[:, 3712:3728]
        kv_diag = wide[:, 3728:4240].rearrange("p (b n) -> p b n", b=B)
        qn_t = wide[:, 4240:4752]
        lin_t = wide[:, 4752:5264]
        res1 = wide[:, 5264:5776].rearrange("p (b n) -> p b n", b=B)
        attn1 = wide[:, 5776:6288].rearrange("p (b n) -> p b n", b=B)
        attn1_t = wide[:, 6288:6800]
        h1_t = wide[:, 6800:8848].rearrange("p (k c) -> p k c", k=FC)
        qk_rs = wide[:, 8848:8976]
        qk_root = wide[:, 8976:9104]
        f2_sum = wide[:, 2560:3072].rearrange("p (b n) -> p b n", b=B)

        E1, I1 = t['L1_ffn_W_down'].shape[0:2]
        NS = t['L1_ffn_Ws_down'].shape[0]
        EC = E1 * I1 // P
        gate_up = weights[:, 0:(E1 + NS) * 2 * I1].rearrange("p (i n) -> p i n", i=2)
        down = weights[:, 2304:2304 + (EC + 1) * D].rearrange("p (m c) -> p m c", c=D)
        wg_t = wide[:, 9216:9216 + E1]
        spread = wide[0:3 * E1, 9728:9728 + E1 * I1 // 2].bitcast(BF16)
        logits1 = wide[:, 10752:10880].rearrange("p (b e) -> p b e", b=B)
        struck1 = wide[:, 10880:11008].rearrange("p (b e) -> p b e", b=B)
        gate1 = wide[:, 11008:11136].rearrange("p (b e) -> p b e", b=B)
        top1 = wide[:, 11136:11168].rearrange("p (b e) -> p b e", b=B)
        ntop1 = wide[:, 11168:11172]
        gsum1 = wide[:, 11172:11176]
        grec1 = wide[:, 11176:11180]
        gate1_parts = wide[:, 12800:12992].bitcast(BF16).rearrange("p (b i e) -> p b i e", b=B, i=3)
        gate1_left = wide[:, 12992:13120].rearrange("p (b e) -> p b e", b=B)
        gate1_t = wide[0:3 * E1, 11264:11520].bitcast(BF16)
        silu = [wide[:, 11776 + 512 * i:12288 + 512 * i] for i in range(2)]
        hid1_t = work[:, 0:(EC + 1) * T]
        x_loaded = sem("x_loaded")
        raw_loaded = sem("raw_loaded")
        ctx_loaded = [sem(f"ctx_loaded{b}") for b in range(B)]
        mask_loaded = sem("mask_loaded")
        ident_zero = sem("ident_zero")
        ident_ready = sem("ident_ready")
        half_ready = sem("half_ready")
        ln_step = sem("ln_step")
        ln_rstd = sem("ln_rstd")
        ln_xn = sem("ln_xn")
        ln_trans = sem("ln_trans")
        ln_done = sem("ln_done")
        small_mm = sem("small_mm")
        small_ready = sem("small_ready")
        qk_mm = sem("qk_mm")
        qk_ready = sem("qk_ready")
        ct_trans = sem("ct_trans")
        ct_ready = sem("ct_ready")
        k_mm = sem("k_mm")
        v_mm = sem("v_mm")
        k_first = sem("k_first")
        k_left1 = sem("k_left1")
        k_second = sem("k_second")
        k_third = sem("k_third")
        v_ready = sem("v_ready")
        s0_mm = sem("s0_mm")
        s0_fill = sem("s0_fill")
        s0_masked = sem("s0_masked")
        s0_max = sem("s0_max")
        s0_exp = sem("s0_exp")
        s0_rsum = sem("s0_rsum")
        p0_trans = sem("p0_trans")
        p0_ready = sem("p0_ready")
        o1_mm = sem("o1_mm")
        o1_ready = sem("o1_ready")
        y0_mm = sem("y0_mm")
        x_done = sem("x_done")
        stored = sem("stored")

        qkv0_loaded = sem("qkv0_loaded")
        attn0_loaded = sem("attn0_loaded")
        q0_mm = sem("q0_mm")
        k0_mm = sem("k0_mm")
        v0_mm = sem("v0_mm")
        q0_ready = sem("q0_ready")
        k0_ready = sem("k0_ready")
        v0_ready = sem("v0_ready")
        s1_mm = sem("s1_mm")
        s1_max = sem("s1_max")
        s1_exp = sem("s1_exp")
        s1_norm = sem("s1_norm")
        p1_trans = sem("p1_trans")
        p1_ready = sem("p1_ready")
        h1_mm = sem("h1_mm")
        h1_ready = sem("h1_ready")
        y1_mm = sem("y1_mm")
        rows_loaded = sem("rows_loaded")
        consts = sem("consts")
        cols_mm = sem("cols_mm")
        cols_ready = sem("cols_ready")
        ffn0_loaded = sem("ffn0_loaded")
        lg0_mm = sem("lg0_mm")
        picks0_step = sem("picks0_step")
        gate_exp = sem("gate_exp")
        gate_step = sem("gate_step")
        g0_trans = sem("g0_trans")
        g0_ready = sem("g0_ready")
        b2_mm = sem("b2_mm")
        h0_mm = sem("h0_mm")
        h0_relu = sem("h0_relu")
        e0_mm = sem("e0_mm")
        x_moe = sem("x_moe")
        consts_d = sem("consts_d")
        ksq_ready = sem("ksq_ready")
        kn_mm = sem("kn_mm")
        kn_max = sem("kn_max")
        lam_step = sem("lam_step")
        q1_mm = sem("q1_mm")
        q1_part = sem("q1_part")
        q1_left = sem("q1_left")
        q1_square = sem("q1_square")
        qn_mm = sem("qn_mm")
        bound_step = sem("bound_step")
        bound_trans = sem("bound_trans")
        safe_ready = sem("safe_ready")
        q_masked_ready = sem("q_masked_ready")
        q_rows_zero = sem("q_rows_zero")
        q_rows_loaded = [sem(f"q_rows_loaded{i}") for i in range(SLOTS)]
        ring_ones = sem("ring_ones")
        stage_set = sem("stage_set")
        shift_loaded = [sem(f"shift_loaded{i}") for i in range(SLOTS)]
        shift_mm = sem("shift_mm")
        shift_maxed = sem("shift_maxed")
        shift_step = sem("shift_step")
        shift_trans = sem("shift_trans")
        shift_rows = sem("shift_rows")
        ring_loaded = [sem(f"ring_loaded{i}") for i in range(SLOTS)]
        scores_mm = sem("scores_mm")
        exp_done = sem("exp_done")
        pv_done = sem("pv_done")
        acc_added = sem("acc_added")
        staged = sem("staged")
        fold_mm = sem("fold_mm")
        folded = sem("folded")
        comb_step = sem("comb_step")
        x_diff = sem("x_diff")
        x_lin = sem("x_lin")
        top1_ready = sem("top1_ready")
        hid_half = sem("hid_half")
        lin_loaded = sem("lin_loaded")
        moe1_loaded = sem("moe1_loaded")
        wg_trans = sem("wg_trans")
        wg_ready = sem("wg_ready")
        lin_mm = sem("lin_mm")
        lin_in = sem("lin_in")
        lin_exp = sem("lin_exp")
        lin_elu = sem("lin_elu")
        lin_norm = sem("lin_norm")
        lin_unit = sem("lin_unit")
        lin_own = sem("lin_own")
        ln_scaled = sem("ln_scaled")
        lin_sq = sem("lin_sq")
        lin_root = sem("lin_root")
        kv_mm = sem("kv_mm")
        kv_ready = sem("kv_ready")
        qn_trans = sem("qn_trans")
        qn_ready = sem("qn_ready")
        lc_mm = sem("lc_mm")
        lc_ready = sem("lc_ready")
        lo_mm = sem("lo_mm")
        a1_trans = sem("a1_trans")
        a1_ready = sem("a1_ready")
        f1_mm = sem("f1_mm")
        f1_ready = sem("f1_ready")
        f2_mm = sem("f2_mm")
        lg1_mm = sem("lg1_mm")
        g1_step = sem("g1_step")
        g1_exp = sem("g1_exp")
        g1_trans = sem("g1_trans")
        g1_ready = sem("g1_ready")
        gu_mm = sem("gu_mm")
        wt_mm = sem("wt_mm")
        silu_ready = sem("silu_ready")
        hid_step = sem("hid_step")
        down_mm = sem("down_mm")
        x_final = sem("x_final")
        block = ctx.enter_context(nc.Block())
        LN_BANK = 6
        LN_STEPS = 2 * B + 1

        def row_stats(dve, n, b, src=x):
            nc.vector.bn_stats(stats[:, b, :], src[:, b, :]).then_inc(ln_step, 1)
            dve.wait_ge(ln_step, LN_STEPS * n + 2 * b + 1)
            nc.vector.bn_aggr(mean_var[:, b, :], stats[:, b, :]).then_inc(ln_step, 1)

        def all_stats(dve, n, ready, base, src=x):
            for b in range(B):
                if ready:
                    dve.wait_ge(ready, base + b + 1)
                nc.vector.bn_stats(stats[:, b, :], src[:, b, :]).then_inc(ln_step, 1)
            for b in range(B):
                dve.wait_ge(ln_step, LN_STEPS * n + b + 1)
                nc.vector.bn_aggr(mean_var[:, b, :], stats[:, b, :]).then_inc(ln_step, 1)

        def norm_vector(dve, n, eps):
            dve.wait_ge(ln_step, LN_STEPS * n + 2 * B)
            nc.vector.tensor_scalar_add(var_eps[:], mean_var[:, :, 1], eps).then_inc(ln_step, 1)
            dve.wait_ge(ln_rstd, n + 1)
            for b in range(B):
                nc.vector.tensor_scalar(xn[:, b, :], x[:, b, :], mean_var[:, b, 0:1], rstd[:, b:b + 1],
                                        ALU.subtract, ALU.mult).then_inc(ln_xn, 1)

        def affine_norm_vector(dve, n, eps, src, dst, i):
            dve.wait_ge(ln_step, LN_STEPS * n + 2 * B)
            nc.vector.tensor_scalar_add(var_eps[:], mean_var[:, :, 1], eps).then_inc(ln_step, 1)
            for b in range(B):
                nc.vector.scalar_tensor_tensor(dst[:, b, :], src[:, b, :], mean_var[:, b, 0:1], affine[:, i, :],
                                               ALU.subtract, ALU.mult).then_inc(ln_scaled, 1)
            dve.wait_ge(ln_rstd, n + 1)
            for b in range(B):
                dve.wait_ge(ln_scaled, 2 * i + b + 1)
                nc.vector.scalar_tensor_tensor(dst[:, b, :], dst[:, b, :], rstd[:, b:b + 1], affine[:, i + 1, :],
                                               ALU.mult, ALU.add).then_inc(ln_xn, 1)

        def norm_gpsimd(pool, n):
            pool.wait_ge(ln_step, LN_STEPS * (n + 1))
            nc.gpsimd.tensor_tensor(rstd[:], var_eps[:], minus_half[:, 0:B], ALU.pow).then_inc(ln_rstd, 1)

        def norm_tensor(pe, n, src=xn):
            for b in range(B):
                pe.wait_ge(ln_xn, B * n + b + 1)
                tr = nc.tensor.transpose(ps[:, LN_BANK, b * S:(b + 1) * S], src[:, b, :], ident[:])
            tr.then_inc(ln_trans, 1)

        def norm_scalar(act, n):
            act.wait_ge(ln_trans, n + 1)
            nc.scalar.copy(xn_t[:], ps[:, LN_BANK, :]).then_inc(ln_done, 1)

        def ct_bank(n):
            return 3 * (n % 2) if n < GB else 0

        def keep_warm(n, bank):
            for _ in range(n):
                nc.tensor.matmul(ps[:, bank, :].rearrange("p (a c) -> p a c", a=4), ident_h[:],
                                 ident_h[:].unsqueeze(1).to_broadcast([P, 4, P]), start=True, stop=True)

        @block.sync
        def _(sp):
            sp.dma_start(x[:], t['x'].rearrange("b s f -> s b f")).then_inc(x_loaded, 16)
            for i, name in enumerate(('L0_xattn_Wq', 'L0_xattn_Wk', 'L0_xattn_Wv', 'L1_xattn_Wk',
                                      'L1_xattn_Wv', 'L1_xattn_Wq')):
                sp.dma_start(raw_w[:, i, :], t[name]).then_inc(raw_loaded, 16)
            ctx_d = t['ctx_1024'].rearrange("b (c p) f -> b p c f", p=P)
            for b in range(B):
                sp.dma_start(ctx_sb[:, b * KC:(b + 1) * KC, :], ctx_d[b]).then_inc(ctx_loaded[b], 16)
                if b >= 1:
                    sp.wait_ge(s0_masked, 2 * b)
                sp.dma_start(mask_sb, t['mask_BxS2_ik1'][b:b + 1, :].broadcast_to([P, KEYS]))\
                  .then_inc(mask_loaded, 16)
                if b == 1:
                    sp.dma_start(b1_rows[0:BR0, :], t['L0_ffn_b1'].rearrange("e (k p) -> (e k) p", p=P)).then_inc(rows_loaded, 16)
                    sp.dma_start(b1_rows[BR0:BR0 + BR1, :], t['L1_attn_b1'].rearrange("(k p) -> k p", p=P)).then_inc(rows_loaded, 16)
                    sp.dma_start(gate_w[:], t['L0_ffn_gate_w']).then_inc(rows_loaded, 16)
                    sp.dma_start(gate_b[:], t['L0_ffn_gate_b'].rearrange("(a e) -> a e", a=1).broadcast_to([P, E0])).then_inc(rows_loaded, 16)
                    sp.dma_start(b2_0[:], t['L0_ffn_b2']).then_inc(rows_loaded, 16)
                    for i, name in enumerate(('q1', 'k1', 'q2', 'k2')):
                        sp.dma_start(lam_load[:, i, :], t['L1_xattn_lambda_' + name].rearrange("(a f) -> a f", a=1)
                                      .broadcast_to([P, 4])).then_inc(rows_loaded, 16)
            sp.dma_start(w_qkv.rearrange("p c (h d) -> p c h d", h=HEADS),
                         t['L0_attn_kernel'].rearrange("c h m d -> m c h d")).then_inc(qkv0_loaded, 16)
            sp.wait_ge(k_third, GROUPS)
            wo_d = t['L0_attn_WO'][0].rearrange("(d i two) m -> two d i m", i=PAIRS, two=2)
            for i in range(2):
                sp.dma_start(w_out0[DH * i:DH * (i + 1), :, :], wo_d[i]).then_inc(attn0_loaded, 16)
            sp.wait_ge(s1_mm, B)
            sp.dma_start(w1_0.rearrange("p e k c -> p e (k c)"), t['L0_ffn_w1'].rearrange("e c h -> c e h"))\
              .then_inc(ffn0_loaded, 16)
            sp.dma_start(w2_0, t['L0_ffn_w2'].rearrange("e (k p) c -> p e k c", p=P)).then_inc(ffn0_loaded, 16)
            def load_keys(b, g, loaded):
                for r, (_, part) in enumerate(PAIRS_QK):
                    sp.dma_start(key_ring[16 * r:16 * (r + 1), g % SLOTS, :],
                                 k_parts[16 * g:16 * (g + 1), part, bass.ds(b * KEYS, KEYS)])\
                      .then_inc(loaded[g % SLOTS], 16)

            sp.wait_ge(x_done, 2 * B)
            for g in range(SLOTS):
                load_keys(0, g, ring_loaded)
            for g in range(HG):
                if g >= SLOTS:
                    sp.wait_ge(q_rows_loaded[g % SLOTS], RING_LOADS)
                for r, (part, _) in enumerate(PAIRS_QK):
                    if g == 0:
                        sp.wait_ge(q_masked_ready, 4 * (part + 1))
                    dst = q_rows[16 * r:16 * (r + 1), :].rearrange("p (b g c) -> p b g c", b=B, g=HG)[:, :, g, :]
                    src = q_masked[16 * g:16 * (g + 1), part, :, :, :].rearrange("p b j c -> p b (j c)")
                    sp.dma_start(dst, src).then_inc(q_rows_loaded[g % SLOTS], 16)

            sp.wait_ge(safe_ready, 1)
            is_safe = sp.value_load(safe)
            with sp.If(is_safe < 1):
                for i in range(SLOTS):
                    sp.wait_ge(ring_loaded[i], RING_LOADS)
                with sp.Fori(0, B) as b:
                    for g in range(HG):
                        sp.wait_ge(shift_mm, b * HH + (4 * g + 4))
                        load_keys(b, g, shift_loaded)
                for g in range(SLOTS):
                    sp.wait_ge(shift_mm, B * HH + 4 * (g + 1))
                    load_keys(0, g, shift_loaded)
            for g in range(SLOTS, HG):
                sp.wait_ge(scores_mm, UNIT0[g - SLOTS + 1])
                load_keys(0, g, ring_loaded)
            with sp.Fori(1, B) as b:
                for g in range(HG):
                    if g < SLOTS:
                        sp.wait_ge(scores_mm, (b - 1) * NU + UNIT0[g - SLOTS + 1 + HG])
                    else:
                        sp.wait_ge(scores_mm, b * NU + UNIT0[g - SLOTS + 1])
                    load_keys(b, g, ring_loaded)
            for dst, name in ((w_qkv1[:, 0:D], 'Wq'), (w_qkv1[:, D:2 * D], 'Wk'), (w_qkv1[:, 2 * D:3 * D], 'Wv'),
                              (w_out1, 'Wo'), (w1_1, 'W1')):
                sp.dma_start(dst, t['L1_attn_' + name]).then_inc(lin_loaded, 16)
            sp.dma_start(w2_1, t['L1_attn_W2'].rearrange("(k p) c -> p k c", p=P)).then_inc(lin_loaded, 16)
            for dst, name in ((b_qkv1[:, 0:D], 'bq'), (b_qkv1[:, D:2 * D], 'bk'), (b_qkv1[:, 2 * D:3 * D], 'bv'),
                              (b_out1, 'bo'), (b2_1, 'b2')):
                sp.dma_start(dst, t['L1_attn_' + name].rearrange("(a f) -> a f", a=1).broadcast_to([P, D]))\
                  .then_inc(lin_loaded, 16)
            for i, name in enumerate(('g1', 'be1', 'g2', 'be2')):
                sp.dma_start(affine[:, i, :], t['L1_attn_' + name].rearrange("(a f) -> a f", a=1).broadcast_to([P, D]))\
                  .then_inc(lin_loaded, 16)
            sp.dma_start(w_gate, t['L1_ffn_Wg']).then_inc(lin_loaded, 16)
            sp.wait_ge(pv_done, (ITEMS + 2) * QUADS)
            for i in range(2):
                half = gate_up[:, i, :].rearrange("p (e n) -> p e n", n=I1)
                cols = slice(I1 * i, I1 * (i + 1))
                sp.dma_start(half[:, 0:E1, :], t['L1_ffn_W_gate_up'][:, :, cols].rearrange("e c n -> c e n")).then_inc(moe1_loaded, 16)
                sp.dma_start(half[:, E1:E1 + NS, :], t['L1_ffn_Ws_gate_up'][:, :, cols].rearrange("e c n -> c e n")).then_inc(moe1_loaded, 16)
            sp.dma_start(down[:, 0:EC, :], t['L1_ffn_W_down'].rearrange("(m e) i c -> (e i) m c", m=EC)).then_inc(moe1_loaded, 16)
            sp.dma_start(down[0:NS * I1, EC, :], t['L1_ffn_Ws_down'].rearrange("e i c -> (e i) c")).then_inc(moe1_loaded, 16)
            sp.wait_ge(x_final, B)
            sp.dma_start(out.rearrange("b s f -> s b f"), x[:]).then_inc(stored, 16)
            sp.wait_ge(stored, 16)

        @block.gpsimd
        def _(pool):
            nc.gpsimd.memset(ident[:], 0.0).then_inc(ident_zero, 1)
            nc.gpsimd.memset(ident_h[:], 0.0).then_inc(ident_zero, 1)
            nc.gpsimd.memset(minus_half[:], -0.5).then_inc(half_ready, 1)
            pool.wait_ge(ident_zero, 2)
            for m in (ident, ident_h):
                nc.gpsimd.affine_select(out=m[:], in_=m[:], compare_op=ALU.not_equal, fill=1.0, base=0,
                                        pattern=[[-1, P]], channel_multiplier=1).then_inc(ident_ready, 1)
            pool.wait_ge(half_ready, 1)
            norm_gpsimd(pool, 0)
            for b in range(2):
                nc.gpsimd.memset(scores0[b], -99999.0).then_inc(s0_fill, 1)
            for n in range(GROUPS):
                pool.wait_ge(k_left1, n + 1)
                nc.gpsimd.tensor_copy(k_parts[:, 1, n * BANK:(n + 1) * BANK], k_left[:, n % 2, :])\
                  .then_inc(k_second, 1)
                pool.wait_ge(k_second, n + 1)
                nc.gpsimd.tensor_tensor(k_parts[:, 2, n * BANK:(n + 1) * BANK], k_left[:, n % 2, :],
                                        k_parts[:, 1, n * BANK:(n + 1) * BANK], ALU.subtract)\
                  .then_inc(k_third, 1)
                if n % GB == 0 and 2 <= n // GB + 1 < B:
                    b = n // GB + 1
                    pool.wait_ge(p0_trans, 4 * (b - 1))
                    nc.gpsimd.memset(scores0[b % 2], -99999.0).then_inc(s0_fill, 1)
            nc.gpsimd.memset(logits0[:], -NEVER).then_inc(consts, 1)
            nc.gpsimd.memset(picks0[:], -NEVER).then_inc(consts, 1)
            norm_gpsimd(pool, 1)
            norm_gpsimd(pool, 2)
            pool.wait_ge(x_done, 2 * B)
            pool.wait_ge(ln_rstd, 3)
            nc.gpsimd.memset(key_ring[KROWS:ROWS, :, :], 1.0).then_inc(ring_ones, 1)
            pool.wait_ge(ring_ones, 1)
            nc.gpsimd.memset(v_stage, 0.0).then_inc(stage_set, 1)
            pool.wait_ge(stage_set, 1)
            for i in range(2):
                nc.gpsimd.memset(v_stage[:, :, :, VCOLS * i + 8:VCOLS * i + 9], 1.0).then_inc(stage_set, 1)
            norm_gpsimd(pool, 3)
            pool.wait_ge(x_moe, B * (E0 + 1))
            pool.wait_ge(ln_rstd, 4)
            pool.wait_ge(stage_set, 3)
            nc.gpsimd.memset(wide[KROWS:ROWS, 4096:8192], 0.0).then_inc(stage_set, 1)
            pool.wait_ge(stage_set, 4)
            with pool.Fori(0, B) as b:
                for g in range(HG):
                    pool.wait_ge(pv_done, b * (HG * QUADS) + (g + 1) * QUADS)
                    nc.gpsimd.tensor_copy(
                        v_stage[:, g % 2, :, 0:2 * VCOLS].rearrange("p c (i v) -> p c i v", i=2)[:, :, :, 0:8],
                        v1[:, bass.ds(b * KC, KC), 16 * g:16 * (g + 1)].rearrange("p c (i v) -> p c i v", i=2))\
                      .then_inc(staged, 1)
            norm_gpsimd(pool, 4)
            norm_gpsimd(pool, 5)
            norm_gpsimd(pool, 6)
            norm_gpsimd(pool, 7)

        @block.scalar
        def _(act):
            act.wait_ge(small_mm, 1)
            nc.scalar.copy(small_w[:, 0:4, :], ps[:, 0, :].rearrange("p (i f) -> p i f", f=D))\
              .then_inc(small_ready, 1)
            nc.scalar.copy(small_w[:, 4, :], ps[:, 1, 0:D]).then_inc(small_ready, 1)
            norm_scalar(act, 0)

            def context_group(n):
                act.wait_ge(ct_trans, n + 1)
                nc.scalar.copy(ctx_t[:, n * BANK:(n + 1) * BANK], ps[:, ct_bank(n), :]).then_inc(ct_ready, 1)

            def keys_values(n):
                act.wait_ge(k_mm, n + 1)
                nc.scalar.copy(k_parts[:, 0, n * BANK:(n + 1) * BANK], ps[:, 1 + n % 2, :]).then_inc(k_first, 1)
                act.wait_ge(v_mm, n + 1)
                nc.scalar.copy(v1[:, 4 * n:4 * n + 4, :], ps[:, 3, :].rearrange("p (c f) -> p c f", f=D))\
                  .then_inc(v_ready, 1)

            def exps(b, i):
                half = scores0[b % 2][:, KEYS // 2 * i:KEYS // 2 * (i + 1)]
                act.wait_ge(s0_max, 3 * b + 3)
                nc.scalar.activation(half, half, ACT.Exp, bias=nmax0[:, b:b + 1],
                                     accum_out=sum0[:, b, i:i + 1]).then_inc(s0_exp, 1)

            def probs_out(b):
                if b >= 1:
                    act.wait_ge(o1_mm, b)
                for j in range(4):
                    act.wait_ge(p0_trans, 4 * b + j + 1)
                    nc.scalar.copy(probs0_t[:, 4 * j:4 * j + 4, :], ps[:, 4 + j, :].rearrange("p (c s) -> p c s", s=S))\
                      .then_inc(p0_ready, 1)

            def context_out(b):
                act.wait_ge(o1_mm, b + 1)
                nc.scalar.copy(o1_t, ps[:, 3, 0:S]).then_inc(o1_ready, 1)

            for j in range(GB):
                context_group(j)
            for b in range(B):
                for j in range(GB):
                    if b + 1 < B:
                        context_group(GB * (b + 1) + j)
                    if j >= 2:
                        exps(b, j - 2)
                    keys_values(GB * b + j)
                probs_out(b)
                context_out(b)
            act.wait_ge(cols_mm, 1)
            nc.scalar.copy(b1_cols[:], ps[:, 1, 0:BR0 + BR1]).then_inc(cols_ready, 1)
            norm_scalar(act, 1)
            for i in range(PAIRS):
                act.wait_ge(q0_mm, i + 1)
                nc.scalar.copy(q0_t[:, i, :], ps[:, i % 2, :]).then_inc(q0_ready, 1)
            def probs1_out(b):
                for j in range(4):
                    act.wait_ge(p1_trans, 4 * b + j + 1)
                    nc.scalar.copy(probs1_t[b % 2][:, j * BANK:(j + 1) * BANK], ps[:, 4 + j % 2, :])\
                      .then_inc(p1_ready, 1)

            for b in range(B):
                if b >= 1:
                    probs1_out(b - 1)
                act.wait_ge(s1_max, 2 * b + 2)
                if b >= 2:
                    act.wait_ge(p1_trans, 4 * (b - 1))
                for h in range(HEADS):
                    ex = nc.scalar.activation(probs1[b % 2][:, h, :], ps[:, h // 4, (h % 4) * S:(h % 4 + 1) * S],
                                              ACT.Exp, bias=nmax1[:, b, h:h + 1], scale=SCALE0,
                                              accum_out=sum1[:, b, h:h + 1])
                ex.then_inc(s1_exp, 1)
            probs1_out(B - 1)

            act.wait_ge(s1_mm, B)
            nc.scalar.activation(k_square, k_parts[:, 0, :], ACT.Square).then_inc(ksq_ready, 1)

            norm_scalar(act, 2)

            def relu(i):
                act.wait_ge(h0_mm, i + 1)
                nc.scalar.activation(h0_t[:, i, :], ps[:, 1 + i % 3, :], ACT.Relu, bias=b1_cols[:, i:i + 1])\
                  .then_inc(h0_relu, 1)

            for i in range(3):
                relu(i)
            act.wait_ge(gate_step, 1)
            for b in range(B):
                ex = nc.scalar.activation(gate_e[:, b, :], logits0[:, b, 0:E0], ACT.Exp, bias=ntop0[:, b:b + 1],
                                          accum_out=gate_sum[:, b:b + 1])
            ex.then_inc(gate_exp, 1)
            act.wait_ge(lam_step, 2)
            nc.scalar.activation(lam_exp, lam_sum, ACT.Exp).then_inc(lam_step, 1)
            for i in range(3, 6):
                relu(i)
            act.wait_ge(g0_trans, 1)
            nc.scalar.copy(gates0_t, ps[0:E0, 7, :]).then_inc(g0_ready, 1)
            for i in range(6, E0 * HC0):
                relu(i)
            norm_scalar(act, 3)
            act.wait_ge(q1_mm, 1)
            nc.scalar.copy(q_parts[:, 0, :], ps[:, 0, :]).then_inc(q1_part, 1)
            nc.scalar.activation(aux_t[:], ps[:, 0, :], ACT.Square).then_inc(q1_square, 1)
            with act.Fori(0, B) as b:
                for g in range(HG):
                    for k, (c, n) in enumerate(UNITS[g]):
                        u = UNIT0[g] + k
                        act.wait_ge(scores_mm, b * NU + (u + 1))
                        if c % 4 == 0:
                            act.wait_ge(pv_done, b * (HG * QUADS) + (QUADS * (g + 1) + c // 4 + 1))
                        bank = UNIT * (u % NBUF)
                        half = probs_d[c // 8]
                        nc.scalar.activation(half[:, (c % 8) * BANK:(c % 8 + n) * BANK],
                                             ps[:, bank:bank + n, :].rearrange("p k c -> p (k c)"),
                                             ACT.Exp, scale=SCALE1).then_inc(exp_done, 1)
            norm_scalar(act, 4)
            act.wait_ge(wg_trans, 1)
            nc.scalar.copy(wg_t, ps[:, 7, 0:E1]).then_inc(wg_ready, 1)
            for b in range(B + 1):
                if b < B:
                    act.wait_ge(lin_in, b + 1)
                    nc.scalar.activation(qk_low[:, b, :], qk1[:, b, :], ACT.Exp).then_inc(lin_exp, 1)
                if b >= 1:
                    act.wait_ge(lin_elu, b)
                    nc.scalar.activation(qk_sq[:, b - 1, :], qk1[:, b - 1, :], ACT.Square).then_inc(lin_sq, 1)
            act.wait_ge(lin_norm, B)
            nc.scalar.activation(qk_root, qk_norm, ACT.Sqrt).then_inc(lin_root, 1)
            act.wait_ge(qn_trans, 1)
            nc.scalar.copy(qn_t, ps[:, 5, :]).then_inc(qn_ready, 1)
            act.wait_ge(lc_mm, 1)
            nc.scalar.copy(lin_t, ps[:, 6, :]).then_inc(lc_ready, 1)
            act.wait_ge(a1_trans, 1)
            nc.scalar.copy(attn1_t, ps[:, 5, :]).then_inc(a1_ready, 1)
            for k in range(FC):
                act.wait_ge(f1_mm, k + 1)
                nc.scalar.activation(h1_t[:, k, :], ps[:, k, :], ACT.Gelu, bias=b1_cols[:, BR0 + k:BR0 + k + 1])\
                  .then_inc(f1_ready, 1)

            norm_scalar(act, 5)
            act.wait_ge(g1_step, 2)
            for b in range(B):
                ex = nc.scalar.activation(gate1[:, b, :], logits1[:, b, :], ACT.Exp, bias=ntop1[:, b:b + 1])
            ex.then_inc(g1_exp, 1)
            for m in range(EC + 1):
                rows = P if m < EC else NS * I1
                act.wait_ge(gu_mm, m + 1)
                if m >= 2:
                    act.wait_ge(hid_step, m - 1)
                nc.scalar.activation(silu[m % 2][0:rows, :], ps[0:rows, 2 + 3 * (m % 2), :], ACT.Silu)\
                  .then_inc(silu_ready, 1)
                if m == 1:
                    act.wait_ge(g1_trans, 1)
                    nc.scalar.copy(gate1_t, ps[0:3 * E1, 1, :]).then_inc(g1_ready, 1)

        @block.vector
        def _(dve):
            dve.wait_ge(x_loaded, 16)
            all_stats(dve, 0, None, 0)
            norm_vector(dve, 0, 1e-5)
            dve.wait_ge(qk_mm, 1)
            nc.vector.tensor_copy(aux_t[:], ps[:, 4, :]).then_inc(qk_ready, 1)

            def keys_left(n):
                dve.wait_ge(k_first, n + 1)
                if n >= 2:
                    dve.wait_ge(k_third, n - 1)
                nc.vector.tensor_tensor(k_left[:, n % 2, :], ps[:, 1 + n % 2, :],
                                        k_parts[:, 0, n * BANK:(n + 1) * BANK], ALU.subtract)\
                  .then_inc(k_left1, 1)

            def mask_half(b, i):
                half = slice(KEYS // 2 * i, KEYS // 2 * (i + 1))
                dve.wait_ge(s0_mm, 2 * b + i + 1)
                dve.wait_ge(s0_fill, b + 1)
                dve.wait_ge(mask_loaded, 16 * (b + 1))
                nc.vector.copy_predicated(scores0[b % 2][:, half], mask_sb[:, half],
                                          ps[:, 4 + 2 * i:6 + 2 * i, :].rearrange("p k c -> p (k c)")).then_inc(s0_masked, 1)

            def max_half(b, i):
                dve.wait_ge(s0_masked, 2 * b + i + 1)
                nc.vector.tensor_reduce(max0[:, b, i:i + 1], scores0[b % 2][:, KEYS // 2 * i:KEYS // 2 * (i + 1)],
                                        AX.X, ALU.max).then_inc(s0_max, 1)

            def max_row(b):
                dve.wait_ge(s0_max, 3 * b + 2)
                nc.vector.tensor_reduce(nmax0[:, b:b + 1], max0[:, b, :], AX.X, ALU.max, negate=True).then_inc(s0_max, 1)

            def add_context(b):
                dve.wait_ge(s0_exp, 2 * b + 2)
                nc.vector.tensor_reduce(rsum0[:, b:b + 1], sum0[:, b, :], AX.X, ALU.add).then_inc(s0_rsum, 1)
                dve.wait_ge(s0_rsum, 2 * b + 1)
                nc.vector.reciprocal(rsum0[:, b:b + 1], rsum0[:, b:b + 1]).then_inc(s0_rsum, 1)
                dve.wait_ge(s0_rsum, 2 * b + 2)
                dve.wait_ge(y0_mm, b + 1)
                nc.vector.scalar_tensor_tensor(x[:, b, :], ps[:, 2, 0:D], rsum0[:, b:b + 1], x[:, b, :],
                                               ALU.mult, ALU.add).then_inc(x_done, 1)

            for b in range(B + 1):
                for j in range(GB if b else 0):
                    if j == 0:
                        if b >= 2:
                            add_context(b - 2)
                        mask_half(b - 1, 0)
                        keys_left(GB * (b - 1) + j)
                        mask_half(b - 1, 1)
                    elif j == 1:
                        max_half(b - 1, 0)
                        keys_left(GB * (b - 1) + j)
                        max_half(b - 1, 1)
                        max_row(b - 1)
                    else:
                        keys_left(GB * (b - 1) + j)
                        if j == 2 and b >= 2:
                            dve.wait_ge(x_done, b - 1)
                            row_stats(dve, 1, b - 2)
            add_context(B - 1)
            dve.wait_ge(x_done, B)
            row_stats(dve, 1, B - 1)
            norm_vector(dve, 1, 1e-5)
            for i in range(PAIRS):
                dve.wait_ge(k0_mm, i + 1)
                nc.vector.tensor_copy(k0_t[:, i, :], ps[:, 2 + i % 2, :]).then_inc(k0_ready, 1)
            dve.wait_ge(x_done, B)
            nc.vector.tensor_reduce(of_half, ident[:].rearrange("p (h c) -> p h c", c=4), AX.X, ALU.add)
            nc.vector.tensor_reduce(of_half_h, ident[:].rearrange("p (h c) -> p h c", c=4), AX.X, ALU.max)
            nc.vector.tensor_reduce(of_j, ident[:].rearrange("p (a j c) -> p j a c", j=4, c=4), AX.XY, ALU.add)
            nc.vector.tensor_reduce(of_j12, ident[:, 0:12].rearrange("p (a j) -> p j a", j=4), AX.X, ALU.add)\
              .then_inc(consts_d, 1)
            dve.wait_ge(rows_loaded, ROW_LOADS)
            nc.vector.tensor_tensor(lam_prod, lam_load[:, 0:4:2, :], lam_load[:, 1:4:2, :], ALU.mult).then_inc(lam_step, 1)
            dve.wait_ge(lam_step, 1)
            nc.vector.tensor_reduce(lam_sum, lam_prod, AX.X, ALU.add).then_inc(lam_step, 1)

            def max_heads(b):
                dve.wait_ge(s1_mm, b + 1)
                nc.vector.tensor_reduce(max1[:, b, :], ps[:, 0:4, :].rearrange("p k (h c) -> p (k h) c", c=S),
                                        AX.X, ALU.max).then_inc(s1_max, 1)
                dve.wait_ge(s1_max, 2 * b + 1)
                nc.vector.tensor_scalar_mul(nmax1[:, b, :], max1[:, b, :], -SCALE0).then_inc(s1_max, 1)

            def normalise(b):
                dve.wait_ge(s1_exp, b + 1)
                nc.vector.reciprocal(rsum1[:, b, :], sum1[:, b, :]).then_inc(s1_norm, 1)
                dve.wait_ge(s1_norm, 2 * b + 1)
                nc.vector.tensor_tensor(probs1[b % 2], probs1[b % 2],
                                        rsum1[:, b, :].unsqueeze(2).to_broadcast([P, HEADS, S]), ALU.mult)\
                  .then_inc(s1_norm, 1)

            def heads_out(b):
                dve.wait_ge(h1_mm, b + 1)
                nc.vector.tensor_copy(heads_t[:, :, b * S:(b + 1) * S],
                                      ps[:, 6:8, :].rearrange("p k (i c) -> p (k i) c", c=S)).then_inc(h1_ready, 1)

            max_heads(0)
            for b in range(B):
                for i in range(2):
                    dve.wait_ge(v0_mm, 2 * b + i + 1)
                    nc.vector.tensor_copy(v0[:, b, BANK * i:BANK * (i + 1)], ps[:, 4 + i, :]).then_inc(v0_ready, 1)
            def add_heads(b):
                dve.wait_ge(y1_mm, b + 1)
                nc.vector.tensor_tensor(x[:, b, :], x[:, b, :], ps[:, 4, 0:D], ALU.add).then_inc(x_done, 1)

            for b in range(B):
                if b >= 1:
                    add_heads(b - 1)
                normalise(b)
                if b + 1 < B:
                    max_heads(b + 1)
                if b >= 1:
                    dve.wait_ge(x_done, B + b)
                    row_stats(dve, 2, b - 1)
                heads_out(b)
            add_heads(B - 1)

            dve.wait_ge(x_done, 2 * B)
            row_stats(dve, 2, B - 1)
            norm_vector(dve, 2, 1e-5)
            dve.wait_ge(consts, 2)
            dve.wait_ge(lg0_mm, 1)
            nc.vector.tensor_tensor(logits0[:, :, 0:E0], ps[:, 0, 0:B * E0].rearrange("p (b e) -> p b e", b=B),
                                    gate_b[:].unsqueeze(1).to_broadcast([P, B, E0]), ALU.add)\
              .then_inc(picks0_step, 1)

            dve.wait_ge(picks0_step, 1)
            for b in range(B):
                mx = nc.vector.max(top0[:, b, :], logits0[:, b, 0:E0])
            mx.then_inc(picks0_step, 1)
            dve.wait_ge(picks0_step, 2)
            nc.vector.tensor_scalar_mul(ntop0[:], top0[:, :, 0], -1.0).then_inc(gate_step, 1)
            nc.vector.tensor_copy(picks0[:, :, 0:2], top0[:, :, 0:2]).then_inc(picks0_step, 1)
            dve.wait_ge(picks0_step, 3)
            for b in range(B):
                mr = nc.vector.match_replace(struck0[:, b, :], picks0[:, b, :], logits0[:, b, :], NEVER)
            mr.then_inc(picks0_step, 1)
            dve.wait_ge(picks0_step, 4)
            nc.vector.tensor_tensor(gates0[:], struck0[:, :, 0:E0], logits0[:, :, 0:E0], ALU.not_equal)\
              .then_inc(gate_step, 1)
            dve.wait_ge(gate_exp, 1)
            nc.vector.reciprocal(gate_r[:], gate_sum[:]).then_inc(gate_step, 1)
            dve.wait_ge(gate_step, 3)
            nc.vector.tensor_tensor(gate_e[:], gate_e[:], gates0[:], ALU.mult).then_inc(gate_step, 1)
            dve.wait_ge(gate_step, 4)
            nc.vector.tensor_tensor(gates0[:], gate_e[:], gate_r[:].unsqueeze(2).to_broadcast([P, B, E0]), ALU.mult)\
              .then_inc(gate_step, 1)
            dve.wait_ge(gate_step, 5)
            dve.wait_ge(b2_mm, 1)
            for b in range(B):
                nc.vector.tensor_tensor(x[:, b, :], x[:, b, :], ps[:, 7, b * D:(b + 1) * D], ALU.add).then_inc(x_moe, 1)
            def largest_norm(n):
                dve.wait_ge(kn_mm, n + 1)
                nc.vector.tensor_reduce(k_norms[:, n:n + 1], ps[0:HH, 6 * (n % 2), :], AX.X, ALU.max).then_inc(kn_max, 1)

            for e in range(E0):
                for n in range(3 * e, min(3 * e + 2, GROUPS)):
                    largest_norm(n)
                dve.wait_ge(e0_mm, e + 1)
                for b in range(B):
                    dve.wait_ge(x_moe, B * e + b + 1)
                    nc.vector.scalar_tensor_tensor(x[:, b, :], ps[:, 4 + e % 2, b * D:(b + 1) * D],
                                                   gates0[:, b, e:e + 1], x[:, b, :], ALU.mult, ALU.add)\
                      .then_inc(x_moe, 1)
                if 3 * e + 2 < GROUPS:
                    largest_norm(3 * e + 2)
                if e == E0 - 2:
                    dve.wait_ge(kn_max, GROUPS)
                    nc.vector.reduce_max(k_norm, k_norms, AX.X).then_inc(bound_step, 1)
                    dve.wait_ge(lam_step, 3)
                    nc.vector.scalar_tensor_tensor(neg_lam, lam_exp[:, 0:1], -1.0, lam_exp[:, 1:2], ALU.mult, ALU.add)\
                      .then_inc(lam_step, 1)
                    dve.wait_ge(lam_step, 4)
                    nc.vector.tensor_scalar_add(neg_lam, neg_lam, -0.8).then_inc(lam_step, 1)
            all_stats(dve, 3, x_moe, B * E0)
            norm_vector(dve, 3, 1e-5)
            nc.vector.memset(wide[KROWS:ROWS, 8192:12288], 0.0).then_inc(q_rows_zero, 1)
            def mask_queries(i):
                for j in range(4):
                    nc.vector.tensor_scalar(q_masked[:, i, :, j, :], q_parts[:, i, :].rearrange("p (b c) -> p b c", b=B),
                                            of_j[:, j:j + 1], None, ALU.mult).then_inc(q_masked_ready, 1)

            dve.wait_ge(q1_part, 1)
            mask_queries(0)
            dve.wait_ge(q1_square, 1)
            dve.wait_ge(ln_trans, 4)
            left = xn[:].rearrange("p b f -> p (b f)")
            nc.vector.tensor_tensor(left, ps[:, 0, :], q_parts[:, 0, :], ALU.subtract).then_inc(q1_left, 1)
            dve.wait_ge(q1_left, 1)
            nc.vector.tensor_copy(q_parts[:, 1, :], left).then_inc(q1_left, 1)
            dve.wait_ge(q1_left, 2)
            mask_queries(1)
            nc.vector.tensor_tensor(q_parts[:, 2, :], left, q_parts[:, 1, :], ALU.subtract).then_inc(q1_left, 1)
            dve.wait_ge(q1_left, 3)
            mask_queries(2)
            dve.wait_ge(qn_mm, 1)
            nc.vector.reduce_max(q_norm, ps[0:HH, 1, :], AX.X).then_inc(bound_step, 1)
            dve.wait_ge(bound_step, 2)
            nc.vector.tensor_tensor(bound_h, q_norm, k_norm, ALU.mult).then_inc(bound_step, 1)
            dve.wait_ge(bound_trans, 1)
            nc.vector.reduce_max(bound, ps[0:1, 2, 0:HH], AX.X).then_inc(bound_step, 1)
            dve.wait_ge(bound_step, 4)
            nc.vector.tensor_scalar(safe, bound, (LIMIT / SCALE1) ** 2 / 1.02, None, ALU.is_le).then_inc(safe_ready, 1)

            dve.wait_ge(safe_ready, 1)
            is_safe = dve.value_load(safe)
            with dve.If(is_safe < 1):
                with dve.Fori(0, B) as b:
                    for h in range(HH):
                        dve.wait_ge(shift_mm, b * HH + (h + 1 + 4 * SLOTS))
                        nc.vector.tensor_reduce(shift_max[:, bass.ds(b * HH + h, 1)],
                                                ps[:, 4 * (h % 2):4 * (h % 2) + 4, :].rearrange("p k c -> p (k c)"),
                                                AX.X, ALU.max, negate=True).then_inc(shift_maxed, 1)
                dve.wait_ge(shift_maxed, B * HH + 2)
                m_v = shift_max.rearrange("p (i j) -> p i j", j=4)
                l_v = shift_left.rearrange("p (i j) -> p i j", j=4)
                nc.vector.tensor_copy(shift_parts[:, :, 0, :], m_v).then_inc(shift_step, 1)
                dve.wait_ge(shift_step, 1)
                nc.vector.tensor_tensor(l_v, m_v, shift_parts[:, :, 0, :], ALU.subtract).then_inc(shift_step, 1)
                dve.wait_ge(shift_step, 2)
                nc.vector.tensor_copy(shift_parts[:, :, 1, :], l_v).then_inc(shift_step, 1)
                dve.wait_ge(shift_step, 3)
                nc.vector.tensor_tensor(shift_parts[:, :, 2, :], l_v, shift_parts[:, :, 1, :], ALU.subtract)\
                  .then_inc(shift_step, 1)
                dve.wait_ge(stage_set, 4)
                for n in range(ITEMS):
                    dve.wait_ge(shift_trans, n + 1)
                    nc.vector.tensor_tensor(
                        q_rows[KROWS:ROWS, n * BANK:(n + 1) * BANK].rearrange("p (j c) -> p j c", j=4),
                        ps[0:12, n % 2, 0:S].unsqueeze(1).to_broadcast([12, 4, S]),
                        of_j12[0:12, :].unsqueeze(2).to_broadcast([12, 4, S]), ALU.mult).then_inc(shift_rows, 1)

            with dve.Fori(0, B) as b:
                for g in range(HG):
                    dve.wait_ge(pv_done, b * (HG * QUADS) + QUADS * (g + 3))
                    acc = acc_sb[32 * (g % GI):32 * (g % GI + 1), g // GI, :]
                    for n in range(4):
                        tile_n = ps[32 * n:32 * (n + 1), 6 + g % 2, :]
                        if n == 0:
                            nc.vector.tensor_copy(acc, tile_n).then_inc(acc_added, 1)
                        else:
                            dve.wait_ge(acc_added, b * (HG * 4) + (4 * (g + 2) + n))
                            nc.vector.tensor_tensor(acc, acc, tile_n, ALU.add).then_inc(acc_added, 1)
                    if g % GI == GI - 1:
                        dve.wait_ge(fold_mm, b * (HG // GI) + (g // GI + 1))
                        nc.vector.tensor_copy(heads_d[:, bass.ds(b * HH + 4 * GI * (g // GI), 4 * GI), :],
                                              ps[:, 7, 0:4 * GI * VCOLS].rearrange("p (h v) -> p h v", v=VCOLS))\
                          .then_inc(folded, 1)
                dve.wait_ge(folded, b * (HG // GI) + (HG // GI + 1))
                heads_b = heads_d[:, bass.ds(b * HH, HH), :]
                den_b = den_r[:, bass.ds(b * HH, HH)]
                nc.vector.reciprocal(den_b, heads_b[:, :, 8]).then_inc(comb_step, 1)
                dve.wait_ge(comb_step, b * 3 + 1)
                nc.vector.tensor_tensor(heads_b[:, :, 0:8], heads_b[:, :, 0:8],
                                        den_b.unsqueeze(2).to_broadcast([P, HH, 8]), ALU.mult).then_inc(comb_step, 1)
                dve.wait_ge(comb_step, b * 3 + 2)
                x_b = x[:, bass.ds(b, 1), :].rearrange("p a (h v) -> p (a h) v", v=8)
                by_half = heads_b[:, :, 0:8].rearrange("p (h i) v -> p h i v", i=2)
                nc.vector.scalar_tensor_tensor(x_b, by_half[:, :, 1, :], neg_lam, x_b, ALU.mult, ALU.add)\
                  .then_inc(comb_step, 1)
                dve.wait_ge(comb_step, b * 3 + 3)
                nc.vector.tensor_tensor(x_b, by_half[:, :, 0, :], x_b, ALU.add).then_inc(x_diff, 1)

            all_stats(dve, 4, x_diff, 0)
            norm_vector(dve, 4, 1e-5)
            nc.vector.tensor_reduce(of_eight, ident[:].rearrange("p (h c) -> p h c", c=DH1), AX.X, ALU.add)\
              .then_inc(kv_ready, 1)
            dve.wait_ge(kv_ready, 1)
            nc.vector.tensor_scalar_mul(of_eight, of_eight, DH1 ** -0.5).then_inc(kv_ready, 1)
            dve.wait_ge(lin_loaded, LIN_LOADS)
            dve.wait_ge(ln_xn, B * 5)
            nc.vector.tensor_tensor(res1, xn[:], b_out1.unsqueeze(1).to_broadcast([P, B, D]), ALU.add).then_inc(lin_own, 1)

            def elu(b):
                dve.wait_ge(lin_exp, b + 1)
                nc.vector.tensor_scalar(qk_low[:, b, :], qk_low[:, b, :], 1.0, -1.0, ALU.min, ALU.add).then_inc(lin_own, 1)
                dve.wait_ge(lin_own, b + 2)
                nc.vector.scalar_tensor_tensor(qk1[:, b, :], qk1[:, b, :], 0.0, qk_low[:, b, :], ALU.max, ALU.add)\
                  .then_inc(lin_elu, 1)

            def norms(b):
                dve.wait_ge(lin_sq, b + 1)
                nc.vector.tensor_reduce(qk_norm[:, 2 * HEADS1 * b:2 * HEADS1 * (b + 1)],
                                        qk_sq[:, b, :].rearrange("p (h c) -> p h c", c=DH1), AX.X, ALU.add)\
                  .then_inc(lin_norm, 1)

            for b in range(B + 2):
                if b < B:
                    dve.wait_ge(lin_mm, b + 1)
                    nc.vector.tensor_tensor(qkv1[:, b, :], ps[:, b, 0:3 * D], b_qkv1, ALU.add).then_inc(lin_in, 1)
                if 1 <= b <= B:
                    elu(b - 1)
                if b >= 2:
                    norms(b - 2)
            dve.wait_ge(lin_root, 1)
            nc.vector.reciprocal(qk_rs, qk_root).then_inc(lin_root, 1)
            dve.wait_ge(lin_root, 2)
            nc.vector.scalar_tensor_tensor(qk_root, qk_rs, -0.5, qk_rs, ALU.mult, ALU.mult).then_inc(lin_root, 1)
            dve.wait_ge(lin_root, 3)
            nc.vector.tensor_tensor(qk_root, qk_root, qk_norm, ALU.mult).then_inc(lin_root, 1)
            dve.wait_ge(lin_root, 4)
            nc.vector.scalar_tensor_tensor(qk_rs, qk_root, 1.5, qk_rs, ALU.add, ALU.mult).then_inc(lin_root, 1)
            dve.wait_ge(lin_root, 5)
            for b in range(B):
                heads = qk1[:, b, :].rearrange("p (h c) -> p h c", c=DH1)
                nc.vector.tensor_tensor(heads, heads, qk_rs[:, 2 * HEADS1 * b:2 * HEADS1 * (b + 1)].unsqueeze(2)
                                        .to_broadcast([P, 2 * HEADS1, DH1]), ALU.mult).then_inc(lin_unit, 1)
            dve.wait_ge(kv_mm, 1)
            dve.wait_ge(kv_ready, 2)
            nc.vector.tensor_tensor(kv_diag.rearrange("p b (h c) -> p b h c", c=DH1),
                                    ps[:, 4, :].rearrange("p (b h c) -> p b h c", b=B, c=DH1),
                                    of_eight.unsqueeze(1).unsqueeze(3).to_broadcast([P, B, HEADS1, DH1]), ALU.mult)\
              .then_inc(kv_ready, 1)
            dve.wait_ge(lo_mm, 1)
            nc.vector.tensor_tensor(res1, res1, ps[:, 7, :].rearrange("p (b n) -> p b n", b=B), ALU.add).then_inc(lin_own, 1)
            dve.wait_ge(lin_own, 6)
            all_stats(dve, 5, None, 0, res1)
            affine_norm_vector(dve, 5, 1e-12, res1, attn1, 0)
            dve.wait_ge(ln_xn, B * 6)
            nc.vector.tensor_tensor(f2_sum, attn1, b2_1.unsqueeze(1).to_broadcast([P, B, D]), ALU.add).then_inc(lin_own, 1)
            dve.wait_ge(lin_own, 7)
            dve.wait_ge(f2_mm, 1)
            nc.vector.tensor_tensor(f2_sum, f2_sum, ps[:, 4, :].rearrange("p (b n) -> p b n", b=B), ALU.add)\
              .then_inc(lin_own, 1)
            dve.wait_ge(lin_own, 8)
            all_stats(dve, 6, None, 0, f2_sum)
            affine_norm_vector(dve, 6, 1e-12, f2_sum, res1, 2)
            for b in range(B):
                dve.wait_ge(ln_xn, B * 6 + b + 1)
                nc.vector.tensor_tensor(x[:, b, :], x[:, b, :], res1[:, b, :], ALU.add).then_inc(x_lin, 1)

            all_stats(dve, 7, x_lin, 0)
            norm_vector(dve, 7, 1e-5)
            for i in range(3):
                rows = slice(E1 * i, E1 * (i + 1))
                sp1 = nc.vector.tensor_copy(spread[rows, :].rearrange("p (e i) -> p e i", i=I1),
                                            ident[rows, rows].unsqueeze(2).to_broadcast([E1, E1, I1]))
            sp1.then_inc(kv_ready, 1)
            dve.wait_ge(lg1_mm, 1)
            nc.vector.tensor_copy(logits1, ps[:, 0, 0:B * E1].rearrange("p (b e) -> p b e", b=B)).then_inc(g1_step, 1)
            dve.wait_ge(g1_step, 1)
            for b in range(B):
                mx = nc.vector.max(top1[:, b, :], logits1[:, b, :])
            mx.then_inc(top1_ready, 1)
            dve.wait_ge(top1_ready, 1)
            nc.vector.tensor_scalar_mul(ntop1, top1[:, :, 0], -1.0).then_inc(g1_step, 1)
            for b in range(B):
                mr = nc.vector.match_replace(struck1[:, b, :], top1[:, b, :], logits1[:, b, :], NEVER)
            mr.then_inc(g1_step, 1)
            dve.wait_ge(g1_step, 3)
            nc.vector.tensor_tensor(struck1, struck1, logits1, ALU.not_equal).then_inc(g1_step, 1)
            dve.wait_ge(g1_step, 4)
            dve.wait_ge(g1_exp, 1)
            nc.vector.tensor_tensor(gate1, gate1, struck1, ALU.mult).then_inc(g1_step, 1)
            dve.wait_ge(g1_step, 5)
            nc.vector.tensor_reduce(gsum1, gate1, AX.X, ALU.add).then_inc(g1_step, 1)
            dve.wait_ge(g1_step, 6)
            nc.vector.reciprocal(grec1, gsum1).then_inc(g1_step, 1)
            dve.wait_ge(g1_step, 7)
            nc.vector.tensor_tensor(gate1, gate1, grec1.unsqueeze(2).to_broadcast([P, B, E1]), ALU.mult).then_inc(g1_step, 1)
            dve.wait_ge(g1_step, 8)
            nc.vector.tensor_copy(gate1_parts[:, :, 0, :], gate1).then_inc(g1_step, 1)
            dve.wait_ge(g1_step, 9)
            nc.vector.tensor_tensor(gate1_left, gate1, gate1_parts[:, :, 0, :], ALU.subtract).then_inc(g1_step, 1)
            dve.wait_ge(g1_step, 10)
            nc.vector.tensor_copy(gate1_parts[:, :, 1, :], gate1_left).then_inc(g1_step, 1)
            dve.wait_ge(g1_step, 11)
            nc.vector.tensor_tensor(gate1_parts[:, :, 2, :], gate1_left, gate1_parts[:, :, 1, :], ALU.subtract)\
              .then_inc(g1_step, 1)
            def silu_times_up(m):
                dve.wait_ge(silu_ready, m + 1)
                nc.vector.tensor_tensor(silu[m % 2], silu[m % 2], ps[:, 3 + 3 * (m % 2), :], ALU.mult).then_inc(hid_half, 1)

            silu_times_up(0)
            for m in range(EC):
                if m == 0:
                    silu_times_up(1)
                elif m >= 2:
                    silu_times_up(m)
                dve.wait_ge(hid_half, m + 1)
                dve.wait_ge(wt_mm, m + 1)
                nc.vector.tensor_tensor(hid1_t[:, m * T:(m + 1) * T], silu[m % 2], ps[:, 4 + 3 * (m % 2), :], ALU.mult)\
                  .then_inc(hid_step, 1)
            rows = NS * I1
            dve.wait_ge(silu_ready, EC + 1)
            nc.vector.scalar_tensor_tensor(hid1_t[0:rows, EC * T:(EC + 1) * T], silu[EC % 2][0:rows, :], 1.0 / NS,
                                           ps[0:rows, 3 + 3 * (EC % 2), :], ALU.mult, ALU.mult).then_inc(hid_step, 1)
            for b in range(B):
                dve.wait_ge(down_mm, b + 1)
                nc.vector.tensor_tensor(x[:, b, :], x[:, b, :], ps[:, b, 0:D], ALU.add).then_inc(x_final, 1)

        @block.tensor
        def _(pe):
            pe.wait_ge(ident_ready, 2)
            keep_warm(9, 0)
            pe.wait_ge(raw_loaded, 96)
            nc.tensor.matmul(ps[:, 0, 0:D], raw_w[:, 0, :], raw_w[:, 1, :], start=True, stop=True)
            for i in range(3):
                nc.tensor.transpose(ps[:, 0, (i + 1) * D:(i + 2) * D], raw_w[:, 2 + i, :] if i == 0 else
                                    raw_w[:, 2 + i, :], ident[:])
            nc.tensor.transpose(ps[:, 1, 0:D], raw_w[:, 5, :], ident[:]).then_inc(small_mm, 1)
            norm_tensor(pe, 0)
            pe.wait_ge(small_ready, 2)
            pe.wait_ge(ln_done, 1)
            nc.tensor.matmul(ps[:, 4, :], wqk0, xn_t[:], start=True, stop=True).then_inc(qk_mm, 1)

            def transpose_group(n):
                if n % GB == 0:
                    pe.wait_ge(ctx_loaded[n // GB], 16)
                if n >= GB:
                    pe.wait_ge(ct_ready, n)
                elif n >= 2:
                    pe.wait_ge(ct_ready, n - 1)
                for c in range(4):
                    tr = nc.tensor.transpose(ps[:, ct_bank(n), c * P:(c + 1) * P], ctx_sb[:, 4 * n + c, :], ident[:])
                tr.then_inc(ct_trans, 1)

            def project_group(n):
                pe.wait_ge(ct_ready, n + 1)
                if n >= 2:
                    pe.wait_ge(k_left1, n - 1)
                if n >= GB and n % GB == 0:
                    pe.wait_ge(x_done, n // GB)
                nc.tensor.matmul(ps[:, 1 + n % 2, :], wk1_t, ctx_t[:, n * BANK:(n + 1) * BANK], start=True, stop=True)\
                  .then_inc(k_mm, 1)
                if n >= 1:
                    pe.wait_ge(v_ready, n)
                for c in range(4):
                    mm = nc.tensor.matmul(ps[:, 3, c * P:(c + 1) * P], ctx_t[:, (4 * n + c) * P:(4 * n + c + 1) * P],
                                          wv1_t, start=True, stop=True)
                mm.then_inc(v_mm, 1)

            def scores(b):
                pe.wait_ge(ct_ready, GB * (b + 1))
                for j in range(GB):
                    if b >= 1:
                        pe.wait_ge(p0_ready, 4 * (b - 1) + j + 1)
                    key0 = (GB * b + j) * BANK
                    mm = nc.tensor.matmul(ps[:, 4 + j, :], aux_t[:, b * S:(b + 1) * S], ctx_t[:, key0:key0 + BANK],
                                          start=True, stop=True)
                    if j % 2 == 1:
                        mm.then_inc(s0_mm, 1)

            def transpose_probs(b):
                for j in range(4):
                    pe.wait_ge(s0_exp, 2 * b + 1 + j // 2)
                    for c in range(4 * j, 4 * j + 4):
                        tr = nc.tensor.transpose(ps[:, 4 + j, (c % 4) * S:(c % 4 + 1) * S],
                                                 scores0[b % 2][:, c * P:(c + 1) * P], ident[:])
                    tr.then_inc(p0_trans, 1)

            def attend(b):
                pe.wait_ge(p0_ready, 4 * (b + 1))
                pe.wait_ge(v_ready, GB * (b + 1))
                for c in range(KC):
                    mm = nc.tensor.matmul(ps[:, 3, 0:S], ctx_sb[:, b * KC + c, :], probs0_t[:, c, :],
                                          start=(c == 0), stop=(c == KC - 1))
                mm.then_inc(o1_mm, 1)
                pe.wait_ge(o1_ready, b + 1)
                pe.wait_ge(k_left1, GB * (b + 1))
                nc.tensor.matmul(ps[:, 2, 0:D], o1_t, wv0_t, start=True, stop=True).then_inc(y0_mm, 1)

            pe.wait_ge(qk_ready, 1)
            for b in range(B + 1):
                for j in range(GB):
                    if b < B:
                        transpose_group(GB * b + j)
                    if b >= 1:
                        project_group(GB * (b - 1) + j)
                if b >= 1:
                    transpose_probs(b - 1)
                if b < B:
                    scores(b)
                if b >= 1:
                    attend(b - 1)
            pe.wait_ge(rows_loaded, ROW_LOADS)
            nc.tensor.transpose(ps[:, 1, 0:BR0 + BR1], b1_rows[:], ident[0:BR0 + BR1, 0:BR0 + BR1]).then_inc(cols_mm, 1)
            keep_warm(14, 0)
            norm_tensor(pe, 1)
            pe.wait_ge(qkv0_loaded, 16)
            pe.wait_ge(cols_ready, 1)
            pe.wait_ge(ln_done, 2)
            for i in range(PAIRS):
                if i >= 2:
                    pe.wait_ge(q0_ready, i - 1)
                nc.tensor.matmul(ps[:, i % 2, :], w_qkv[:, 0, 2 * DH * i:2 * DH * (i + 1)], xn_t[:],
                                 start=True, stop=True).then_inc(q0_mm, 1)
                if i >= 2:
                    pe.wait_ge(k0_ready, i - 1)
                nc.tensor.matmul(ps[:, 2 + i % 2, :], w_qkv[:, 1, 2 * DH * i:2 * DH * (i + 1)], xn_t[:],
                                 start=True, stop=True).then_inc(k0_mm, 1)

            def scores_heads(b):
                for i in range(PAIRS):
                    for odd in range(2):
                        rows = slice(DH * odd, DH * (odd + 1))
                        mm = nc.tensor.matmul(ps[:, 2 * odd + i // 4, (i % 4) * S:(i % 4 + 1) * S],
                                              q0_t[rows, i, b * S:(b + 1) * S], k0_t[rows, i, b * S:(b + 1) * S],
                                              start=True, stop=True)
                mm.then_inc(s1_mm, 1)

            pe.wait_ge(q0_ready, PAIRS)
            pe.wait_ge(k0_ready, PAIRS)
            scores_heads(0)
            for b in range(B):
                if b >= 1:
                    pe.wait_ge(v0_ready, 2 * b - 1)
                nc.tensor.matmul(ps[:, 4, :], xn_t[:, b * S:(b + 1) * S], w_qkv[:, 2, 0:BANK],
                                 start=True, stop=True).then_inc(v0_mm, 1)
                if b >= 1:
                    pe.wait_ge(v0_ready, 2 * b)
                nc.tensor.matmul(ps[:, 5, :], xn_t[:, b * S:(b + 1) * S], w_qkv[:, 2, BANK:2 * BANK],
                                 start=True, stop=True).then_inc(v0_mm, 1)
            pe.wait_ge(v0_ready, 2 * B)
            def project_heads(b):
                pe.wait_ge(attn0_loaded, 32)
                pe.wait_ge(h1_ready, b + 1)
                for i in range(PAIRS):
                    mm = nc.tensor.matmul(ps[:, 4, 0:D], heads_t[:, i, b * S:(b + 1) * S], w_out0[:, i, :],
                                          start=(i == 0), stop=(i == PAIRS - 1))
                mm.then_inc(y1_mm, 1)

            for b in range(B):
                if b >= 1:
                    project_heads(b - 1)
                if b + 1 < B:
                    pe.wait_ge(s1_exp, b + 1)
                    scores_heads(b + 1)
                if b == B - 1:
                    keep_warm(8, 5)
                pe.wait_ge(s1_norm, 2 * b + 2)
                if b >= 1:
                    pe.wait_ge(x_done, B + b)
                for j in range(4):
                    n = 4 * b + j
                    if n >= 2:
                        pe.wait_ge(p1_ready, n - 1)
                    for c in range(4):
                        tr = nc.tensor.transpose(ps[:, 4 + j % 2, c * S:(c + 1) * S], probs1[b % 2][:, 4 * j + c, :],
                                                 ident[:])
                    tr.then_inc(p1_trans, 1)
                pe.wait_ge(p1_ready, 4 * (b + 1))
                if b >= 1:
                    pe.wait_ge(h1_ready, b)
                for i in range(PAIRS):
                    for odd in range(2):
                        at = (PAIRS * odd + i) * S
                        head = 2 * i + odd
                        mm = nc.tensor.matmul(ps[DH * odd:DH * (odd + 1), 6 + i // 4, (i % 4) * S:(i % 4 + 1) * S],
                                              v0[:, b, head * DH:(head + 1) * DH], probs1_t[b % 2][:, at:at + S],
                                              start=True, stop=True)
                mm.then_inc(h1_mm, 1)
            project_heads(B - 1)

            keep_warm(14, 0)
            norm_tensor(pe, 2)
            pe.wait_ge(ln_done, 3)
            for b in range(B):
                mm = nc.tensor.matmul(ps[:, 0, b * E0:(b + 1) * E0], xn_t[:, b * S:(b + 1) * S], gate_w[:],
                                      start=True, stop=True)
            mm.then_inc(lg0_mm, 1)
            pe.wait_ge(ffn0_loaded, 32)

            def hidden(i):
                if i >= 3:
                    pe.wait_ge(h0_relu, i - 2)
                nc.tensor.matmul(ps[:, 1 + i % 3, :], w1_0[:, i // HC0, i % HC0, :], xn_t[:], start=True, stop=True)\
                  .then_inc(h0_mm, 1)

            def expert(e):
                pe.wait_ge(h0_relu, HC0 * (e + 1))
                if e >= 2:
                    pe.wait_ge(x_moe, B * e)
                for b in range(B):
                    for k in range(HC0):
                        mm = nc.tensor.matmul(ps[:, 4 + e % 2, b * D:(b + 1) * D], h0_t[:, HC0 * e + k, b * S:(b + 1) * S],
                                              w2_0[:, e, k, :], start=(k == 0), stop=(k == HC0 - 1))
                mm.then_inc(e0_mm, 1)

            def key_norm(n):
                if n >= 2:
                    pe.wait_ge(kn_max, n - 1)
                nc.tensor.matmul(ps[0:HH, 6 * (n % 2), :], of_half_h, k_square[:, n * BANK:(n + 1) * BANK],
                                 start=True, stop=True).then_inc(kn_mm, 1)

            for i in range(6):
                hidden(i)
            pe.wait_ge(gate_step, 5)
            for b in range(B):
                tr = nc.tensor.transpose(ps[0:E0, 7, b * S:(b + 1) * S], gates0[:, b, :], ident[:])
            tr.then_inc(g0_trans, 1)
            pe.wait_ge(g0_ready, 1)
            for b in range(B):
                mm = nc.tensor.matmul(ps[:, 7, b * D:(b + 1) * D], gates0_t[:, b * S:(b + 1) * S], b2_0[:],
                                      start=True, stop=True)
            mm.then_inc(b2_mm, 1)
            for e in range(E0):
                if e == 0:
                    pe.wait_ge(consts_d, 1)
                    pe.wait_ge(ksq_ready, 1)
                for i in range(2):
                    if 2 * e + i + 6 < E0 * HC0:
                        hidden(2 * e + i + 6)
                    if 3 * e + i < GROUPS:
                        key_norm(3 * e + i)
                expert(e)
                if 3 * e + 2 < GROUPS:
                    key_norm(3 * e + 2)
            pe.wait_ge(kn_max, GROUPS)
            norm_tensor(pe, 3)
            pe.wait_ge(ln_done, 4)
            nc.tensor.matmul(ps[:, 0, :], wq1_t, xn_t[:], start=True, stop=True).then_inc(q1_mm, 1)
            pe.wait_ge(q1_square, 1)
            nc.tensor.matmul(ps[0:HH, 1, :], of_half, aux_t[:], start=True, stop=True).then_inc(qn_mm, 1)
            pe.wait_ge(bound_step, 3)
            nc.tensor.transpose(ps[0:1, 2, 0:HH], bound_h, ident[0:HH, 0:HH]).then_inc(bound_trans, 1)
            pe.wait_ge(stage_set, 4)
            pe.wait_ge(q_rows_zero, 1)
            pe.wait_ge(ring_ones, 1)
            pe.wait_ge(safe_ready, 1)
            is_safe = pe.value_load(safe)
            with pe.If(is_safe < 1):
                pe.sem_inc(shift_maxed, 2)
                pe.sem_inc(shift_mm, 4 * SLOTS)
                for i in range(SLOTS):
                    pe.wait_ge(q_rows_loaded[i], HG // SLOTS * RING_LOADS)
                with pe.Fori(0, B) as b:
                    for g in range(HG):
                        pe.wait_ge(shift_loaded[g % SLOTS], (b * (HG // SLOTS) + (g // SLOTS + 1)) * RING_LOADS)
                        for j in range(4):
                            h = 4 * g + j
                            pe.wait_ge(shift_maxed, b * HH + (h + 1))
                            for n in range(4):
                                mm = nc.tensor.matmul(ps[:, 4 * (h % 2) + n, :],
                                                      q_rows[0:KROWS, bass.ds(b * (HG * BANK) + (g * BANK + j * S), S)],
                                                      key_ring[0:KROWS, g % SLOTS, n * BANK:(n + 1) * BANK],
                                                      start=True, stop=True)
                            mm.then_inc(shift_mm, 1)
                pe.wait_ge(shift_step, 4)
                for n in range(ITEMS):
                    if n >= 2:
                        pe.wait_ge(shift_rows, n - 1)
                    nc.tensor.matmul(ps[0:12, n % 2, 0:S], shift_parts[:, n, :, :].rearrange("p g c -> p (g c)"),
                                     ident_h[:], start=True, stop=True).then_inc(shift_trans, 1)
                pe.wait_ge(shift_rows, ITEMS)
                for i in range(SLOTS):
                    pe.wait_ge(shift_loaded[i], (B * (HG // SLOTS) + 1) * RING_LOADS)

            pe.sem_inc(exp_done, NBUF)
            pe.sem_inc(pv_done, 2 * QUADS)
            pe.sem_inc(acc_added, 2 * 4)
            pe.sem_inc(folded, 1)

            def score_unit(b, u):
                g = max(i for i in range(HG) if UNIT0[i] <= u)
                c, n = UNITS[g][u - UNIT0[g]]
                if c == 0:
                    pe.wait_ge(q_rows_loaded[g % SLOTS], (g // SLOTS + 1) * RING_LOADS)
                    pe.wait_ge(ring_loaded[g % SLOTS], (b * (HG // SLOTS) + (g // SLOTS + 1)) * RING_LOADS)
                pe.wait_ge(exp_done, b * NU + (u + 1))
                for i in range(n):
                    mm = nc.tensor.matmul(ps[:, UNIT * (u % NBUF) + i, :],
                                          key_ring[0:ROWS, g % SLOTS, (c + i) * P:(c + i + 1) * P],
                                          q_rows[0:ROWS, bass.ds(b * (HG * BANK) + g * BANK, BANK)],
                                          start=True, stop=True)
                mm.then_inc(scores_mm, 1)

            def weigh_quad(b, g, w, u):
                if w == 0:
                    pe.wait_ge(acc_added, b * (HG * 4) + 4 * (g + 1))
                    if g % GI == 1:
                        pe.wait_ge(folded, b * (HG // GI) + (g // GI + 1))
                    pe.wait_ge(staged, b * HG + (g + 1))
                pe.wait_ge(exp_done, b * NU + (u + 1 + NBUF))
                for n in range(4):
                    c = 4 * w + n
                    mm = nc.tensor.matmul(ps[32 * n:32 * (n + 1), 6 + g % 2, :], v_stage[:, g % 2, c, :],
                                          probs_d[c // 8][:, (c % 8) * BANK:(c % 8 + 1) * BANK],
                                          start=(w == 0), stop=(w == QUADS - 1))
                mm.then_inc(pv_done, 1)

            def fold_items(b, q):
                pe.wait_ge(acc_added, b * (HG * 4) + 4 * (GI * (q + 1) + 2))
                for j in range(4):
                    mm = nc.tensor.matmul(
                        ps[:, 7, 0:4 * GI * VCOLS].rearrange("p (i j v) -> p i j v", i=GI, j=4)[:, :, j, :],
                        acc_sb[:, q, j * S:(j + 1) * S],
                        ident[:].rearrange("p (i r) -> p i r", i=GI)[:, :, VCOLS * (j // 2):VCOLS * (j // 2 + 1)],
                        start=True, stop=True)
                mm.then_inc(fold_mm, 1)

            def item(b, g, last, fold=None):
                for k, (c, n) in enumerate(UNITS[g]):
                    u = UNIT0[g] + k
                    if u + NBUF < NU:
                        score_unit(b, u + NBUF)
                    elif not last:
                        score_unit(b + 1, u + NBUF - NU)
                    if (c + n) % 4 == 0:
                        weigh_quad(b, g, c // 4, u)
                    if fold and c == 10:
                        fold_items(*fold)

            def later_items(b, last):
                for g in range(1, HG):
                    item(b, g, last, (b, g // GI - 1) if g % GI == 0 else None)

            for u in range(NBUF):
                score_unit(0, u)
            item(0, 0, False)
            with pe.Fori(0, B - 1) as b:
                later_items(b, False)
                item(b + 1, 0, False, (b, 1))
            later_items(B - 1, True)
            fold_items(B - 1, 1)

            pe.wait_ge(lin_loaded, LIN_LOADS)
            pe.wait_ge(folded, ITEMS // GI + 1)
            keep_warm(20, 0)
            norm_tensor(pe, 4)
            nc.tensor.transpose(ps[:, 7, 0:E1], w_gate, ident[0:E1, 0:E1]).then_inc(wg_trans, 1)
            pe.wait_ge(ln_done, 5)
            for b in range(B):
                nc.tensor.matmul(ps[:, b, 0:3 * D], xn_t[:, b * S:(b + 1) * S], w_qkv1, start=True, stop=True)\
                  .then_inc(lin_mm, 1)
            keep_warm(24, 6)
            for b in range(B):
                pe.wait_ge(lin_unit, b + 1)
                tr = nc.tensor.transpose(ps[:, 5, b * S:(b + 1) * S], qk1[:, b, 0:D], ident[:])
                if b == B - 1:
                    tr.then_inc(qn_trans, 1)
                mm = nc.tensor.matmul(ps[:, 4, b * D:(b + 1) * D], qk1[:, b, D:2 * D], v1s[:, b, :], start=True, stop=True)
            mm.then_inc(kv_mm, 1)
            pe.wait_ge(qn_ready, 1)
            pe.wait_ge(kv_ready, 3)
            for b in range(B):
                mm = nc.tensor.matmul(ps[:, 6, b * S:(b + 1) * S], kv_diag[:, b, :], qn_t[:, b * S:(b + 1) * S],
                                      start=True, stop=True)
            mm.then_inc(lc_mm, 1)
            pe.wait_ge(wg_ready, 1)
            pe.wait_ge(lc_ready, 1)
            for b in range(B):
                mm = nc.tensor.matmul(ps[:, 7, b * D:(b + 1) * D], lin_t[:, b * S:(b + 1) * S], w_out1,
                                      start=True, stop=True)
            mm.then_inc(lo_mm, 1)
            keep_warm(8, 6)
            for b in range(B):
                pe.wait_ge(ln_xn, B * 5 + b + 1)
                tr = nc.tensor.transpose(ps[:, 5, b * S:(b + 1) * S], attn1[:, b, :], ident[:])
            tr.then_inc(a1_trans, 1)
            pe.wait_ge(a1_ready, 1)
            for k in range(FC):
                nc.tensor.matmul(ps[:, k, :], w1_1[:, k * P:(k + 1) * P], attn1_t, start=True, stop=True).then_inc(f1_mm, 1)
            for b in range(B):
                for k in range(FC):
                    if b == 0:
                        pe.wait_ge(f1_ready, k + 1)
                    mm = nc.tensor.matmul(ps[:, 4, b * D:(b + 1) * D], h1_t[:, k, b * S:(b + 1) * S], w2_1[:, k, :],
                                          start=(k == 0), stop=(k == FC - 1))
            mm.then_inc(f2_mm, 1)

            keep_warm(30, 5)
            norm_tensor(pe, 7)
            pe.wait_ge(moe1_loaded, 96)
            pe.wait_ge(ln_done, 6)
            for b in range(B):
                mm = nc.tensor.matmul(ps[:, 0, b * E1:(b + 1) * E1], xn_t[:, b * S:(b + 1) * S], wg_t, start=True, stop=True)
            mm.then_inc(lg1_mm, 1)

            def gate_and_up(m):
                rows = P if m < EC else NS * I1
                if m >= 2:
                    pe.wait_ge(hid_step, m - 1)
                for i in range(2):
                    mm = nc.tensor.matmul(ps[0:rows, 2 + i + 3 * (m % 2), :], gate_up[:, i, m * P:m * P + rows],
                                          xn_t[:], start=True, stop=True)
                return mm

            def weights_of(m):
                return nc.tensor.matmul(ps[:, 4 + 3 * (m % 2), :], spread[:, m * P:(m + 1) * P], gate1_t,
                                        start=True, stop=True)

            gate_and_up(0).then_inc(gu_mm, 1)
            gate_and_up(1).then_inc(gu_mm, 1)
            pe.wait_ge(g1_step, 12)
            for b in range(B):
                tr = nc.tensor.matmul(ps[0:3 * E1, 1, b * S:(b + 1) * S], gate1_parts[:, b, :, :].rearrange("p i e -> p (i e)"),
                                      ident_h[:], start=True, stop=True)
            tr.then_inc(g1_trans, 1)
            pe.wait_ge(g1_ready, 1)
            pe.wait_ge(kv_ready, 4)
            weights_of(0).then_inc(wt_mm, 1)
            weights_of(1).then_inc(wt_mm, 1)
            for m in range(2, EC):
                gate_and_up(m).then_inc(gu_mm, 1)
                weights_of(m).then_inc(wt_mm, 1)
            gate_and_up(EC).then_inc(gu_mm, 1)
            for b in range(B):
                for m in range(EC + 1):
                    if b == 0:
                        pe.wait_ge(hid_step, m + 1)
                    rows = P if m < EC else NS * I1
                    mm = nc.tensor.matmul(ps[:, b, 0:D], hid1_t[0:rows, m * T + b * S:m * T + (b + 1) * S],
                                          down[0:rows, m, :], start=(m == 0), stop=(m == EC))
                mm.then_inc(down_mm, 1)


def kernel(**inputs):
    import numpy as np
    import concourse.bacc as bacc
    from concourse.bass_utils import run_bass_kernel_spmd

    nc = bacc.Bacc("TRN2", target_bir_lowering=False, num_devices=1)
    arrays, tensors = {}, {}
    for name in NAMES:
        a = np.ascontiguousarray(inputs[name])
        arrays["in_" + name] = a
        tensors[name] = nc.dram_tensor("in_" + name, a.shape, mybir.dt.from_np(a.dtype), kind="ExternalInput").ap()
    out = nc.dram_tensor("out_x", inputs['x'].shape, F32, kind="ExternalOutput").ap()
    build_program(nc, tensors, out)
    r = run_bass_kernel_spmd(nc, [arrays], core_ids=[0])
    return r.results[0]["out_x"]
```
